# Optimizing a Trainium2 kernel written in Bass

```python
import numpy as np
import jax
import jax.numpy as jnp

def _softmax(x, axis=-1):
    return jax.nn.softmax(x, axis=axis)

def _gelu(x):
    return jax.nn.gelu(x, approximate=True)

def _silu(x):
    return jax.nn.silu(x)

def _sigmoid(x):
    return jax.nn.sigmoid(x)

def _layernorm(x, axis=-1, eps=1e-05):
    m = jnp.mean(x, axis=axis, keepdims=True)
    v = jnp.var(x, axis=axis, keepdims=True)
    return (x - m) / jnp.sqrt(v + eps)

def _scatter_add(tgt, idx, src, axis=0):
    return tgt.at[idx].add(src)

def _segment_sum(src, seg, n):
    return jax.ops.segment_sum(src, seg, n)
kernel_name = 'mk_vit_tower_postln_d4_tok_img768_r4_12778d'

def setup_inputs(seed: int=0):
    np.random.seed(seed)
    _w = jnp.asarray

    def _rec_inputs():
        import jax
        import jax.numpy as jnp
        _rk = jax.random.key(seed)
        x = -0.000356955 + 1 * jax.random.normal(jax.random.fold_in(_rk, 1), (16, 3, 128, 128), jnp.float32)
        return x
    x = _rec_inputs()

    def _L0_tok_setup():
        import jax, jax.numpy as jnp
        import numpy as np
        PATCH = 16
        EMB = 192
        key = jax.random.key(seed)
        k1, k2 = jax.random.split(key)
        x = jax.random.normal(k1, (128, 3, 224, 224), dtype=jnp.float32)
        W = jax.random.normal(k2, (EMB, PATCH * PATCH * 3), dtype=jnp.float32) * 0.02
        return {'x': x, 'W': W}
    _L0_tok_all = _L0_tok_setup()
    _L0_tok_in = {k: v for k, v in _L0_tok_all.items() if k in ('W',)}
    del _L0_tok_all

    def _L0_attn_setup():
        import jax, jax.numpy as jnp
        import numpy as np
        NH = 12
        LEVEL = 4

        def _build_sets(T, Lmin):
            l_list, r_list = ([], [])
            L = Lmin
            while L <= T:
                for i in range(T // L):
                    l_list.append(i * L)
                    r_list.append((i + 1) * L - 1)
                L *= 2
            return (np.asarray(l_list, np.int32), np.asarray(r_list, np.int32))

        def _get_slice(x_cum, l_idx, r_idx):
            r = x_cum[:, :, r_idx, :]
            l = x_cum[:, :, np.maximum(np.asarray(l_idx) - 1, 0), :]
            mask = (np.asarray(l_idx) >= 1).astype(x_cum.dtype)[None, None, :, None]
            return r - l * mask

        def _get_slice_dyn(x_cum, l_idx, r_idx):
            r = x_cum[:, :, r_idx, :]
            l = x_cum[:, :, jnp.maximum(l_idx - 1, 0), :]
            mask = (l_idx >= 1).astype(x_cum.dtype)[None, None, :, None]
            return r - l * mask
        key = jax.random.key(seed)
        k0, k1, k2, k3 = jax.random.split(key, 4)
        B, T, C = (8, 512, 192)
        hs = C // NH
        s = 0.02
        return {'x': jax.random.normal(k0, (B, T, C), jnp.float32), 'Wqkv': jax.random.normal(k1, (3 * C, C), jnp.float32) * s, 'Wproj': jax.random.normal(k2, (C, C), jnp.float32) * s, 'Wv': jax.random.normal(k3, (hs, hs * hs), jnp.float32) * s, 'bv': jnp.zeros((hs,), jnp.float32)}
    _L0_attn_all = _L0_attn_setup()
    _L0_attn_in = {k: v for k, v in _L0_attn_all.items() if k in ('Wqkv', 'Wproj', 'Wv', 'bv')}
    del _L0_attn_all

    def _L0_ffn_setup():
        import math
        import jax, jax.numpy as jnp
        import numpy as np
        N_HEAD = 12
        N_EXP = 8
        TOP_K = 2
        TRAIN_CAPACITY = 1.25
        MIN_CAPACITY = 4
        LN_EPS = 1e-05
        NEG_INF = -1e+30

        def _layer_norm(x, w, b):
            mu = jnp.mean(x, axis=-1, keepdims=True)
            var = jnp.var(x, axis=-1, keepdims=True)
            return (x - mu) * jax.lax.rsqrt(var + LN_EPS) * w + b

        def _attention(x, qkv_w, qkv_b, proj_w, proj_b):
            B, T, C = x.shape
            H, D = (N_HEAD, C // N_HEAD)
            qkv = x @ qkv_w + qkv_b
            q, k, v = jnp.split(qkv, 3, axis=-1)
            q = q.reshape(B, T, H, D).transpose(0, 2, 1, 3)
            k = k.reshape(B, T, H, D).transpose(0, 2, 1, 3)
            v = v.reshape(B, T, H, D).transpose(0, 2, 1, 3)
            scores = jnp.einsum('bhqd,bhkd->bhqk', q, k) / math.sqrt(D)
            causal = jnp.tril(jnp.ones((T, T), bool))
            scores = jnp.where(causal, scores, NEG_INF)
            attn = jax.nn.softmax(scores, axis=-1)
            y = jnp.einsum('bhqk,bhkd->bhqd', attn, v)
            y = y.transpose(0, 2, 1, 3).reshape(B, T, C)
            return y @ proj_w + proj_b

        def _moe(x, w_g, fc_w, fc_b, pj_w, pj_b):
            B, T, C = x.shape
            N, E, K = (B * T, N_EXP, TOP_K)
            cap = int(math.floor(K * TRAIN_CAPACITY * N / E))
            cap += cap % 2
            cap = max(cap, MIN_CAPACITY)
            logits = (x @ w_g).reshape(N, E)
            _, topk_idx = jax.lax.top_k(logits, K)
            hot = jax.nn.one_hot(topk_idx, E, dtype=jnp.int32)
            sel = hot.sum(axis=1) > 0
            router_probs = jax.nn.softmax(jnp.where(sel, logits, NEG_INF), axis=-1)
            exp_mask = hot.transpose(1, 0, 2)
            exp_rank = jnp.cumsum(exp_mask.reshape(K * N, E), axis=0) - 1
            exp_rank = exp_rank.reshape(K, N, E)
            exp_mask = exp_mask * (exp_rank < cap).astype(jnp.int32)
            exp_rank = jnp.sum(exp_mask * exp_rank, axis=-1)
            exp_weights = exp_mask.astype(x.dtype) * router_probs[None]
            rank_sc = jax.nn.one_hot(exp_rank, cap, dtype=x.dtype)
            cb_weight = jnp.einsum('kne,knc->nec', exp_weights, rank_sc)
            sec_mask = (cb_weight != 0).astype(x.dtype)
            xf = x.reshape(N, C)
            xb = jnp.einsum('nec,nd->ecd', sec_mask, xf)
            h = jax.nn.gelu(jnp.einsum('ecd,edf->ecf', xb, fc_w) + fc_b, approximate=False)
            out = jnp.einsum('ecf,efd->ecd', h, pj_w) + pj_b
            y = jnp.einsum('nec,ecd->nd', cb_weight, out)
            return y.reshape(B, T, C)
        key = jax.random.key(seed)
        ks = jax.random.split(key, 12)
        B, T, C = (4, 256, 192)
        E, F = (N_EXP, 4 * C)
        s = 0.02
        return {'x': jax.random.normal(ks[0], (B, T, C), jnp.float32), 'ln1_w': jnp.ones((C,), jnp.float32), 'ln1_b': jnp.zeros((C,), jnp.float32), 'ln2_w': jnp.ones((C,), jnp.float32), 'ln2_b': jnp.zeros((C,), jnp.float32), 'attn_qkv_w': jax.random.normal(ks[1], (C, 3 * C), jnp.float32) * s, 'attn_qkv_b': jnp.zeros((3 * C,), jnp.float32), 'attn_proj_w': jax.random.normal(ks[2], (C, C), jnp.float32) * s, 'attn_proj_b': jnp.zeros((C,), jnp.float32), 'w_g': jax.random.normal(ks[3], (C, E), jnp.float32) * s, 'exp_fc_w': jax.random.normal(ks[4], (E, C, F), jnp.float32) * s, 'exp_fc_b': jnp.zeros((E, 1, F), jnp.float32), 'exp_proj_w': jax.random.normal(ks[5], (E, F, C), jnp.float32) * s, 'exp_proj_b': jnp.zeros((E, 1, C), jnp.float32)}
    _L0_ffn_all = _L0_ffn_setup()
    _L0_ffn_in = {k: v for k, v in _L0_ffn_all.items() if k in ('ln1_w', 'ln1_b', 'ln2_w', 'ln2_b', 'attn_qkv_w', 'attn_qkv_b', 'attn_proj_w', 'attn_proj_b', 'w_g', 'exp_fc_w', 'exp_fc_b', 'exp_proj_w', 'exp_proj_b')}
    del _L0_ffn_all

    def _L1_attn_setup():
        import jax, jax.numpy as jnp
        import numpy as np
        N_HEADS = 12
        EMB_DIM = 192
        H_DIM = EMB_DIM // N_HEADS
        key = jax.random.key(seed)
        ks = jax.random.split(key, 9)
        s = 0.02
        x = jax.random.normal(ks[0], (8, 256, EMB_DIM), dtype=jnp.float32)
        Wq = jax.random.normal(ks[1], (EMB_DIM, EMB_DIM), dtype=jnp.float32) * s
        Wk = jax.random.normal(ks[2], (EMB_DIM, EMB_DIM), dtype=jnp.float32) * s
        Wv = jax.random.normal(ks[3], (EMB_DIM, EMB_DIM), dtype=jnp.float32) * s
        Wo = jax.random.normal(ks[4], (EMB_DIM, EMB_DIM), dtype=jnp.float32) * s
        bq = jax.random.normal(ks[5], (EMB_DIM,), dtype=jnp.float32) * s
        bk = jax.random.normal(ks[6], (EMB_DIM,), dtype=jnp.float32) * s
        bv = jax.random.normal(ks[7], (EMB_DIM,), dtype=jnp.float32) * s
        bo = jax.random.normal(ks[8], (EMB_DIM,), dtype=jnp.float32) * s
        return {'x': x, 'Wq': Wq, 'bq': bq, 'Wk': Wk, 'bk': bk, 'Wv': Wv, 'bv': bv, 'Wo': Wo, 'bo': bo}
    _L1_attn_all = _L1_attn_setup()
    _L1_attn_in = {k: v for k, v in _L1_attn_all.items() if k in ('Wq', 'bq', 'Wk', 'bk', 'Wv', 'bv', 'Wo', 'bo')}
    del _L1_attn_all

    def _L1_ffn_setup():
        import jax, jax.numpy as jnp
        import numpy as np
        SEQ, BATCH, EMBED = (256, 2, 192)
        E = 16
        FFN_H = 384
        K_SHARED = 1
        K_ROUTE = 3
        LN_EPS = 1e-05
        NEG_INF = -1000000000.0
        key = jax.random.key(seed)
        ks = jax.random.split(key, 4)
        x = jax.random.normal(ks[0], (SEQ, BATCH, EMBED), dtype=jnp.float32)
        gate_w = jax.random.normal(ks[1], (EMBED, E), dtype=jnp.float32) * 0.02
        gate_b = jnp.zeros((E,), jnp.float32)
        fc1_w = jax.random.normal(ks[2], (E, EMBED, FFN_H), dtype=jnp.float32) * 0.02
        fc1_b = jnp.zeros((E, FFN_H), jnp.float32)
        ln_w = jnp.ones((E, FFN_H), jnp.float32)
        ln_b = jnp.zeros((E, FFN_H), jnp.float32)
        fc2_w = jax.random.normal(ks[3], (E, FFN_H, EMBED), dtype=jnp.float32) * 0.02
        fc2_b = jnp.zeros((E, EMBED), jnp.float32)
        return {'x': x, 'gate_w': gate_w, 'gate_b': gate_b, 'fc1_w': fc1_w, 'fc1_b': fc1_b, 'ln_w': ln_w, 'ln_b': ln_b, 'fc2_w': fc2_w, 'fc2_b': fc2_b}
    _L1_ffn_all = _L1_ffn_setup()
    _L1_ffn_in = {k: v for k, v in _L1_ffn_all.items() if k in ('gate_w', 'gate_b', 'fc1_w', 'fc1_b', 'ln_w', 'ln_b', 'fc2_w', 'fc2_b')}
    del _L1_ffn_all

    def _L2_attn_setup():
        import jax, jax.numpy as jnp
        import numpy as np
        import math
        H = 12

        def _ln(x, w, b, eps=1e-05):
            mu = x.mean(-1, keepdims=True)
            var = ((x - mu) ** 2).mean(-1, keepdims=True)
            return (x - mu) / jnp.sqrt(var + eps) * w + b

        def _reference_tuple_inner(x, Wqkv, bqkv, Wb1, Wb2, temperature, Wproj, bproj, ln_w, ln_b, mn_w, mn_b):
            B, L, D = x.shape
            d = D // H
            x_norm = _ln(x, ln_w, ln_b)
            qkv = x_norm @ Wqkv + bqkv
            q, k, v = jnp.split(qkv, 3, axis=-1)
            params = (jax.nn.silu(x @ Wb1) @ Wb2).reshape(B, L, H, 5)
            sem_amp = jax.nn.sigmoid(params[..., 0])
            sem_phase = jnp.tanh(params[..., 1]) * math.pi
            ctx_amp = jax.nn.sigmoid(params[..., 2])
            ctx_phase = jnp.tanh(params[..., 3]) * math.pi
            temp = jnp.clip(temperature, 0.1, 2.0)
            interference = jnp.tanh(sem_amp * ctx_amp * jnp.cos(sem_phase - ctx_phase)) * temp
            gate = jax.nn.sigmoid(interference)
            q_f = (jax.nn.elu(q) + 1.0).reshape(B, L, H, d)
            k_f = (jax.nn.elu(k) + 1.0).reshape(B, L, H, d)
            v_f = v.reshape(B, L, H, d)
            kv_gated = jnp.einsum('blhd,blhe->blhde', k_f, v_f) * (1.0 + gate)[..., None, None]
            kv_states = jnp.cumsum(kv_gated, axis=1)
            z_states = jnp.cumsum(k_f, axis=1)
            out_num = jnp.einsum('blhd,blhde->blhe', q_f, kv_states)
            den = jnp.sum(q_f * z_states, axis=-1, keepdims=True) + 1e-06
            out = _ln(out_num / den, mn_w, mn_b)
            attn_out = out.reshape(B, L, D)
            return (attn_out @ Wproj + bproj, gate)
        key = jax.random.key(seed)
        B, L, D, R = (2, 256, 192, 128)
        d_head = D // H
        ks = jax.random.split(key, 6)
        s = 0.02
        return {'x': jax.random.normal(ks[0], (B, L, D), jnp.float32), 'Wqkv': jax.random.normal(ks[1], (D, 3 * D), jnp.float32) * s, 'bqkv': jnp.zeros((3 * D,), jnp.float32), 'Wb1': jax.random.normal(ks[2], (D, R), jnp.float32) * s, 'Wb2': jax.random.normal(ks[3], (R, H * 5), jnp.float32) * s, 'temperature': jnp.ones((1,), jnp.float32) * 0.5, 'Wproj': jax.random.normal(ks[4], (D, D), jnp.float32) * s, 'bproj': jnp.zeros((D,), jnp.float32), 'ln_w': jnp.ones((D,), jnp.float32), 'ln_b': jnp.zeros((D,), jnp.float32), 'mn_w': jnp.ones((d_head,), jnp.float32), 'mn_b': jnp.zeros((d_head,), jnp.float32)}
    _L2_attn_all = _L2_attn_setup()
    _L2_attn_in = {k: v for k, v in _L2_attn_all.items() if k in ('Wqkv', 'bqkv', 'Wb1', 'Wb2', 'temperature', 'Wproj', 'bproj', 'ln_w', 'ln_b', 'mn_w', 'mn_b')}
    del _L2_attn_all

    def _L2_ffn_setup():
        import jax, jax.numpy as jnp
        import numpy as np
        import math
        B, S, D = (4, 1024, 192)
        E = 8
        TOP_K = 2
        H = 512
        CAP_F = 1.25
        EPS = 1e-06
        ALPHA = 1.0
        key = jax.random.key(seed)
        k0, k1, k2, k3 = jax.random.split(key, 4)
        x = jax.random.normal(k0, (B, S, D), jnp.float32)
        gate_w = jax.random.normal(k1, (E, D), jnp.float32) * 0.02
        w13 = jax.random.normal(k2, (E, 2 * H, D), jnp.float32) * 0.02
        w2 = jax.random.normal(k3, (E, D, H), jnp.float32) * 0.02
        norm_w = jnp.ones((E, D), jnp.float32)
        return {'x': x, 'gate_w': gate_w, 'w13': w13, 'w2': w2, 'norm_w': norm_w}
    _L2_ffn_all = _L2_ffn_setup()
    _L2_ffn_in = {k: v for k, v in _L2_ffn_all.items() if k in ('gate_w', 'w13', 'w2', 'norm_w')}
    del _L2_ffn_all

    def _L3_attn_setup():
        import jax, jax.numpy as jnp
        import numpy as np
        DIM, HEADS, SEQ_LEN = (192, 12, 1024)
        HEAD_DIM = DIM // HEADS
        RMS_EPS = 1.1920928955078125e-07
        ATTN_SCALE = 0.12

        def _rms_norm(x):
            return x * jax.lax.rsqrt(jnp.mean(x * x, axis=-1, keepdims=True) + RMS_EPS)

        def _rotary_tables(T, head_dim):
            freqs = (1.0 / 1024.0) ** jnp.linspace(0.0, 1.0, head_dim // 4, dtype=jnp.float32)
            freqs = jnp.concatenate([freqs, jnp.zeros(head_dim // 4, dtype=jnp.float32)])
            t = jnp.arange(T, dtype=jnp.float32)
            theta = t[:, None] * freqs[None, :]
            return (jnp.cos(theta), jnp.sin(theta))

        def _apply_rotary(x, cos, sin):
            x1, x2 = jnp.split(x.astype(jnp.float32), 2, axis=-1)
            c = cos[None, :, None, :]
            s = sin[None, :, None, :]
            y1 = x1 * c + x2 * s
            y2 = -x1 * s + x2 * c
            return jnp.concatenate([y1, y2], axis=-1).astype(x.dtype)
        key = jax.random.key(seed)
        k1, k2, k3 = jax.random.split(key, 3)
        x = jax.random.normal(k1, (1, SEQ_LEN, DIM), dtype=jnp.float32)
        std = 0.5 * DIM ** (-0.5)
        bound = 3.0 ** 0.5 * std
        qkv_w = jax.random.uniform(k2, (3, DIM, DIM), dtype=jnp.float32, minval=-bound, maxval=bound)
        c_proj_w = jax.random.normal(k3, (DIM, DIM), dtype=jnp.float32) * DIM ** (-0.5)
        return {'x': x, 'qkv_w': qkv_w, 'c_proj_w': c_proj_w}
    _L3_attn_all = _L3_attn_setup()
    _L3_attn_in = {k: v for k, v in _L3_attn_all.items() if k in ('qkv_w', 'c_proj_w')}
    del _L3_attn_all

    def _L3_ffn_setup():
        import jax, jax.numpy as jnp
        import numpy as np
        ACT_SCALE = 0.02
        W_SCALE = 0.01
        EFF_SCALE = ACT_SCALE * W_SCALE
        B, S, D, M = (8, 1024, 192, 192)
        key = jax.random.key(seed)
        kx, kw, kb = jax.random.split(key, 3)
        x = jax.random.normal(kx, (B, S, D), dtype=jnp.float32)
        weight_t = jax.random.randint(kw, (D, M), -128, 128, dtype=jnp.int32).astype(jnp.int8)
        bias = jax.random.normal(kb, (M,), dtype=jnp.float32)
        return {'x': x, 'weight_t': weight_t, 'bias': bias}
    _L3_ffn_all = _L3_ffn_setup()
    _L3_ffn_in = {k: v for k, v in _L3_ffn_all.items() if k in ('weight_t', 'bias')}
    del _L3_ffn_all
    return {'x': x, 'L0_tok_W': _L0_tok_in['W'], 'L0_attn_Wqkv': _L0_attn_in['Wqkv'], 'L0_attn_Wproj': _L0_attn_in['Wproj'], 'L0_attn_Wv': _L0_attn_in['Wv'], 'L0_attn_bv': _L0_attn_in['bv'], 'L0_ffn_ln1_w': _L0_ffn_in['ln1_w'], 'L0_ffn_ln1_b': _L0_ffn_in['ln1_b'], 'L0_ffn_ln2_w': _L0_ffn_in['ln2_w'], 'L0_ffn_ln2_b': _L0_ffn_in['ln2_b'], 'L0_ffn_attn_qkv_w': _L0_ffn_in['attn_qkv_w'], 'L0_ffn_attn_qkv_b': _L0_ffn_in['attn_qkv_b'], 'L0_ffn_attn_proj_w': _L0_ffn_in['attn_proj_w'], 'L0_ffn_attn_proj_b': _L0_ffn_in['attn_proj_b'], 'L0_ffn_w_g': _L0_ffn_in['w_g'], 'L0_ffn_exp_fc_w': _L0_ffn_in['exp_fc_w'], 'L0_ffn_exp_fc_b': _L0_ffn_in['exp_fc_b'], 'L0_ffn_exp_proj_w': _L0_ffn_in['exp_proj_w'], 'L0_ffn_exp_proj_b': _L0_ffn_in['exp_proj_b'], 'L1_attn_Wq': _L1_attn_in['Wq'], 'L1_attn_bq': _L1_attn_in['bq'], 'L1_attn_Wk': _L1_attn_in['Wk'], 'L1_attn_bk': _L1_attn_in['bk'], 'L1_attn_Wv': _L1_attn_in['Wv'], 'L1_attn_bv': _L1_attn_in['bv'], 'L1_attn_Wo': _L1_attn_in['Wo'], 'L1_attn_bo': _L1_attn_in['bo'], 'L1_ffn_gate_w': _L1_ffn_in['gate_w'], 'L1_ffn_gate_b': _L1_ffn_in['gate_b'], 'L1_ffn_fc1_w': _L1_ffn_in['fc1_w'], 'L1_ffn_fc1_b': _L1_ffn_in['fc1_b'], 'L1_ffn_ln_w': _L1_ffn_in['ln_w'], 'L1_ffn_ln_b': _L1_ffn_in['ln_b'], 'L1_ffn_fc2_w': _L1_ffn_in['fc2_w'], 'L1_ffn_fc2_b': _L1_ffn_in['fc2_b'], 'L2_attn_Wqkv': _L2_attn_in['Wqkv'], 'L2_attn_bqkv': _L2_attn_in['bqkv'], 'L2_attn_Wb1': _L2_attn_in['Wb1'], 'L2_attn_Wb2': _L2_attn_in['Wb2'], 'L2_attn_temperature': _L2_attn_in['temperature'], 'L2_attn_Wproj': _L2_attn_in['Wproj'], 'L2_attn_bproj': _L2_attn_in['bproj'], 'L2_attn_ln_w': _L2_attn_in['ln_w'], 'L2_attn_ln_b': _L2_attn_in['ln_b'], 'L2_attn_mn_w': _L2_attn_in['mn_w'], 'L2_attn_mn_b': _L2_attn_in['mn_b'], 'L2_ffn_gate_w': _L2_ffn_in['gate_w'], 'L2_ffn_w13': _L2_ffn_in['w13'], 'L2_ffn_w2': _L2_ffn_in['w2'], 'L2_ffn_norm_w': _L2_ffn_in['norm_w'], 'L3_attn_qkv_w': _L3_attn_in['qkv_w'], 'L3_attn_c_proj_w': _L3_attn_in['c_proj_w'], 'L3_ffn_weight_t': _L3_ffn_in['weight_t'], 'L3_ffn_bias': _L3_ffn_in['bias']}

def reference(x, L0_tok_W, L0_attn_Wqkv, L0_attn_Wproj, L0_attn_Wv, L0_attn_bv, L0_ffn_ln1_w, L0_ffn_ln1_b, L0_ffn_ln2_w, L0_ffn_ln2_b, L0_ffn_attn_qkv_w, L0_ffn_attn_qkv_b, L0_ffn_attn_proj_w, L0_ffn_attn_proj_b, L0_ffn_w_g, L0_ffn_exp_fc_w, L0_ffn_exp_fc_b, L0_ffn_exp_proj_w, L0_ffn_exp_proj_b, L1_attn_Wq, L1_attn_bq, L1_attn_Wk, L1_attn_bk, L1_attn_Wv, L1_attn_bv, L1_attn_Wo, L1_attn_bo, L1_ffn_gate_w, L1_ffn_gate_b, L1_ffn_fc1_w, L1_ffn_fc1_b, L1_ffn_ln_w, L1_ffn_ln_b, L1_ffn_fc2_w, L1_ffn_fc2_b, L2_attn_Wqkv, L2_attn_bqkv, L2_attn_Wb1, L2_attn_Wb2, L2_attn_temperature, L2_attn_Wproj, L2_attn_bproj, L2_attn_ln_w, L2_attn_ln_b, L2_attn_mn_w, L2_attn_mn_b, L2_ffn_gate_w, L2_ffn_w13, L2_ffn_w2, L2_ffn_norm_w, L3_attn_qkv_w, L3_attn_c_proj_w, L3_ffn_weight_t, L3_ffn_bias):
    import jax
    import jax.numpy as jnp

    def _L0_tok_ref(x, W):
        import jax, jax.numpy as jnp
        import numpy as np
        PATCH = 16
        EMB = 192
        B, C, H, Wd = x.shape
        p = PATCH
        hp, wp = (H // p, Wd // p)
        num_patches = hp * wp
        xp = x.reshape(B, C, hp, p, wp, p).transpose(0, 1, 2, 4, 3, 5)
        xp = xp.reshape(B, C, num_patches, p, p).transpose(0, 2, 1, 3, 4)
        xp = xp.reshape(B, num_patches, C * p * p)
        return jnp.einsum('bnf,ef->bne', xp, W)

    def _L0_attn_ref(x, Wqkv, Wproj, Wv, bv):
        import jax, jax.numpy as jnp
        import numpy as np
        NH = 12
        LEVEL = 4

        def _build_sets(T, Lmin):
            l_list, r_list = ([], [])
            L = Lmin
            while L <= T:
                for i in range(T // L):
                    l_list.append(i * L)
                    r_list.append((i + 1) * L - 1)
                L *= 2
            return (np.asarray(l_list, np.int32), np.asarray(r_list, np.int32))

        def _get_slice(x_cum, l_idx, r_idx):
            r = x_cum[:, :, r_idx, :]
            l = x_cum[:, :, np.maximum(np.asarray(l_idx) - 1, 0), :]
            mask = (np.asarray(l_idx) >= 1).astype(x_cum.dtype)[None, None, :, None]
            return r - l * mask

        def _get_slice_dyn(x_cum, l_idx, r_idx):
            r = x_cum[:, :, r_idx, :]
            l = x_cum[:, :, jnp.maximum(l_idx - 1, 0), :]
            mask = (l_idx >= 1).astype(x_cum.dtype)[None, None, :, None]
            return r - l * mask
        B, T, C = x.shape
        nh = NH
        hs = C // nh
        Lmin = 2 ** LEVEL
        scale = 1.0 / jnp.sqrt(jnp.asarray(hs, x.dtype))
        qkv = x @ Wqkv.T
        q, k, v0 = jnp.split(qkv, 3, axis=-1)
        q = q.reshape(B, T, nh, hs).transpose(0, 2, 1, 3)
        k = k.reshape(B, T, nh, hs).transpose(0, 2, 1, 3)
        v0 = v0.reshape(B, T, nh, hs).transpose(0, 2, 1, 3)
        Wv3 = Wv.reshape(hs, hs, hs)
        v = jnp.einsum('bhti,bhtj,eij->bhte', k, v0, Wv3) + bv
        k_cum = jnp.cumsum(k, axis=2)
        v_cum = jnp.cumsum(v, axis=2)
        l_idx, r_idx = _build_sets(T, Lmin)
        K = _get_slice(k_cum, l_idx, r_idx)
        V = _get_slice(v_cum, l_idx, r_idx)
        t_idx = jnp.arange(T)
        mask = t_idx[:, None] >= jnp.asarray(r_idx)[None, :]
        logits = jnp.einsum('bhtd,bhsd->bhts', q, K) * scale
        logits = jnp.where(mask[None, None], logits, -jnp.inf)
        l_tail = t_idx // Lmin * Lmin
        K_tail = _get_slice_dyn(k_cum, l_tail, t_idx)
        V_tail = _get_slice_dyn(v_cum, l_tail, t_idx)
        tail_logits = jnp.sum(q * K_tail, axis=-1) * scale
        att = jax.nn.softmax(jnp.concatenate([logits, tail_logits[..., None]], axis=-1), axis=-1)
        out = jnp.einsum('bhts,bhsd->bhtd', att[..., :-1], V) + att[..., -1:] * V_tail
        out = out.transpose(0, 2, 1, 3).reshape(B, T, C)
        return out @ Wproj.T

    def _L0_ffn_ref(x, ln1_w, ln1_b, ln2_w, ln2_b, attn_qkv_w, attn_qkv_b, attn_proj_w, attn_proj_b, w_g, exp_fc_w, exp_fc_b, exp_proj_w, exp_proj_b):
        import math
        import jax, jax.numpy as jnp
        import numpy as np
        N_HEAD = 12
        N_EXP = 8
        TOP_K = 2
        TRAIN_CAPACITY = 1.25
        MIN_CAPACITY = 4
        LN_EPS = 1e-05
        NEG_INF = -1e+30

        def _layer_norm(x, w, b):
            mu = jnp.mean(x, axis=-1, keepdims=True)
            var = jnp.var(x, axis=-1, keepdims=True)
            return (x - mu) * jax.lax.rsqrt(var + LN_EPS) * w + b

        def _attention(x, qkv_w, qkv_b, proj_w, proj_b):
            B, T, C = x.shape
            H, D = (N_HEAD, C // N_HEAD)
            qkv = x @ qkv_w + qkv_b
            q, k, v = jnp.split(qkv, 3, axis=-1)
            q = q.reshape(B, T, H, D).transpose(0, 2, 1, 3)
            k = k.reshape(B, T, H, D).transpose(0, 2, 1, 3)
            v = v.reshape(B, T, H, D).transpose(0, 2, 1, 3)
            scores = jnp.einsum('bhqd,bhkd->bhqk', q, k) / math.sqrt(D)
            causal = jnp.tril(jnp.ones((T, T), bool))
            scores = jnp.where(causal, scores, NEG_INF)
            attn = jax.nn.softmax(scores, axis=-1)
            y = jnp.einsum('bhqk,bhkd->bhqd', attn, v)
            y = y.transpose(0, 2, 1, 3).reshape(B, T, C)
            return y @ proj_w + proj_b

        def _moe(x, w_g, fc_w, fc_b, pj_w, pj_b):
            B, T, C = x.shape
            N, E, K = (B * T, N_EXP, TOP_K)
            cap = int(math.floor(K * TRAIN_CAPACITY * N / E))
            cap += cap % 2
            cap = max(cap, MIN_CAPACITY)
            logits = (x @ w_g).reshape(N, E)
            _, topk_idx = jax.lax.top_k(logits, K)
            hot = jax.nn.one_hot(topk_idx, E, dtype=jnp.int32)
            sel = hot.sum(axis=1) > 0
            router_probs = jax.nn.softmax(jnp.where(sel, logits, NEG_INF), axis=-1)
            exp_mask = hot.transpose(1, 0, 2)
            exp_rank = jnp.cumsum(exp_mask.reshape(K * N, E), axis=0) - 1
            exp_rank = exp_rank.reshape(K, N, E)
            exp_mask = exp_mask * (exp_rank < cap).astype(jnp.int32)
            exp_rank = jnp.sum(exp_mask * exp_rank, axis=-1)
            exp_weights = exp_mask.astype(x.dtype) * router_probs[None]
            rank_sc = jax.nn.one_hot(exp_rank, cap, dtype=x.dtype)
            cb_weight = jnp.einsum('kne,knc->nec', exp_weights, rank_sc)
            sec_mask = (cb_weight != 0).astype(x.dtype)
            xf = x.reshape(N, C)
            xb = jnp.einsum('nec,nd->ecd', sec_mask, xf)
            h = jax.nn.gelu(jnp.einsum('ecd,edf->ecf', xb, fc_w) + fc_b, approximate=False)
            out = jnp.einsum('ecf,efd->ecd', h, pj_w) + pj_b
            y = jnp.einsum('nec,ecd->nd', cb_weight, out)
            return y.reshape(B, T, C)
        x = x + _attention(_layer_norm(x, ln1_w, ln1_b), attn_qkv_w, attn_qkv_b, attn_proj_w, attn_proj_b)
        x = x + _moe(_layer_norm(x, ln2_w, ln2_b), w_g, exp_fc_w, exp_fc_b, exp_proj_w, exp_proj_b)
        return x

    def _L1_attn_ref(x, Wq, bq, Wk, bk, Wv, bv, Wo, bo):
        import jax, jax.numpy as jnp
        import numpy as np
        N_HEADS = 12
        EMB_DIM = 192
        H_DIM = EMB_DIM // N_HEADS
        B, T, E = x.shape
        H, D = (N_HEADS, H_DIM)
        q = (x @ Wq.T + bq).reshape(B, T, H, D).transpose(0, 2, 1, 3)
        k = (x @ Wk.T + bk).reshape(B, T, H, D).transpose(0, 2, 1, 3)
        v = (x @ Wv.T + bv).reshape(B, T, H, D).transpose(0, 2, 1, 3)
        scores = jnp.einsum('bhqd,bhkd->bhqk', q, k)
        causal = jnp.tril(jnp.ones((T, T), dtype=bool))
        scores = jnp.where(causal, scores, -jnp.inf)
        attn = jax.nn.softmax(scores / jnp.sqrt(jnp.float32(D)), axis=-1)
        ctx = jnp.einsum('bhqk,bhkd->bhqd', attn, v)
        ctx = ctx.transpose(0, 2, 1, 3).reshape(B, T, E)
        return ctx @ Wo.T + bo

    def _L1_ffn_ref(x, gate_w, gate_b, fc1_w, fc1_b, ln_w, ln_b, fc2_w, fc2_b):
        import jax, jax.numpy as jnp
        import numpy as np
        SEQ, BATCH, EMBED = (256, 2, 192)
        E = 16
        FFN_H = 384
        K_SHARED = 1
        K_ROUTE = 3
        LN_EPS = 1e-05
        NEG_INF = -1000000000.0
        S, B, D = x.shape
        T = S * B
        xf = x.reshape(T, D)
        scores = xf @ gate_w + gate_b
        scores = scores.at[:, :K_SHARED].set(NEG_INF)
        probs = jax.nn.softmax(scores, axis=-1)
        topv, topi = jax.lax.top_k(probs, K_ROUTE)
        combine = jnp.zeros((T, E), xf.dtype)
        combine = combine.at[jnp.arange(T)[:, None], topi].add(topv)
        combine = combine.at[:, :K_SHARED].add(1.0)
        h = jnp.einsum('td,edh->eth', xf, fc1_w) + fc1_b[:, None, :]
        h = jax.nn.gelu(h, approximate=False)
        mu = h.mean(-1, keepdims=True)
        var = h.var(-1, keepdims=True)
        h = (h - mu) * jax.lax.rsqrt(var + LN_EPS) * ln_w[:, None, :] + ln_b[:, None, :]
        y = jnp.einsum('eth,ehd->etd', h, fc2_w) + fc2_b[:, None, :]
        out = jnp.einsum('te,etd->td', combine, y)
        return out.reshape(S, B, D)

    def _L2_attn_ref(x, Wqkv, bqkv, Wb1, Wb2, temperature, Wproj, bproj, ln_w, ln_b, mn_w, mn_b):
        import jax, jax.numpy as jnp
        import numpy as np
        import math
        H = 12

        def _ln(x, w, b, eps=1e-05):
            mu = x.mean(-1, keepdims=True)
            var = ((x - mu) ** 2).mean(-1, keepdims=True)
            return (x - mu) / jnp.sqrt(var + eps) * w + b

        def _reference_tuple_inner(x, Wqkv, bqkv, Wb1, Wb2, temperature, Wproj, bproj, ln_w, ln_b, mn_w, mn_b):
            B, L, D = x.shape
            d = D // H
            x_norm = _ln(x, ln_w, ln_b)
            qkv = x_norm @ Wqkv + bqkv
            q, k, v = jnp.split(qkv, 3, axis=-1)
            params = (jax.nn.silu(x @ Wb1) @ Wb2).reshape(B, L, H, 5)
            sem_amp = jax.nn.sigmoid(params[..., 0])
            sem_phase = jnp.tanh(params[..., 1]) * math.pi
            ctx_amp = jax.nn.sigmoid(params[..., 2])
            ctx_phase = jnp.tanh(params[..., 3]) * math.pi
            temp = jnp.clip(temperature, 0.1, 2.0)
            interference = jnp.tanh(sem_amp * ctx_amp * jnp.cos(sem_phase - ctx_phase)) * temp
            gate = jax.nn.sigmoid(interference)
            q_f = (jax.nn.elu(q) + 1.0).reshape(B, L, H, d)
            k_f = (jax.nn.elu(k) + 1.0).reshape(B, L, H, d)
            v_f = v.reshape(B, L, H, d)
            kv_gated = jnp.einsum('blhd,blhe->blhde', k_f, v_f) * (1.0 + gate)[..., None, None]
            kv_states = jnp.cumsum(kv_gated, axis=1)
            z_states = jnp.cumsum(k_f, axis=1)
            out_num = jnp.einsum('blhd,blhde->blhe', q_f, kv_states)
            den = jnp.sum(q_f * z_states, axis=-1, keepdims=True) + 1e-06
            out = _ln(out_num / den, mn_w, mn_b)
            attn_out = out.reshape(B, L, D)
            return (attn_out @ Wproj + bproj, gate)
        return _reference_tuple_inner(x, Wqkv, bqkv, Wb1, Wb2, temperature, Wproj, bproj, ln_w, ln_b, mn_w, mn_b)[0]

    def _L2_ffn_ref(x, gate_w, w13, w2, norm_w):
        import jax, jax.numpy as jnp
        import numpy as np
        import math
        B, S, D = (4, 1024, 192)
        E = 8
        TOP_K = 2
        H = 512
        CAP_F = 1.25
        EPS = 1e-06
        ALPHA = 1.0
        Bx, Sx, Dx = x.shape
        N = Bx * Sx
        cap = int(math.ceil(CAP_F * TOP_K * N / E))
        xf = x.reshape(N, Dx)
        logits = xf.astype(jnp.float32) @ gate_w.T
        probs = jax.nn.softmax(logits, axis=-1)
        top_p, top_i = jax.lax.top_k(probs, TOP_K)
        w = top_p / jnp.sum(top_p, axis=-1, keepdims=True)
        flat_e = top_i.reshape(-1)
        onehot = jax.nn.one_hot(flat_e, E, dtype=jnp.int32)
        pos = jnp.take_along_axis(jnp.cumsum(onehot, axis=0) - 1, flat_e[:, None], axis=1)[:, 0]
        keep = pos < cap
        didx = flat_e * cap + jnp.minimum(pos, cap - 1)
        safe = jnp.where(keep, didx, E * cap)
        x_rep = jnp.repeat(xf, TOP_K, axis=0)
        buf = jnp.zeros((E * cap + 1, Dx), x.dtype).at[safe].set(x_rep)
        buf = buf[:-1].reshape(E, cap, Dx)
        z = 2.0 * buf
        z = z * jax.lax.rsqrt(jnp.mean(z * z, axis=-1, keepdims=True) + EPS)
        z = z * norm_w[:, None, :]
        gu = jnp.einsum('ecd,ehd->ech', z, w13)
        g, u = jnp.split(gu, 2, axis=-1)
        y = buf + ALPHA * jnp.einsum('ech,edh->ecd', jax.nn.silu(g) * u, w2)
        y_tok = y.reshape(E * cap, Dx)[didx]
        cw = (w.reshape(-1) * keep.astype(w.dtype)).astype(x.dtype)
        out = (cw[:, None] * y_tok).reshape(N, TOP_K, Dx).sum(axis=1)
        return out.reshape(Bx, Sx, Dx)

    def _L3_attn_ref(x, qkv_w, c_proj_w):
        import jax, jax.numpy as jnp
        import numpy as np
        DIM, HEADS, SEQ_LEN = (192, 12, 1024)
        HEAD_DIM = DIM // HEADS
        RMS_EPS = 1.1920928955078125e-07
        ATTN_SCALE = 0.12

        def _rms_norm(x):
            return x * jax.lax.rsqrt(jnp.mean(x * x, axis=-1, keepdims=True) + RMS_EPS)

        def _rotary_tables(T, head_dim):
            freqs = (1.0 / 1024.0) ** jnp.linspace(0.0, 1.0, head_dim // 4, dtype=jnp.float32)
            freqs = jnp.concatenate([freqs, jnp.zeros(head_dim // 4, dtype=jnp.float32)])
            t = jnp.arange(T, dtype=jnp.float32)
            theta = t[:, None] * freqs[None, :]
            return (jnp.cos(theta), jnp.sin(theta))

        def _apply_rotary(x, cos, sin):
            x1, x2 = jnp.split(x.astype(jnp.float32), 2, axis=-1)
            c = cos[None, :, None, :]
            s = sin[None, :, None, :]
            y1 = x1 * c + x2 * s
            y2 = -x1 * s + x2 * c
            return jnp.concatenate([y1, y2], axis=-1).astype(x.dtype)
        B, T, dim = x.shape
        H, D = (HEADS, HEAD_DIM)
        qkv = jnp.einsum('btd,kfd->btkf', x, qkv_w)
        qkv = qkv.reshape(B, T, 3, H, D)
        q, k, v = (qkv[:, :, 0], qkv[:, :, 1], qkv[:, :, 2])
        q, k = (_rms_norm(q), _rms_norm(k))
        cos, sin = _rotary_tables(T, D)
        q, k = (_apply_rotary(q, cos, sin), _apply_rotary(k, cos, sin))
        scores = jnp.einsum('bthd,bshd->bhts', q, k) * ATTN_SCALE
        causal = jnp.tril(jnp.ones((T, T), dtype=bool))
        scores = jnp.where(causal[None, None], scores, jnp.finfo(scores.dtype).min)
        probs = jax.nn.softmax(scores, axis=-1)
        y = jnp.einsum('bhts,bshd->bthd', probs, v).reshape(B, T, dim)
        return y @ c_proj_w.T

    def _L3_ffn_ref(x, weight_t, bias):
        import jax, jax.numpy as jnp
        import numpy as np
        ACT_SCALE = 0.02
        W_SCALE = 0.01
        EFF_SCALE = ACT_SCALE * W_SCALE
        B, S, D, M = (8, 1024, 192, 192)
        orig_shape = x.shape
        x_flat = x.reshape(-1, orig_shape[-1])
        x_int8 = jnp.clip(jnp.round(x_flat / ACT_SCALE), -128, 127).astype(jnp.int8)
        acc_i32 = jnp.matmul(x_int8, weight_t, preferred_element_type=jnp.int32)
        out = acc_i32.astype(jnp.float32) * jnp.float32(EFF_SCALE) + bias
        return out.reshape(orig_shape[:-1] + (M,))
    h = _L0_tok_ref(x, L0_tok_W)
    h = _layernorm(h + _L0_attn_ref(h, L0_attn_Wqkv, L0_attn_Wproj, L0_attn_Wv, L0_attn_bv), axis=-1)
    h = _layernorm(h + _L0_ffn_ref(h, L0_ffn_ln1_w, L0_ffn_ln1_b, L0_ffn_ln2_w, L0_ffn_ln2_b, L0_ffn_attn_qkv_w, L0_ffn_attn_qkv_b, L0_ffn_attn_proj_w, L0_ffn_attn_proj_b, L0_ffn_w_g, L0_ffn_exp_fc_w, L0_ffn_exp_fc_b, L0_ffn_exp_proj_w, L0_ffn_exp_proj_b), axis=-1)
    h = _layernorm(h + _L1_attn_ref(h, L1_attn_Wq, L1_attn_bq, L1_attn_Wk, L1_attn_bk, L1_attn_Wv, L1_attn_bv, L1_attn_Wo, L1_attn_bo), axis=-1)
    h = _layernorm(h + _L1_ffn_ref(h, L1_ffn_gate_w, L1_ffn_gate_b, L1_ffn_fc1_w, L1_ffn_fc1_b, L1_ffn_ln_w, L1_ffn_ln_b, L1_ffn_fc2_w, L1_ffn_fc2_b), axis=-1)
    h = _layernorm(h + _L2_attn_ref(h, L2_attn_Wqkv, L2_attn_bqkv, L2_attn_Wb1, L2_attn_Wb2, L2_attn_temperature, L2_attn_Wproj, L2_attn_bproj, L2_attn_ln_w, L2_attn_ln_b, L2_attn_mn_w, L2_attn_mn_b), axis=-1)
    h = _layernorm(h + _L2_ffn_ref(h, L2_ffn_gate_w, L2_ffn_w13, L2_ffn_w2, L2_ffn_norm_w), axis=-1)
    h = _layernorm(h + _L3_attn_ref(h, L3_attn_qkv_w, L3_attn_c_proj_w), axis=-1)
    h = _layernorm(h + _L3_ffn_ref(h, L3_ffn_weight_t, L3_ffn_bias), axis=-1)
    return h

_drawn_inputs = setup_inputs


def setup_inputs(seed=0):
    import zlib

    import numpy as np

    out = dict(_drawn_inputs(seed))
    spreads = {'L0_attn_bv': (0.0, 0.1),
     'L0_ffn_ln1_w': (1.0, 0.6),
     'L0_ffn_ln1_b': (0.0, 0.685),
     'L0_ffn_ln2_w': (1.0, 0.6),
     'L0_ffn_ln2_b': (0.0, 0.467),
     'L0_ffn_attn_qkv_b': (0.0, 0.371),
     'L0_ffn_attn_proj_b': (0.0, 0.1),
     'L0_ffn_exp_fc_b': (0.0, 0.553),
     'L0_ffn_exp_proj_b': (0.0, 0.1),
     'L1_ffn_gate_b': (0.0, 0.1),
     'L1_ffn_fc1_b': (0.0, 0.1),
     'L1_ffn_ln_w': (1.0, 0.2),
     'L1_ffn_ln_b': (0.0, 0.1),
     'L1_ffn_fc2_b': (0.0, 0.1),
     'L2_attn_bqkv': (0.0, 0.1),
     'L2_attn_bproj': (0.0, 0.1),
     'L2_attn_ln_w': (1.0, 0.2),
     'L2_attn_ln_b': (0.0, 0.1),
     'L2_attn_mn_w': (1.0, 0.2),
     'L2_attn_mn_b': (0.0, 0.302),
     'L2_ffn_norm_w': (1.0, 0.6)}
    factors = {'L0_attn_Wqkv': 3.061,
     'L0_attn_Wv': 4.567,
     'L1_attn_Wq': 8.0,
     'L1_attn_bq': 8.0,
     'L1_attn_Wk': 8.0,
     'L1_attn_bk': 8.0,
     'L1_attn_bv': 5.886,
     'L2_attn_Wb1': 8.0,
     'L2_attn_Wb2': 8.0,
     'L2_ffn_gate_w': 7.354,
     'L2_ffn_w13': 6.997,
     'L2_ffn_w2': 6.953}
    for name, (base, spread) in spreads.items():
        noise = np.random.default_rng([zlib.crc32(name.encode()), seed]).standard_normal(out[name].shape)
        drawn = base * np.exp(spread * noise) if base else spread * noise
        out[name] = jnp.asarray(drawn.astype(out[name].dtype))
    for name, factor in factors.items():
        out[name] = (out[name] * factor).astype(out[name].dtype)
    return out
```

```python
import math
from contextlib import ExitStack

import numpy as np
import concourse.bass as bass
from concourse import mybir

P = 128
IMAGES, PATCHES = 16, 64
TOKENS = IMAGES * PATCHES
TILES = TOKENS // P
C = 192
KH = C // 2
HEADS, HD = 12, 16
BLOCKS = 3
PAIRS = HEADS // 2
PATCH_IN = 768
KT_PATCH = PATCH_IN // P
BANK = 512
LN_EPS = 1e-5
MASKED = -1e30
ROUND = 1.5 * 2 ** 23
SEG = 16

F32 = mybir.dt.float32
BF16 = mybir.dt.bfloat16
I32 = mybir.dt.int32
U32 = mybir.dt.uint32
ALU = mybir.AluOpType
ACT = mybir.ActivationFunctionType
AX = mybir.AxisListType

CONST_COLS = [
    ("ident", 128), ("fold64", 64), ("fold128", 128), ("earlier", 128), ("ones", 128),
    ("causal_add", 64), ("causal01", 64), ("tail01", 64), ("seg_add", 8),
    ("cos", 8), ("sin", 8), ("nsin", 8), ("iota", 16),
    ("bv", 16), ("mn_w", 16), ("mn_b", 16), ("temperature", 1), ("l3_bias", C), ("wb2", 60),
]
CONST_AT = {}
_at = 0
for _n, _w in CONST_COLS:
    CONST_AT[_n] = (_at, _w)
    _at += _w
CONST_WIDTH = _at

SMALL_COLS = [("gate0", 8), ("gate1", 16), ("gate2", 8), ("wb1", 128),
              ("ln1_w", 1), ("ln1_b", 1), ("ln2_w", 1), ("ln2_b", 1), ("l2_w", 1), ("l2_b", 1)]
SMALL_AT = {}
_at = 0
for _n, _w in SMALL_COLS:
    SMALL_AT[_n] = (_at, _w)
    _at += _w
SMALL_WIDTH = _at

MOES = {
    "l0": dict(experts=8, up=6, hid=6, cap=320, weight="w_l0"),
    "l1": dict(experts=16, up=3, hid=3, cap=None, weight="w_l1"),
    "l2": dict(experts=8, up=8, hid=4, cap=320, weight="w_l2"),
}


class Signals(dict):

    def __init__(self, nc, ctx):
        super().__init__()
        self.nc, self.ctx, self.start = nc, ctx, {}

    def __missing__(self, name):
        self[name] = self.ctx.enter_context(self.nc.semaphore(name))
        self.start[name] = 0
        return self[name]

    def at(self, name):
        self[name]
        return self.start[name]

    def passed(self, **counts):
        for name, n in counts.items():
            self.start[name] += n


class Core:
    pass


def const(k, name):
    a, w = CONST_AT[name]
    return k.const[:, a:a + w]


def small(k, name):
    a, w = SMALL_AT[name]
    return k.small[:, :, a:a + w]


def bcast(ap, shape):
    return ap.to_broadcast(shape)


def allocate(nc, ctx):
    k = Core()
    k.nc = nc

    def sb(name, shape, dt=F32):
        return ctx.enter_context(nc.sbuf_tensor(name, shape, dt))

    k.S = Signals(nc, ctx)
    k.const = sb("const", [P, CONST_WIDTH])
    k.small = sb("small", [KH + 1, 2, SMALL_WIDTH])
    k.wattn = sb("wattn", [KH + 1, 2, 4 * C])
    k.h = sb("h", [P, TILES, C])
    k.x1 = sb("x1", [P, TILES, C])
    k.ht = sb("ht", [KH + 1, 2, TOKENS])
    k.xs = [sb(f"xs{u}", [P, C]) for u in (0, 1)]
    k.ys = [sb(f"ys{u}", [P, C]) for u in (0, 1)]
    k.stats = sb("stats", [P, 2, 6])
    k.meanvar = sb("meanvar", [P, 2, 2])
    k.vareps = sb("vareps", [P, 2])
    k.rstd = sb("rstd", [P, 2])
    k.pause = sb("pause", [P, 1])
    k.minus_half = sb("minus_half", [P, 2 * HEADS])
    k.ps = ctx.enter_context(nc.psum_tensor("ps", [P, 8, BANK], F32))
    return k


def bank(k, b):
    return k.ps[:, b, :]


def banks(k, b, n):
    return k.ps[:, b:b + n, :].rearrange("p b c -> p (b c)")


def load_constants(nc, k, io):
    S = k.S
    with nc.Block() as block:
        @block.sync
        def _(sp):
            sp.dma_start(k.const[:, :], io["const"]).then_inc(S["const_loaded"], 16)
            sp.dma_start(k.small[:, :, :], io["small"]).then_inc(S["const_loaded"], 16)
            sp.wait_ge(S["const_loaded"], 32)

        @block.gpsimd
        def _(pool):
            nc.gpsimd.memset(k.minus_half[:, :], -0.5)

        @block.vector
        def _(dve):
            nc.vector.memset(k.ht[KH:KH + 1, :, :], 1.0)


def embed(nc, k, io):
    S = k.S
    with ExitStack() as own:
        xt = own.enter_context(nc.sbuf_tensor("patches_t", [P, KT_PATCH, TOKENS], F32))
        w = own.enter_context(nc.sbuf_tensor("w_embed", [P, KT_PATCH, C], F32))
        block = own.enter_context(nc.Block())

        @block.sync
        def _(sp):
            sp.dma_start(w[:, :, :], io["w_embed"]).then_inc(S["w_embed_loaded"], 16)
            for kt in range(0, KT_PATCH, 2):
                sp.dma_start(xt[:, kt, :], io["patches_t"][kt]).then_inc(S[f"patches_loaded{kt}"], 16)

        @block.scalar
        def _(act):
            for kt in range(1, KT_PATCH, 2):
                act.dma_start(xt[:, kt, :], io["patches_t"][kt]).then_inc(S[f"patches_loaded{kt}"], 16)

        @block.tensor
        def _(pe):
            pe.wait_ge(S["w_embed_loaded"], 16)
            for kt in range(KT_PATCH):
                pe.wait_ge(S[f"patches_loaded{kt}"], 16)
                for t in range(TILES):
                    last = nc.tensor.matmul(bank(k, t)[:, 0:C], xt[:, kt, t * P:(t + 1) * P], w[:, kt, :],
                                            start=(kt == 0), stop=(kt == KT_PATCH - 1))
            last.then_inc(S["embedded"], 1)

        @block.vector
        def _(dve):
            dve.wait_ge(S["embedded"], 1)
            nc.vector.tensor_copy(k.h[:, :, :], k.ps[:, :, 0:C])


def ln_stats(nc, k, dve, rows, i, tag, eps=LN_EPS):
    S = k.S
    for u in (0, 1):
        last = nc.vector.bn_stats(k.stats[:, u, :], rows[u])
    last.then_inc(S[tag + "stats_ready"], 1)
    dve.wait_ge(S[tag + "stats_ready"], i + (S.at(tag + "stats_ready") + 1))
    nc.vector.memset(k.pause[:, :], 0.0)
    for u in (0, 1):
        last = nc.vector.bn_aggr(k.meanvar[:, u, :], k.stats[:, u, :])
    last.then_inc(S[tag + "meanvar_ready"], 1)
    dve.wait_ge(S[tag + "meanvar_ready"], i + (S.at(tag + "meanvar_ready") + 1))
    nc.vector.tensor_scalar_add(k.vareps[:, :], k.meanvar[:, :, 1], eps).then_inc(S[tag + "vareps_ready"], 1)


def ln_power(nc, k, pool, i, tag):
    S = k.S
    pool.wait_ge(S[tag + "vareps_ready"], i + (S.at(tag + "vareps_ready") + 1))
    nc.gpsimd.tensor_tensor(k.rstd[:, :], k.vareps[:, :], k.minus_half[:, 0:2], ALU.pow).then_inc(S[tag + "rstd_ready"], 1)


def ln_apply(nc, k, dve, u, dst, src, i, tag):
    S = k.S
    dve.wait_ge(S[tag + "rstd_ready"], i + (S.at(tag + "rstd_ready") + 1))
    return nc.vector.tensor_scalar(dst, src, k.meanvar[:, u, 0:1], k.rstd[:, u:u + 1], ALU.subtract, ALU.mult)


LN_SIGNALS = ("stats_ready", "meanvar_ready", "vareps_ready", "rstd_ready")


def allocate_attention(nc, k, ctx):
    def two(name, shape):
        return [ctx.enter_context(nc.sbuf_tensor(f"{name}{u}", shape, F32)) for u in (0, 1)]

    a = Core()
    a.xt = two("xt", [KH + 1, 2, P])
    a.qkv = two("qkv", [P, 3, C])
    a.wide = two("wide", [P, 3, HEADS, 2, HD])
    a.qt = two("qt", [P, BLOCKS, P])
    a.kt = two("kt", [P, BLOCKS, 4, PATCHES])
    a.vd = two("vd", [P, PAIRS, 2, 2, HD])
    a.sc = two("sc", [P, HEADS, PATCHES])
    a.pr = two("pr", [P, HEADS, PATCHES])
    a.prt = two("prt", [P, PAIRS, P])
    a.max = two("smax", [P, HEADS])
    a.sum = two("ssum", [P, HEADS])
    a.rsum = two("rsum", [P, HEADS])
    a.seg = two("seg", [P, HEADS, 8])
    a.segp = two("segp", [P, HEADS, 8])
    a.os = two("os", [P, HEADS, HD])
    a.ot = two("ot", [KH + 1, 2, P])
    a.t24 = two("t24", [P, 2 * HEADS])
    a.r24 = two("r24", [P, 2 * HEADS])
    a.tmp = two("tmp", [P, 2, HEADS, HD])
    a.tmp2 = two("tmp2", [P, 2, HEADS, HD])
    a.gate1 = ctx.enter_context(nc.sbuf_tensor("gate1", [P, TILES, HEADS], F32))
    k.a = a


def clear_attention(nc, k):
    a = k.a
    with nc.Block() as block:
        @block.gpsimd
        def _(pool):
            for u in (0, 1):
                nc.gpsimd.memset(a.wide[u][:, :, :, :, :], 0.0)

        @block.vector
        def _(dve):
            for u in (0, 1):
                nc.vector.memset(a.kt[u][:, :, :, :], 0.0)
                nc.vector.memset(a.vd[u][:, :, :, :, :], 0.0)
                nc.vector.memset(a.xt[u][KH:KH + 1, :, :], 1.0)
                nc.vector.memset(a.ot[u][KH:KH + 1, :, :], 1.0)


def attention(nc, k, io, layer, kind, pre_ln=None, keep=False):
    S, a = k.S, k.a
    scale = {"softmax": HD ** -0.5, "segments": HD ** -0.5, "rotary": 0.12, "linear": 1.0}[kind]
    raw = kind == "softmax"
    psum = lambda u, b: bank(k, 4 * u + b)
    two = (0, 1)

    with ExitStack() as own:
        if kind == "segments":
            bil_w = own.enter_context(nc.sbuf_tensor("bil_w", [KH, PAIRS * 2 // 2, 256], F32))
            kft = [own.enter_context(nc.sbuf_tensor(f"kft{u}", [KH, 2, P], F32)) for u in two]
            prod = [own.enter_context(nc.sbuf_tensor(f"prod{u}", [P, HEADS, HD, HD], F32)) for u in two]
        block = own.enter_context(nc.Block())

        def n(name, i, u, each=1, more=0):
            return i * (2 * each) + (S.at(name) + u * each + more + 1)

        @block.sync
        def _(sp):
            sp.dma_start(k.wattn[:, :, :], io["wattn"][layer]).then_inc(S["wattn_loaded"], 16)
            if kind == "segments":
                sp.dma_start(bil_w[:, :, :], io["bil_w"]).then_inc(S["bil_w_loaded"], 16)

        @block.tensor
        def _(pe):
            pe.wait_ge(S["wattn_loaded"], S.at("wattn_loaded") + 16)
            if kind == "segments":
                pe.wait_ge(S["bil_w_loaded"], 16)
            ident = const(k, "ident")
            with pe.Fori(0, TILES // 2) as i:
                for u in two:
                    pe.wait_ge(S["x_ready"], n("x_ready", i, u))
                    for f in two:
                        last = nc.tensor.transpose(psum(u, 0)[0:KH, f * P:(f + 1) * P],
                                                   k.xs[u][:, f * KH:(f + 1) * KH], ident)
                    last.then_inc(S["x_turned"], 1)
                for u in two:
                    pe.wait_ge(S["xt_ready"], n("xt_ready", i, u))
                    for c in range(3):
                        for f in two:
                            out = banks(k, 4 * u + 2, 2)[:, c * 256:c * 256 + C]
                            last = nc.tensor.matmul(out, a.xt[u][0:KH + f, f, :],
                                                    k.wattn[0:KH + f, f, c * C:(c + 1) * C],
                                                    start=(f == 0), stop=(f == 1))
                    last.then_inc(S["qkv_projected"], 1)
                if kind == "segments":
                    for u in two:
                        pe.wait_ge(S["qkv_ready"], n("qkv_ready", i, u))
                        for f in two:
                            last = nc.tensor.transpose(psum(u, 0)[0:KH, f * P:(f + 1) * P],
                                                       a.qkv[u][:, 1, f * KH:(f + 1) * KH], ident)
                        last.then_inc(S["k_turned"], 1)
                    for c in range(6):
                        for u in two:
                            if c == 0:
                                pe.wait_ge(S["kft_ready"], n("kft_ready", i, u))
                            if c >= 3:
                                pe.wait_ge(S[f"bil_used{u}"], i * 6 + (S.at(f"bil_used{u}") + c - 2))
                            nc.tensor.matmul(psum(u, 1 + c % 3)[:, :], kft[u][:, c // 3, :],
                                             bil_w[:, 2 * (c % 3):2 * (c % 3) + 2, :].rearrange("p a b -> p (a b)"),
                                             start=True, stop=True).then_inc(S["bil_ready"], 1)
                for u in two:
                    pe.wait_ge(S["wide_ready"], n("wide_ready", i, u))
                    wide = a.wide[u][:, :, :, :, :].rearrange("p c h b d -> p c (h b d)")
                    for m in range(BLOCKS):
                        nc.tensor.transpose(psum(u, 2)[:, m * P:(m + 1) * P],
                                            wide[:, 0, m * P:(m + 1) * P], ident)
                    for m in range(BLOCKS):
                        nc.tensor.matmul(psum(u, 3)[:, m * PATCHES:(m + 1) * PATCHES],
                                         wide[:, 1, m * P:(m + 1) * P], const(k, "fold64"),
                                         start=True, stop=True)
                    nc.tensor.matmul(psum(u, 1)[:, 0:2 * C], const(k, "fold128"), wide[:, 2, :],
                                     start=True, stop=True).then_inc(S["folded"], 1)
                for u in two:
                    pe.wait_ge(S["qk_ready"], n("qk_ready", i, u))
                    pe.wait_ge(S["vd_ready"], n("vd_ready", i, u))
                    for m in range(BLOCKS):
                        last = nc.tensor.matmul(banks(k, 4 * u, 2)[:, m * 256:(m + 1) * 256], a.qt[u][:, m, :],
                                                a.kt[u][:, m, :, :].rearrange("p h t -> p (h t)"),
                                                start=True, stop=True)
                    last.then_inc(S["scored"], 1)
                for u in two:
                    ready = "p_ready" if kind in ("linear", "segments") else "exped"
                    pe.wait_ge(S[ready], n(ready, i, u))
                    for p in range(PAIRS):
                        last = nc.tensor.transpose(banks(k, 4 * u, 2)[:, p * P:(p + 1) * P],
                                                   a.pr[u][:, 2 * p:2 * p + 2, :].rearrange("p h t -> p (h t)"), ident)
                    last.then_inc(S["p_turned"], 1)
                for u in two:
                    pe.wait_ge(S["prt_ready"], n("prt_ready", i, u))
                    for p in range(PAIRS):
                        last = nc.tensor.matmul(psum(u, 2)[:, p * 64:(p + 1) * 64], a.prt[u][:, p, :],
                                                a.vd[u][:, p, :, :, :].rearrange("p a b d -> p (a b d)"),
                                                start=True, stop=True)
                    last.then_inc(S["mixed"], 1)
                for u in two:
                    pe.wait_ge(S["os_ready"], n("os_ready", i, u))
                    os = a.os[u][:, :, :].rearrange("p h d -> p (h d)")
                    for f in two:
                        last = nc.tensor.transpose(psum(u, 3)[0:KH, f * P:(f + 1) * P],
                                                   os[:, f * KH:(f + 1) * KH], ident)
                    last.then_inc(S["o_turned"], 1)
                for u in two:
                    pe.wait_ge(S["ot_ready"], n("ot_ready", i, u))
                    for f in two:
                        last = nc.tensor.matmul(psum(u, 3)[:, 256:256 + C], a.ot[u][0:KH + f, f, :],
                                                k.wattn[0:KH + f, f, 3 * C:4 * C], start=(f == 0), stop=(f == 1))
                    last.then_inc(S["projected"], 1)

        @block.scalar
        def _(act):
            with act.Fori(0, TILES // 2) as i:
                for u in two:
                    act.wait_ge(S["x_turned"], n("x_turned", i, u))
                    if pre_ln:
                        for f in two:
                            last = nc.scalar.activation(a.xt[u][0:KH, f, :], psum(u, 0)[0:KH, f * P:(f + 1) * P],
                                                        ACT.Identity, scale=small(k, pre_ln + "_w")[0:KH, f, :],
                                                        bias=small(k, pre_ln + "_b")[0:KH, f, :])
                    else:
                        last = nc.scalar.activation(a.xt[u][0:KH, :, :].rearrange("p f t -> p (f t)"),
                                                    psum(u, 0)[0:KH, 0:2 * P], ACT.Copy)
                    last.then_inc(S["xt_ready"], 1)
                for u in two:
                    act.wait_ge(S["qkv_projected"], n("qkv_projected", i, u))
                    src = k.ps[:, 4 * u + 2:4 * u + 4, :].rearrange("p b (c x) -> p (b c) x", c=2)
                    if raw:
                        for b in two:
                            r = slice(64 * b, 64 * b + 64)
                            last = nc.scalar.activation(
                                a.wide[u][r, :, :, b, :],
                                src[r, 0:3, 0:C].rearrange("p c (h d) -> p c h d", d=HD), ACT.Copy)
                        last.then_inc(S["wide_ready"], 1)
                    else:
                        nc.scalar.activation(a.qkv[u][:, :, :], src[:, 0:3, 0:C], ACT.Copy).then_inc(S["qkv_ready"], 1)
                if kind == "linear":
                    for u in two:
                        act.wait_ge(S["clipped"], n("clipped", i, u))
                        nc.scalar.activation(a.tmp2[u][:, :, :, :], a.tmp[u][:, :, :, :], ACT.Exp).then_inc(S["elu_exp"], 1)
                if kind == "segments":
                    for u in two:
                        act.wait_ge(S["k_turned"], n("k_turned", i, u))
                        nc.scalar.activation(kft[u][:, :, :].rearrange("p f t -> p (f t)"),
                                             psum(u, 0)[0:KH, 0:2 * P], ACT.Copy).then_inc(S["kft_ready"], 1)
                for u in two:
                    act.wait_ge(S["folded"], n("folded", i, u))
                    nc.scalar.activation(a.qt[u][:, :, :].rearrange("p m t -> p (m t)"), psum(u, 2)[:, 0:3 * P], ACT.Copy)
                    for j in range(4):
                        r = slice(32 * j, 32 * j + 32)
                        last = nc.scalar.activation(a.kt[u][r, :, j, :],
                                                    psum(u, 3)[r, 0:BLOCKS * PATCHES].rearrange("p (m t) -> p m t", m=BLOCKS),
                                                    ACT.Copy)
                    last.then_inc(S["qk_ready"], 1)
                if kind != "linear":
                    for u in two:
                        act.wait_ge(S["centred"], n("centred", i, u))
                        src, dst = (a.seg, a.segp) if kind == "segments" else (a.sc, a.pr)
                        nc.scalar.activation(dst[u][:, :, :], src[u][:, :, :], ACT.Exp, scale=scale).then_inc(S["exped"], 1)
                for u in two:
                    act.wait_ge(S["p_turned"], n("p_turned", i, u))
                    nc.scalar.activation(a.prt[u][:, :, :].rearrange("p a t -> p (a t)"),
                                         banks(k, 4 * u, 2)[:, 0:PAIRS * P], ACT.Copy).then_inc(S["prt_ready"], 1)
                for u in two:
                    act.wait_ge(S["o_turned"], n("o_turned", i, u))
                    nc.scalar.activation(a.ot[u][0:KH, :, :].rearrange("p f t -> p (f t)"),
                                         psum(u, 3)[0:KH, 0:2 * P], ACT.Copy).then_inc(S["ot_ready"], 1)

        @block.gpsimd
        def _(pool):
            with pool.Fori(0, TILES // 2) as i:
                if pre_ln:
                    ln_power(nc, k, pool, i, "in_")
                else:
                    for u in two:
                        nc.gpsimd.tensor_copy(k.xs[u][:, :], k.h[:, bass.ds(i * 2 + u, 1), :].rearrange("p a c -> p (a c)")).then_inc(S["x_ready"], 1)
                if kind == "rotary":
                    for u in two:
                        pool.wait_ge(S["ms_ready"], n("ms_ready", i, u))
                        nc.gpsimd.tensor_tensor(a.r24[u][:, :], a.t24[u][:, :], k.minus_half[:, :], ALU.pow).then_inc(S["rms_ready"], 1)
                if kind != "linear":
                    for u in two:
                        pool.wait_ge(S["max_ready"], n("max_ready", i, u))
                        s, w = (a.seg, 8) if kind == "segments" else (a.sc, PATCHES)
                        nc.gpsimd.tensor_tensor(s[u][:, :, :], s[u][:, :, :],
                                                bcast(a.max[u][:, :].unsqueeze(2), [P, HEADS, w]),
                                                ALU.subtract).then_inc(S["centred"], 1)
                else:
                    for u in two:
                        pool.wait_ge(S["hvar_ready"], n("hvar_ready", i, u))
                        nc.gpsimd.tensor_tensor(a.r24[u][:, 0:HEADS], a.t24[u][:, 0:HEADS], k.minus_half[:, 0:HEADS],
                                                ALU.pow).then_inc(S["hrstd_ready"], 1)
                if not keep:
                    ln_power(nc, k, pool, i, "out_")

        @block.vector
        def _(dve):
            with dve.Fori(0, TILES // 2) as i:
                tile_of = lambda t, u: t[:, bass.ds(i * 2 + u, 1), :].rearrange("p a c -> p (a c)")
                if pre_ln:
                    ln_stats(nc, k, dve, [tile_of(k.h, u) for u in two], i, "in_")
                    for u in two:
                        ln_apply(nc, k, dve, u, k.xs[u][:, :], tile_of(k.h, u), i, "in_").then_inc(S["x_ready"], 1)
                if kind == "segments":
                    for u in two:
                        dve.wait_ge(S["qkv_ready"], n("qkv_ready", i, u))
                    for c in range(6):
                        for u in two:
                            dve.wait_ge(S["bil_ready"], i * 12 + (S.at("bil_ready") + 2 * c + u + 1))
                            v0 = a.qkv[u][:, 2, 32 * c:32 * c + 32].rearrange("p (h d) -> p h d", h=2)
                            nc.vector.tensor_tensor(
                                prod[u][:, 2 * c:2 * c + 2, :, :],
                                psum(u, 1 + c % 3).rearrange("p (h e j) -> p h e j", h=2, e=HD),
                                bcast(v0.unsqueeze(2), [P, 2, HD, HD]), ALU.mult).then_inc(S[f"bil_used{u}"], 1)
                    for u in two:
                        dve.wait_ge(S[f"bil_used{u}"], i * 6 + (S.at(f"bil_used{u}") + 6))
                        nc.vector.tensor_reduce(a.tmp[u][:, 0, :, :].rearrange("p h e -> p (h e)"),
                                                prod[u][:, :, :, :].rearrange("p h e j -> p (h e) j"),
                                                AX.X, ALU.add).then_inc(S["v_summed"], 1)
                    for u in two:
                        dve.wait_ge(S["v_summed"], n("v_summed", i, u))
                        for b in two:
                            r = slice(64 * b, 64 * b + 64)
                            nc.vector.tensor_tensor(a.wide[u][r, 2, :, b, :], a.tmp[u][r, 0, :, :],
                                                    bcast(const(k, "bv")[r, :].unsqueeze(1), [64, HEADS, HD]), ALU.add)
                            last = nc.vector.tensor_copy(a.wide[u][r, 0:2, :, b, :].rearrange("p c h d -> p c h d"),
                                                         a.qkv[u][r, 0:2, :].rearrange("p c (h d) -> p c h d", d=HD))
                        last.then_inc(S["wide_ready"], 1)
                if kind == "linear":
                    for u in two:
                        dve.wait_ge(S["qkv_ready"], n("qkv_ready", i, u))
                        nc.vector.tensor_scalar_min(a.tmp[u][:, :, :, :].rearrange("p c h d -> p (c h d)"),
                                                    a.qkv[u][:, 0:2, :].rearrange("p c x -> p (c x)"), 0.0).then_inc(S["clipped"], 1)
                    for u in two:
                        g = k.a.gate1[:, bass.ds(i * 2 + u, 1), :].rearrange("p a h -> p (a h)")
                        dve.wait_ge(S["elu_exp"], n("elu_exp", i, u))
                        for b in two:
                            r = slice(64 * b, 64 * b + 64)
                            for c in two:
                                nc.vector.scalar_tensor_tensor(
                                    out=a.wide[u][r, c, :, b, :],
                                    in0=a.qkv[u][r, c, :].rearrange("p (h d) -> p h d", d=HD), scalar=0.0,
                                    in1=a.tmp2[u][r, c, :, :], op0=ALU.max, op1=ALU.add)
                            last = nc.vector.tensor_tensor(a.wide[u][r, 2, :, b, :],
                                                           a.qkv[u][r, 2, :].rearrange("p (h d) -> p h d", d=HD),
                                                           bcast(g[r, :].unsqueeze(2), [64, HEADS, HD]), ALU.mult)
                        last.then_inc(S["wide_ready"], 1)
                if kind == "rotary":
                    for u in two:
                        dve.wait_ge(S["qkv_ready"], n("qkv_ready", i, u))
                        qk = a.qkv[u][:, 0:2, :].rearrange("p c x -> p (c x)")
                        nc.vector.tensor_tensor(a.tmp[u][:, :, :, :].rearrange("p c h d -> p (c h d)"), qk, qk,
                                                ALU.mult).then_inc(S["squared"], 1)
                    for u in two:
                        dve.wait_ge(S["squared"], n("squared", i, u))
                        nc.vector.tensor_reduce(a.r24[u][:, :], a.tmp[u][:, :, :, :].rearrange("p c h d -> p (c h) d"),
                                                AX.X, ALU.add).then_inc(S["square_sums"], 1)
                    for u in two:
                        dve.wait_ge(S["square_sums"], n("square_sums", i, u))
                        nc.vector.tensor_scalar(a.t24[u][:, :], a.r24[u][:, :], 1.0 / HD, 1.1920928955078125e-07,
                                                ALU.mult, ALU.add).then_inc(S["ms_ready"], 1)
                    for u in two:
                        dve.wait_ge(S["rms_ready"], n("rms_ready", i, u))
                        nc.vector.tensor_tensor(a.tmp[u][:, :, :, :].rearrange("p c h d -> p (c h) d"),
                                                a.qkv[u][:, 0:2, :].rearrange("p c (h d) -> p (c h) d", d=HD),
                                                bcast(a.r24[u][:, :].unsqueeze(2), [P, 2 * HEADS, HD]),
                                                ALU.mult).then_inc(S["normed"], 1)
                    for u in two:
                        dve.wait_ge(S["normed"], n("normed", i, u))
                        x = a.tmp[u][:, :, :, :].rearrange("p c h d -> p (c h) d")
                        y = a.tmp2[u][:, :, :, :].rearrange("p c h d -> p (c h) d")
                        sh = [P, 2 * HEADS, HD // 2]
                        nc.vector.tensor_tensor(y[:, :, 0:8], x[:, :, 8:16], bcast(const(k, "sin").unsqueeze(1), sh), ALU.mult)
                        last = nc.vector.tensor_tensor(y[:, :, 8:16], x[:, :, 0:8], bcast(const(k, "nsin").unsqueeze(1), sh), ALU.mult)
                        last.then_inc(S["crossed"], 1)
                    for u in two:
                        dve.wait_ge(S["crossed"], n("crossed", i, u))
                        x4 = a.tmp[u][:, :, :, :].rearrange("p c h (s d) -> p (c h s) d", s=2)
                        nc.vector.tensor_tensor(x4, x4, bcast(const(k, "cos").unsqueeze(1), [P, 4 * HEADS, HD // 2]),
                                                ALU.mult).then_inc(S["cosined"], 1)
                    for u in two:
                        dve.wait_ge(S["cosined"], n("cosined", i, u))
                        for b in two:
                            r = slice(64 * b, 64 * b + 64)
                            nc.vector.tensor_tensor(a.wide[u][r, 0:2, :, b, :].rearrange("p c h d -> p c h d"),
                                                    a.tmp[u][r, :, :, :], a.tmp2[u][r, :, :, :], ALU.add)
                            last = nc.vector.tensor_copy(a.wide[u][r, 2, :, b, :],
                                                         a.qkv[u][r, 2, :].rearrange("p (h d) -> p h d", d=HD))
                        last.then_inc(S["wide_ready"], 1)
                for u in two:
                    dve.wait_ge(S["folded"], n("folded", i, u))
                    v = psum(u, 1)[:, 0:2 * C].rearrange("p (a h b d) -> p a h b d", a=PAIRS, h=2, b=2)
                    for h in two:
                        r = slice(64 * h, 64 * h + 64)
                        last = nc.vector.tensor_copy(a.vd[u][r, :, h, :, :].rearrange("p a b d -> p a (b d)"),
                                                     v[r, :, h, :, :].rearrange("p a b d -> p a (b d)"))
                    last.then_inc(S["vd_ready"], 1)

                score = lambda u: banks(k, 4 * u, 2)[:, 0:HEADS * PATCHES].rearrange("p (h t) -> p h t", t=PATCHES)
                every = [P, HEADS, PATCHES]
                if kind in ("softmax", "rotary"):
                    for u in two:
                        dve.wait_ge(S["scored"], n("scored", i, u))
                        nc.vector.tensor_tensor(a.sc[u][:, :, :], score(u), bcast(const(k, "causal_add").unsqueeze(1), every),
                                                ALU.add).then_inc(S["masked"], 1)
                    for u in two:
                        dve.wait_ge(S["masked"], n("masked", i, u))
                        nc.vector.tensor_reduce(a.max[u][:, :], a.sc[u][:, :, :], AX.X, ALU.max).then_inc(S["max_ready"], 1)
                    for u in two:
                        dve.wait_ge(S["exped"], n("exped", i, u))
                        nc.vector.tensor_reduce(a.sum[u][:, :], a.pr[u][:, :, :], AX.X, ALU.add).then_inc(S["p_ready"], 1)
                    for u in two:
                        dve.wait_ge(S["p_ready"], n("p_ready", i, u))
                        nc.vector.reciprocal(a.rsum[u][:, :], a.sum[u][:, :]).then_inc(S["rsum_ready"], 1)
                if kind == "linear":
                    for u in two:
                        dve.wait_ge(S["scored"], n("scored", i, u))
                        nc.vector.tensor_tensor(a.pr[u][:, :, :], score(u), bcast(const(k, "causal01").unsqueeze(1), every),
                                                ALU.mult).then_inc(S["p_ready"], 1)
                    for u in two:
                        dve.wait_ge(S["p_ready"], n("p_ready", i, u))
                        nc.vector.tensor_reduce(a.sum[u][:, :], a.pr[u][:, :, :], AX.X, ALU.add).then_inc(S["masked"], 1)
                    for u in two:
                        dve.wait_ge(S["masked"], n("masked", i, u))
                        nc.vector.tensor_scalar_add(a.max[u][:, :], a.sum[u][:, :], 1e-6).then_inc(S["max_ready"], 1)
                    for u in two:
                        dve.wait_ge(S["max_ready"], n("max_ready", i, u))
                        nc.vector.reciprocal(a.rsum[u][:, :], a.max[u][:, :]).then_inc(S["rsum_ready"], 1)
                if kind == "segments":
                    for u in two:
                        dve.wait_ge(S["scored"], n("scored", i, u))
                        nc.vector.tensor_reduce(a.seg[u][:, :, 0:4], score(u).rearrange("p h (s t) -> p h s t", t=SEG),
                                                AX.X, ALU.add).then_inc(S["seg16"], 1)
                    for u in two:
                        nc.vector.tensor_tensor(a.sc[u][:, :, :], score(u), bcast(const(k, "tail01").unsqueeze(1), every),
                                                ALU.mult).then_inc(S["masked"], 1)
                    for u in two:
                        dve.wait_ge(S["seg16"], n("seg16", i, u))
                        pairs = a.seg[u][:, :, 0:4].rearrange("p h (s t) -> p h s t", t=2)
                        nc.vector.tensor_tensor(a.seg[u][:, :, 4:6], pairs[:, :, :, 0], pairs[:, :, :, 1],
                                                ALU.add).then_inc(S["seg32"], 1)
                    for u in two:
                        dve.wait_ge(S["masked"], n("masked", i, u))
                        nc.vector.tensor_reduce(a.seg[u][:, :, 7:8], a.sc[u][:, :, :], AX.X, ALU.add)
                    for u in two:
                        dve.wait_ge(S["seg32"], n("seg32", i, u))
                        nc.vector.tensor_tensor(a.seg[u][:, :, 6:7], a.seg[u][:, :, 4:5], a.seg[u][:, :, 5:6],
                                                ALU.add).then_inc(S["seg64"], 1)
                    for u in two:
                        dve.wait_ge(S["seg64"], n("seg64", i, u))
                        nc.vector.tensor_tensor(a.seg[u][:, :, :], a.seg[u][:, :, :],
                                                bcast(const(k, "seg_add").unsqueeze(1), [P, HEADS, 8]),
                                                ALU.add).then_inc(S["seg_masked"], 1)
                    for u in two:
                        dve.wait_ge(S["seg_masked"], n("seg_masked", i, u))
                        nc.vector.tensor_reduce(a.max[u][:, :], a.seg[u][:, :, :], AX.X, ALU.max).then_inc(S["max_ready"], 1)
                    for u in two:
                        dve.wait_ge(S["exped"], n("exped", i, u))
                        nc.vector.tensor_reduce(a.sum[u][:, :], a.segp[u][:, :, :], AX.X, ALU.add).then_inc(S["sum_ready"], 1)
                    for u in two:
                        w4 = a.seg[u][:, :, 0:4].rearrange("p h (s t) -> p h s t", t=2)
                        nc.vector.tensor_tensor(w4, a.segp[u][:, :, 0:4].rearrange("p h (s t) -> p h s t", t=2),
                                                bcast(a.segp[u][:, :, 4:6].unsqueeze(3), [P, HEADS, 2, 2]),
                                                ALU.add).then_inc(S["w32"], 1)
                        nc.vector.tensor_tensor(a.sc[u][:, :, :], bcast(const(k, "tail01").unsqueeze(1), every),
                                                bcast(a.segp[u][:, :, 7:8], every), ALU.mult).then_inc(S["tail_ready"], 1)
                    for u in two:
                        dve.wait_ge(S["sum_ready"], n("sum_ready", i, u))
                        nc.vector.reciprocal(a.rsum[u][:, :], a.sum[u][:, :]).then_inc(S["rsum_ready"], 1)
                        dve.wait_ge(S["w32"], n("w32", i, u))
                        nc.vector.tensor_tensor(a.seg[u][:, :, 0:4], a.seg[u][:, :, 0:4],
                                                bcast(a.segp[u][:, :, 6:7], [P, HEADS, 4]), ALU.add).then_inc(S["w64"], 1)
                    for u in two:
                        dve.wait_ge(S["w64"], n("w64", i, u))
                        dve.wait_ge(S["tail_ready"], n("tail_ready", i, u))
                        nc.vector.tensor_tensor(a.pr[u][:, :, :].rearrange("p h (s t) -> p h s t", t=SEG),
                                                a.sc[u][:, :, :].rearrange("p h (s t) -> p h s t", t=SEG),
                                                bcast(a.seg[u][:, :, 0:4].unsqueeze(3), [P, HEADS, 4, SEG]),
                                                ALU.add).then_inc(S["p_ready"], 1)
                for u in two:
                    dve.wait_ge(S["rsum_ready"], n("rsum_ready", i, u))
                    dve.wait_ge(S["mixed"], n("mixed", i, u))
                    o = psum(u, 2)[:, 0:2 * C].rearrange("p (h b d) -> p h b d", b=2, d=HD)
                    for b in two:
                        r = slice(64 * b, 64 * b + 64)
                        last = nc.vector.tensor_tensor(a.os[u][r, :, :], o[r, :, b, :],
                                                       bcast(a.rsum[u][r, :].unsqueeze(2), [64, HEADS, HD]), ALU.mult)
                    last.then_inc(S["o_scaled" if kind == "linear" else "os_ready"], 1)
                if kind == "linear":
                    heads = [P, HEADS, HD]
                    for u in two:
                        dve.wait_ge(S["o_scaled"], n("o_scaled", i, u))
                        nc.vector.tensor_reduce(a.sum[u][:, :], a.os[u][:, :, :], AX.X, ALU.add).then_inc(S["hsum"], 1)
                    for u in two:
                        dve.wait_ge(S["hsum"], n("hsum", i, u))
                        nc.vector.tensor_scalar_mul(a.sum[u][:, :], a.sum[u][:, :], 1.0 / HD).then_inc(S["hmean"], 1)
                    for u in two:
                        dve.wait_ge(S["hmean"], n("hmean", i, u))
                        nc.vector.tensor_tensor(a.os[u][:, :, :], a.os[u][:, :, :], bcast(a.sum[u][:, :].unsqueeze(2), heads),
                                                ALU.subtract).then_inc(S["hcentred"], 1)
                    for u in two:
                        dve.wait_ge(S["hcentred"], n("hcentred", i, u))
                        nc.vector.tensor_tensor(a.tmp[u][:, 0, :, :], a.os[u][:, :, :], a.os[u][:, :, :],
                                                ALU.mult).then_inc(S["hsquared"], 1)
                    for u in two:
                        dve.wait_ge(S["hsquared"], n("hsquared", i, u))
                        nc.vector.tensor_reduce(a.sum[u][:, :], a.tmp[u][:, 0, :, :], AX.X, ALU.add).then_inc(S["hsqsum"], 1)
                    for u in two:
                        dve.wait_ge(S["hsqsum"], n("hsqsum", i, u))
                        nc.vector.tensor_scalar(a.t24[u][:, 0:HEADS], a.sum[u][:, :], 1.0 / HD, LN_EPS,
                                                ALU.mult, ALU.add).then_inc(S["hvar_ready"], 1)
                    for u in two:
                        dve.wait_ge(S["hrstd_ready"], n("hrstd_ready", i, u))
                        nc.vector.tensor_tensor(a.os[u][:, :, :], a.os[u][:, :, :],
                                                bcast(a.r24[u][:, 0:HEADS].unsqueeze(2), heads), ALU.mult).then_inc(S["hnormed"], 1)
                    for u in two:
                        dve.wait_ge(S["hnormed"], n("hnormed", i, u))
                        nc.vector.tensor_tensor(a.os[u][:, :, :], a.os[u][:, :, :],
                                                bcast(const(k, "mn_w").unsqueeze(1), heads), ALU.mult).then_inc(S["hweighted"], 1)
                    for u in two:
                        dve.wait_ge(S["hweighted"], n("hweighted", i, u))
                        nc.vector.tensor_tensor(a.os[u][:, :, :], a.os[u][:, :, :],
                                                bcast(const(k, "mn_b").unsqueeze(1), heads), ALU.add).then_inc(S["os_ready"], 1)
                for u in two:
                    dve.wait_ge(S["projected"], n("projected", i, u))
                    nc.vector.tensor_tensor(tile_of(k.x1, u) if keep else k.ys[u][:, :], tile_of(k.h, u),
                                            psum(u, 3)[:, 256:256 + C], ALU.add).then_inc(S["y_ready"], 1)
                if not keep:
                    dve.wait_ge(S["y_ready"], n("y_ready", i, 1))
                    ln_stats(nc, k, dve, [y[:, :] for y in k.ys], i, "out_")
                    for u in two:
                        ln_apply(nc, k, dve, u, tile_of(k.h, u), k.ys[u][:, :], i, "out_")

    both = ["x_ready", "x_turned", "xt_ready", "qkv_projected", "wide_ready", "folded", "qk_ready", "vd_ready",
            "scored", "p_ready", "p_turned", "prt_ready", "mixed", "os_ready", "o_turned", "ot_ready",
            "projected", "y_ready", "rsum_ready", "masked", "max_ready"]
    pairs = ["in_" + x for x in LN_SIGNALS if pre_ln] + ["out_" + x for x in LN_SIGNALS if not keep]
    if kind != "softmax":
        both.append("qkv_ready")
    if kind != "linear":
        both += ["centred", "exped"]
    S.passed(wattn_loaded=16, **dict.fromkeys(both, TILES), **dict.fromkeys(pairs, TILES // 2))


def turn(nc, k, source, target, kind="raw"):
    S = k.S
    two = (0, 1)
    block_of = k.nc.Block()
    with block_of as block:
        def n(name, i, u):
            return i * 2 + (S.at(name) + u + 1)

        @block.vector
        def _(dve):
            with dve.Fori(0, TILES // 2) as i:
                tile_of = lambda t, u: t[:, bass.ds(i * 2 + u, 1), :].rearrange("p a c -> p (a c)")
                if kind == "raw":
                    for u in two:
                        dve.wait_ge(S["x_turned"], n("x_turned", i, u))
                        nc.vector.tensor_copy(k.xs[u][:, :], tile_of(source, u)).then_inc(S["x_ready"], 1)
                if kind == "ln2":
                    ln_stats(nc, k, dve, [tile_of(source, u) for u in two], i, "in_")
                    for u in two:
                        dve.wait_ge(S["x_turned"], n("x_turned", i, u))
                        ln_apply(nc, k, dve, u, k.xs[u][:, :], tile_of(source, u), i, "in_").then_inc(S["x_ready"], 1)
                if kind == "rms":
                    once = lambda name: i + (S.at(name) + 1)
                    for u in two:
                        last = nc.vector.tensor_tensor(k.ys[u][:, :], tile_of(source, u), tile_of(source, u), ALU.mult)
                    last.then_inc(S["in_stats_ready"], 1)
                    dve.wait_ge(S["in_stats_ready"], once("in_stats_ready"))
                    for u in two:
                        last = nc.vector.tensor_reduce(k.meanvar[:, u, 0:1], k.ys[u][:, :], AX.X, ALU.add)
                    last.then_inc(S["in_meanvar_ready"], 1)
                    dve.wait_ge(S["in_meanvar_ready"], once("in_meanvar_ready"))
                    nc.vector.tensor_scalar(k.vareps[:, :], k.meanvar[:, :, 0], 4.0 / C, 1e-6,
                                            ALU.mult, ALU.add).then_inc(S["in_vareps_ready"], 1)
                    dve.wait_ge(S["in_rstd_ready"], once("in_rstd_ready"))
                    for u in two:
                        dve.wait_ge(S["x_turned"], n("x_turned", i, u))
                        nc.vector.tensor_scalar(k.xs[u][:, :], tile_of(source, u), k.rstd[:, u:u + 1], 2.0,
                                                ALU.mult, ALU.mult).then_inc(S["x_ready"], 1)

        if kind != "raw":
            @block.gpsimd
            def _(pool):
                with pool.Fori(0, TILES // 2) as i:
                    ln_power(nc, k, pool, i, "in_")

        @block.tensor
        def _(pe):
            pe.sem_inc(S["x_turned"], 2)
            with pe.Fori(0, TILES // 2) as i:
                for u in two:
                    pe.wait_ge(S["x_ready"], n("x_ready", i, u))
                    pe.wait_ge(S["turned_free"], n("turned_free", i, u))
                    for f in two:
                        last = nc.tensor.transpose(bank(k, u)[0:KH, f * P:(f + 1) * P],
                                                   k.xs[u][:, f * KH:(f + 1) * KH], const(k, "ident"))
                    last.then_inc(S["x_turned"], 1)

        @block.scalar
        def _(act):
            act.sem_inc(S["turned_free"], 2)
            with act.Fori(0, TILES // 2) as i:
                for u in two:
                    act.wait_ge(S["x_turned"], n("x_turned", i, u + 2))
                    for f in two:
                        dst = target[0:KH, f, bass.ds(i * (2 * P) + u * P, P)]
                        src = bank(k, u)[0:KH, f * P:(f + 1) * P]
                        if kind == "ln2":
                            last = nc.scalar.activation(dst, src, ACT.Identity, scale=small(k, "ln2_w")[0:KH, f, :],
                                                        bias=small(k, "ln2_b")[0:KH, f, :])
                        else:
                            last = nc.scalar.activation(dst, src, ACT.Copy)
                    last.then_inc(S["turned_free"], 1)
    pairs = ["in_" + x for x in LN_SIGNALS] if kind != "raw" else []
    S.passed(**dict.fromkeys(pairs, TILES // 2), x_ready=TILES, x_turned=TILES + 2, turned_free=TILES + 2)


def gates(nc, k):
    S, a = k.S, k.a
    with ExitStack() as own:
        sb = lambda name, shape: own.enter_context(nc.sbuf_tensor(name, shape, F32))
        hidden = sb("gate_hidden", [P, TOKENS])
        params = sb("gate_params", [P, TILES, 5, HEADS])
        amp = sb("gate_amp", [P, 2, TILES, HEADS])
        phase = sb("gate_phase", [P, 2, TILES, HEADS])
        temp = sb("gate_temp", [P, 1])
        block = own.enter_context(nc.Block())

        @block.tensor
        def _(pe):
            for g in range(2):
                for f in range(2):
                    last = nc.tensor.matmul(bank(k, g), small(k, "wb1")[0:KH, f, :], k.ht[0:KH, f, g * BANK:(g + 1) * BANK],
                                            start=(f == 0), stop=(f == 1))
            last.then_inc(S["gate_up"], 1)
            pe.wait_ge(S["gate_hidden_ready"], 1)
            for t in range(TILES):
                last = nc.tensor.matmul(bank(k, 2)[:, t * 60:(t + 1) * 60], hidden[:, t * P:(t + 1) * P],
                                        const(k, "wb2"), start=True, stop=True)
            last.then_inc(S["gate_down"], 1)

        @block.scalar
        def _(act):
            act.wait_ge(S["gate_up"], 1)
            nc.scalar.activation(hidden[:, :], banks(k, 0, 2), ACT.Silu).then_inc(S["gate_hidden_ready"], 1)
            act.wait_ge(S["gate_params_ready"], 1)
            for j in range(2):
                nc.scalar.activation(amp[:, j, :, :], params[:, :, 2 * j, :], ACT.Tanh, scale=0.5)
                last = nc.scalar.activation(phase[:, j, :, :], params[:, :, 2 * j + 1, :], ACT.Tanh)
            last.then_inc(S["gate_tanh"], 1)
            act.wait_ge(S["gate_difference"], 1)
            nc.scalar.activation(phase[:, 1, :, :], phase[:, 0, :, :], ACT.Sin, scale=math.pi / 2).then_inc(S["gate_sine"], 1)
            act.wait_ge(S["gate_angle"], 1)
            nc.scalar.activation(amp[:, 1, :, :], amp[:, 0, :, :], ACT.Tanh).then_inc(S["gate_inter"], 1)
            act.wait_ge(S["gate_scaled"], 1)
            nc.scalar.activation(amp[:, 1, :, :], amp[:, 0, :, :], ACT.Tanh, scale=0.5).then_inc(S["gate_last"], 1)

        @block.vector
        def _(dve):
            steps = [0]

            def then(ins):
                steps[0] += 1
                ins.then_inc(S["gate_step"], 1)
                dve.wait_ge(S["gate_step"], steps[0])

            then(nc.vector.tensor_scalar(temp[:, :], const(k, "temperature"), 0.1, 2.0, ALU.max, ALU.min))
            dve.wait_ge(S["gate_down"], 1)
            nc.vector.tensor_copy(params[:, :, :, :].rearrange("p t j h -> p (t j h)"),
                                  bank(k, 2)[:, 0:TILES * 60]).then_inc(S["gate_params_ready"], 1)
            dve.wait_ge(S["gate_tanh"], 1)
            then(nc.vector.tensor_scalar(amp[:, :, :, :], amp[:, :, :, :], 0.5, 0.5, ALU.mult, ALU.add))
            nc.vector.tensor_tensor(phase[:, 0, :, :], phase[:, 0, :, :], phase[:, 1, :, :],
                                    ALU.subtract).then_inc(S["gate_difference"], 1)
            then(nc.vector.tensor_tensor(amp[:, 0, :, :], amp[:, 0, :, :], amp[:, 1, :, :], ALU.mult))
            dve.wait_ge(S["gate_sine"], 1)
            then(nc.vector.tensor_tensor(phase[:, 0, :, :], phase[:, 1, :, :], phase[:, 1, :, :], ALU.mult))
            then(nc.vector.tensor_scalar(phase[:, 1, :, :], phase[:, 0, :, :], -2.0, 1.0, ALU.mult, ALU.add))
            nc.vector.tensor_tensor(amp[:, 0, :, :], amp[:, 0, :, :], phase[:, 1, :, :], ALU.mult).then_inc(S["gate_angle"], 1)
            dve.wait_ge(S["gate_inter"], 1)
            nc.vector.tensor_scalar(amp[:, 0, :, :], amp[:, 1, :, :], temp[:, :], None, ALU.mult).then_inc(S["gate_scaled"], 1)
            dve.wait_ge(S["gate_last"], 1)
            nc.vector.tensor_scalar(a.gate1[:, :, :], amp[:, 1, :, :], 0.5, 1.5, ALU.mult, ALU.add)


def route(nc, k, layer):
    S = k.S
    E = MOES[f"l{layer}"]["experts"]
    cap = MOES[f"l{layer}"]["cap"]
    top = 3 if layer == 1 else 2
    tag = f"route{layer}_"
    with ExitStack() as own:
        sb = lambda name, shape, dt=F32: own.enter_context(nc.sbuf_tensor(tag + name, shape, dt))
        logits = sb("logits", [P, TILES, E])
        probs = sb("probs", [P, TILES, E])
        best = sb("best", [P, TILES, 8])
        index = sb("index", [P, TILES, 8], U32)
        indexf = sb("indexf", [P, TILES, 8])
        hot = sb("hot", [P, top, TILES, E])
        weight = sb("weight", [P, top, TILES])
        small1 = sb("small1", [P, TILES])
        prefix = sb("prefix", [P, 2, TILES, E])
        counted = sb("counted", [P, 2, TILES, E])
        kept = sb("kept", [P, 2, TILES, E])
        block = own.enter_context(nc.Block())
        shape = [P, TILES, E]

        @block.tensor
        def _(pe):
            for t in range(TILES):
                for f in range(2):
                    last = nc.tensor.matmul(bank(k, 0)[:, t * E:(t + 1) * E], k.ht[0:KH + f, f, t * P:(t + 1) * P],
                                            small(k, f"gate{layer}")[0:KH + f, f, :], start=(f == 0), stop=(f == 1))
            last.then_inc(S["logits_done"], 1)
            if cap:
                width = 2 if layer == 0 else 1
                pe.wait_ge(S["prefix_ready"], S.at("prefix_ready") + 1)
                src = hot if layer == 0 else counted
                out = bank(k, 1)[:, 0:width * TILES * E]
                nc.tensor.matmul(out, const(k, "earlier"), src[:, 0:width, :, :].rearrange("p c t e -> p (c t e)"),
                                 start=True, stop=False)
                nc.tensor.matmul(out, const(k, "ones"), prefix[:, 0:width, :, :].rearrange("p c t e -> p (c t e)"),
                                 start=False, stop=True).then_inc(S["ranked"], 1)

        @block.scalar
        def _(act):
            if layer == 0:
                act.wait_ge(S["route_gap"], 1)
                nc.scalar.activation(weight[:, 1, :], small1[:, :], ACT.Exp).then_inc(S["route_exp"], 1)
            else:
                act.wait_ge(S["route_gap"], S.at("route_gap") + 1)
                nc.scalar.activation(probs[:, :, :], logits[:, :, :], ACT.Exp).then_inc(S["route_exp"], 1)

        @block.vector
        def _(dve):
            at = [S.at("route_step")]

            def then(ins):
                at[0] += 1
                ins.then_inc(S["route_step"], 1)
                dve.wait_ge(S["route_step"], at[0])

            dve.wait_ge(S["logits_done"], S.at("logits_done") + 1)
            then(nc.vector.tensor_copy(logits[:, :, :], bank(k, 0)[:, 0:TILES * E].rearrange("p (t e) -> p t e", e=E)))
            source = logits
            if layer > 0:
                if layer == 1:
                    then(nc.vector.memset(logits[:, :, 0:1], -1e9))
                then(nc.vector.tensor_reduce(small1[:, :], logits[:, :, :], AX.X, ALU.max))
                nc.vector.tensor_tensor(logits[:, :, :], logits[:, :, :], bcast(small1[:, :].unsqueeze(2), shape),
                                        ALU.subtract).then_inc(S["route_gap"], 1)
                dve.wait_ge(S["route_exp"], S.at("route_exp") + 1)
                then(nc.vector.tensor_reduce(small1[:, :], probs[:, :, :], AX.X, ALU.add))
                then(nc.vector.reciprocal(small1[:, :], small1[:, :]))
                then(nc.vector.tensor_tensor(probs[:, :, :], probs[:, :, :], bcast(small1[:, :].unsqueeze(2), shape), ALU.mult))
                source = probs
            for t in range(TILES):
                last = nc.vector.max(best[:, t, :], source[:, t, :])
            then(last)
            for t in range(TILES):
                last = nc.vector.max_index(index[:, t, :], best[:, t, :], source[:, t, :])
            then(last)
            then(nc.vector.tensor_copy(indexf[:, :, :], index[:, :, :]))
            for c in range(top):
                last = nc.vector.tensor_tensor(hot[:, c, :, :], bcast(const(k, "iota")[:, 0:E].unsqueeze(1), shape),
                                               bcast(indexf[:, :, c:c + 1], shape), ALU.is_equal)
            then(last)
            if layer == 0:
                nc.vector.tensor_tensor(small1[:, :], best[:, :, 1], best[:, :, 0], ALU.subtract).then_inc(S["route_gap"], 1)
                dve.wait_ge(S["route_exp"], 1)
                then(nc.vector.tensor_scalar_add(small1[:, :], weight[:, 1, :], 1.0))
                then(nc.vector.reciprocal(weight[:, 0, :], small1[:, :]))
                then(nc.vector.tensor_tensor(weight[:, 1, :], weight[:, 1, :], weight[:, 0, :], ALU.mult))
            elif layer == 1:
                for c in range(top):
                    last = nc.vector.tensor_copy(weight[:, c, :], best[:, :, c])
                then(last)
            else:
                then(nc.vector.tensor_tensor(small1[:, :], best[:, :, 0], best[:, :, 1], ALU.add))
                then(nc.vector.reciprocal(small1[:, :], small1[:, :]))
                for c in range(top):
                    last = nc.vector.tensor_tensor(weight[:, c, :], best[:, :, c], small1[:, :], ALU.mult)
                then(last)
            if cap:
                if layer == 0:
                    order = [(c, t) for c in range(2) for t in range(TILES)]
                    tokens = hot
                else:
                    then(nc.vector.tensor_tensor(counted[:, 0, :, :], hot[:, 0, :, :], hot[:, 1, :, :], ALU.add))
                    order = [(0, t) for t in range(TILES)]
                    tokens = counted
                last = nc.vector.memset(prefix[:, 0, 0, :], 0.0)
                for (c0, t0), (c1, t1) in zip(order, order[1:]):
                    then(last)
                    last = nc.vector.tensor_tensor(prefix[:, c1, t1, :], prefix[:, c0, t0, :], tokens[:, c0, t0, :], ALU.add)
                last.then_inc(S["prefix_ready"], 1)
                dve.wait_ge(S["ranked"], S.at("ranked") + 1)
                for c in range(2):
                    rank = bank(k, 1)[:, 0:2 * TILES * E].rearrange("p (c t e) -> p c t e", c=2, e=E)[:, c if layer == 0 else 0, :, :]
                    last = nc.vector.tensor_scalar(kept[:, c, :, :], rank, float(cap), None, ALU.is_lt)
                then(last)
                for c in range(2):
                    last = nc.vector.tensor_tensor(hot[:, c, :, :], hot[:, c, :, :], kept[:, c, :, :], ALU.mult)
                then(last)
            for c in range(top):
                last = nc.vector.tensor_tensor(hot[:, c, :, :], hot[:, c, :, :], bcast(weight[:, c, :].unsqueeze(2), shape), ALU.mult)
            then(last)
            dst = k.combine[:, :, 0:E]
            then(nc.vector.tensor_tensor(dst, hot[:, 0, :, :], hot[:, 1, :, :], ALU.add))
            if top == 3:
                then(nc.vector.tensor_tensor(dst, dst, hot[:, 2, :, :], ALU.add))
                then(nc.vector.tensor_scalar_add(k.combine[:, :, 0:1], k.combine[:, :, 0:1], 1.0))
            route.steps = at[0] - S.at("route_step")
    S.passed(logits_done=1, route_gap=1, route_exp=1, route_step=route.steps,
             **(dict(prefix_ready=1, ranked=1) if cap else {}))


def allocate_experts(nc, k, ctx):
    def sb(name, shape):
        return ctx.enter_context(nc.sbuf_tensor(name, shape, F32))

    k.combine = sb("combine", [P, TILES, 16])
    k.combine_t = sb("combine_t", [48, TILES, P])
    k.expert_rows = sb("expert_rows", [48, C])
    k.acc = sb("acc", [P, TILES, C])
    k.xrt = sb("xrt", [KH, 2, TOKENS])


def experts(nc, k, io, layer, x):
    S = k.S
    M = MOES[f"l{layer}"]
    E, UP, HID = M["experts"], M["up"], M["hid"]
    W2 = C + 1 if layer == 1 else C
    GROUP = 4
    RING = {0: 4, 1: 3, 2: 2}[layer]
    DOWN = 1 if layer == 1 else GROUP
    CREDIT = 2 * DOWN + 1
    tag = f"l{layer}_"
    name = lambda x: tag + x
    two = (0, 1)
    with ExitStack() as own:
        sb = lambda nm, shape: own.enter_context(nc.sbuf_tensor(tag + nm, shape, F32))
        w1 = [sb(f"w1_{s}", [KH, 2, UP * P]) for s in two]
        w2 = [sb(f"w2_{s}", [P, HID, C]) for s in two]
        side = [sb(f"side{s}", [P, 16]) for s in two]
        hid = [sb(f"hid{g}", [P, HID, BANK]) for g in two]
        if layer == 1:
            w2s = [sb(f"w2s{s}", [P, HID, W2]) for s in two]
            square = [sb(f"square{g}", [P, HID, BANK]) for g in two]
            mean, msq, vareps, rstd, weight = [sb(nm, [P, GROUP]) for nm in ("mean", "msq", "vareps", "rstd", "weight")]
            coef = sb("coef", [P, TILES, 48])
            fixed_t = sb("fixed_t", [KH, 2, 2, 16])
        if layer == 2:
            silu = [sb(f"silu{b}", [P, BANK]) for b in two]
            kept_sum = sb("kept_sum", [P, TILES])
        block = own.enter_context(nc.Block())
        halves = banks(k, 4, 4).rearrange("p (t c) -> p t c", t=TILES)[:, :, 0:C]

        def n(i, s, g, each=1, j=0, credit=0):
            return i * (4 * each) + ((2 * s + g) * each + j + 1 + credit)

        def e(i, s, more=1):
            return i * 2 + (s + more)

        @block.sync
        def _(sp):
            with sp.Fori(0, E // 2) as i:
                for s in two:
                    sp.wait_ge(S[name("down_done")], i * (4 * DOWN) + (2 * DOWN * s + 1))
                    at = bass.ds(e(i, s, 0), 1)
                    sp.dma_start(w1[s][:, :, :].rearrange("p f h -> p (f h)"),
                                 io[tag + "w1"][at, :, :].rearrange("a p x -> p (a x)")).then_inc(S[name(f"w{s}_loaded")], 16)
                    sp.dma_start(w2[s][:, :, :].rearrange("p f h -> p (f h)"),
                                 io[tag + "w2"][at, :, :].rearrange("a p x -> p (a x)")).then_inc(S[name(f"w{s}_loaded")], 16)
                    sp.dma_start(side[s][:, :],
                                 io[tag + "side"][at, :, :].rearrange("a p x -> p (a x)")).then_inc(S[name(f"w{s}_loaded")], 16)

        if layer == 1:
            @block.gpsimd
            def _(pool):
                nc.gpsimd.memset(w2s[0][:, :, C:C + 1], 1.0)
                nc.gpsimd.memset(w2s[1][:, :, C:C + 1], 1.0)
                with pool.Fori(0, E // 2) as i:
                    for s in two:
                        pool.wait_ge(S[name(f"w{s}_loaded")], i * 48 + 48)
                        pool.wait_ge(S[name("down_done")], i * (4 * DOWN) + (2 * DOWN * s + 1))
                        nc.gpsimd.tensor_tensor(w2s[s][:, :, 0:C], w2[s][:, :, :],
                                                bcast(side[s][:, 4:4 + HID].unsqueeze(2), [P, HID, C]),
                                                ALU.mult).then_inc(S[name("w2s_ready")], 1)
                        for g in two:
                            pool.wait_ge(S[name("vareps_ready")], n(i, s, g))
                            nc.gpsimd.tensor_tensor(rstd[:, :], vareps[:, :], k.minus_half[:, 0:GROUP],
                                                    ALU.pow).then_inc(S[name("rstd_ready")], 1)

        @block.tensor
        def _(pe):
            pe.sem_inc(S[name("down_done")], CREDIT)
            ident = const(k, "ident")
            if layer == 0:
                for t in range(TILES):
                    last = nc.tensor.transpose(banks(k, 0, 2)[0:8, t * P:(t + 1) * P], k.combine[:, t, 0:8], ident)
                last.then_inc(S[name("combine_turned")], 1)
                pe.wait_ge(S[name("rows_loaded")], 16)
                pe.wait_ge(S[name("combine_t_ready")], 1)
                for t in range(TILES):
                    last = nc.tensor.matmul(halves[:, t, :], k.combine_t[0:8, t, :], k.expert_rows[0:8, :],
                                            start=True, stop=True)
                last.then_inc(S[name("rows_added")], 1)
            with pe.Fori(0, E // 2) as i:
                for s in two:
                    pe.wait_ge(S[name(f"w{s}_loaded")], i * 48 + 48)
                    if layer == 1:
                        pe.wait_ge(S[name("fixed_read")], e(i, s))
                        for f in two:
                            for m in range(HID):
                                last = nc.tensor.matmul(bank(k, 3)[0:KH, 2 * f:2 * f + 2], w2[s][:, m, f * KH:(f + 1) * KH],
                                                        side[s][:, 4 + m:8 + m:3], start=(m == 0), stop=(m == HID - 1))
                        last.then_inc(S[name("fixed_done")], 1)
                    if layer == 2:
                        pe.wait_ge(S[name("w1_scaled")], e(i, s))
                    for g in two:
                        for m in range(UP):
                            if layer == 2:
                                if m % 2 == 0:
                                    pe.wait_ge(S[name("hid_ready")], n(i, s, g, HID, m // 2))
                                b = m % 4
                            else:
                                pe.wait_ge(S[name("hid_ready")], n(i, s, g, HID, m))
                                b = m if layer == 1 else (UP * g + m) % 4
                            for f in two:
                                last = nc.tensor.matmul(bank(k, b), w1[s][:, f, m * P:(m + 1) * P],
                                                        x[0:KH, f, g * BANK:(g + 1) * BANK], start=(f == 0), stop=(f == 1))
                            last.then_inc(S[name("up_done")], 1)
                        if layer == 1:
                            pe.wait_ge(S[name("w2s_ready")], e(i, s))
                        pe.wait_ge(S[name("hid_ready")], n(i, s, g, HID, HID - 1, RING))
                        for t in range(GROUP):
                            pe.wait_ge(S[name("acc_done")], n(i, s, g, GROUP, t))
                            for m in range(HID):
                                rhs = w2s[s][:, m, :] if layer == 1 else w2[s][:, m, :]
                                last = nc.tensor.matmul(bank(k, 4 + t)[:, 0:W2], hid[g][:, m, t * P:(t + 1) * P], rhs,
                                                        start=(m == 0), stop=(m == HID - 1))
                            if layer != 1:
                                last.then_inc(S[name("down_done")], 1)
                        if layer == 1:
                            pe.wait_ge(S[name("square_ready")], n(i, s, g))
                            for t in range(GROUP):
                                last = nc.tensor.matmul(bank(k, 4 + t)[:, 200:201], square[g][:, 0, t * P:(t + 1) * P],
                                                        const(k, "ones")[:, 0:1], start=True, stop=True)
                            last.then_inc(S[name("down_done")], 1)
            if layer == 1:
                pe.wait_ge(S[name("coef_ready")], 1)
                for f in two:
                    nc.tensor.transpose(bank(k, 0)[0:32, f * KH:(f + 1) * KH],
                                        fixed_t[:, f, :, :].rearrange("p j e -> p (j e)"), ident[0:KH, 0:KH])
                for t in range(TILES):
                    last = nc.tensor.transpose(banks(k, 1, 2)[0:48, t * P:(t + 1) * P], coef[:, t, :], ident)
                last.then_inc(S[name("combine_turned")], 1)
                pe.wait_ge(S[name("rows_loaded")], 16)
                pe.wait_ge(S[name("combine_t_ready")], 1)
                for t in range(TILES):
                    last = nc.tensor.matmul(halves[:, t, :], k.combine_t[0:48, t, :], k.expert_rows[0:48, :],
                                            start=True, stop=True)
                last.then_inc(S[name("rows_added")], 1)

        @block.scalar
        def _(act):
            if layer == 0:
                act.dma_start(k.expert_rows[0:8, :], io["l0_rows"]).then_inc(S[name("rows_loaded")], 16)
            if layer == 1:
                act.dma_start(k.expert_rows[32:48, :], io["l1_rows"]).then_inc(S[name("rows_loaded")], 16)
            if layer != 2:
                act.sem_inc(S[name("hid_ready")], RING)
            with act.Fori(0, E // 2) as i:
                for s in two:
                    act.wait_ge(S[name(f"w{s}_loaded")], i * 48 + 48)
                    if layer == 2:
                        for f in two:
                            last = nc.scalar.activation(w1[s][:, f, :], w1[s][:, f, :], ACT.Copy, scale=side[s][0:KH, f:f + 1])
                        last.then_inc(S[name("w1_scaled")], 1)
                    for g in two:
                        if layer == 2:
                            for j in range(HID):
                                act.wait_ge(S[name("up_done")], n(i, s, g, UP, 2 * j))
                                act.wait_ge(S[name("hid_ready")], n(i, s, g, HID, j))
                                nc.scalar.activation(silu[j % 2][:, :], bank(k, (2 * j) % 4), ACT.Silu).then_inc(S[name("silu_ready")], 1)
                        else:
                            act.wait_ge(S[name("down_done")], i * (4 * DOWN) + ((2 * s + g + 1) * DOWN + 1))
                            for m in range(UP):
                                b = m if layer == 1 else (UP * g + m) % 4
                                act.wait_ge(S[name("up_done")], n(i, s, g, UP, m))
                                nc.scalar.activation(hid[g][:, m, :], bank(k, b), ACT.Gelu,
                                                     bias=side[s][:, m:m + 1]).then_inc(S[name("hid_ready")], 1)

        @block.vector
        def _(dve):
            if layer == 0:
                dve.wait_ge(S[name("combine_turned")], 1)
                nc.vector.tensor_copy(k.combine_t[0:8, :, :].rearrange("p t c -> p (t c)"),
                                      banks(k, 0, 2)[0:8, :]).then_inc(S[name("combine_t_ready")], 1)
                dve.wait_ge(S[name("rows_added")], 1)
                nc.vector.tensor_copy(k.acc[:, :, :], halves).then_inc(S[name("acc_started")], 1)
            if layer == 1:
                nc.vector.memset(k.acc[:, :, :], 0.0).then_inc(S[name("acc_started")], 1)
                dve.sem_inc(S[name("fixed_read")], 1)
            if layer == 2:
                nc.vector.tensor_reduce(kept_sum[:, :], k.combine[:, :, 0:E], AX.X, ALU.add).then_inc(S[name("kept_summed")], 1)
                dve.wait_ge(S[name("kept_summed")], 1)
                nc.vector.tensor_tensor(k.acc[:, :, :], k.h[:, :, :], bcast(kept_sum[:, :].unsqueeze(2), [P, TILES, C]),
                                        ALU.mult).then_inc(S[name("acc_started")], 1)
                dve.sem_inc(S[name("hid_ready")], RING)
            dve.wait_ge(S[name("acc_started")], 1)
            dve.sem_inc(S[name("acc_done")], GROUP)
            with dve.Fori(0, E // 2) as i:
                for s in two:
                    expert = bass.ds(e(i, s, 0), 1)
                    if layer == 1:
                        dve.wait_ge(S[name("fixed_done")], e(i, s))
                        nc.vector.tensor_copy(fixed_t[:, :, :, expert].rearrange("p f j e -> p f (j e)"),
                                              bank(k, 3)[0:KH, 0:4].rearrange("p (f j) -> p f j", f=2)).then_inc(S[name("fixed_read")], 1)
                    for g in two:
                        if layer == 2:
                            dve.wait_ge(S[name("down_done")], i * (4 * DOWN) + ((2 * s + g + 1) * DOWN + 1))
                            for j in range(HID):
                                dve.wait_ge(S[name("silu_ready")], n(i, s, g, HID, j))
                                dve.wait_ge(S[name("up_done")], n(i, s, g, UP, 2 * j + 1))
                                nc.vector.tensor_tensor(hid[g][:, j, :], silu[j % 2][:, :], bank(k, (2 * j + 1) % 4),
                                                        ALU.mult).then_inc(S[name("hid_ready")], 1)
                        if layer == 1:
                            h, sq = hid[g], square[g]
                            step = lambda j: n(i, s, g, 5, j)
                            dve.wait_ge(S[name("hid_ready")], n(i, s, g, HID, HID - 1, RING))
                            nc.vector.tensor_tensor(sq[:, :, :], h[:, :, :], h[:, :, :], ALU.mult).then_inc(S[name("step")], 1)
                            dve.wait_ge(S[name("step")], step(0))
                            nc.vector.tensor_tensor(sq[:, 0, :], sq[:, 0, :], sq[:, 1, :], ALU.add).then_inc(S[name("step")], 1)
                            dve.wait_ge(S[name("step")], step(1))
                            nc.vector.tensor_tensor(sq[:, 0, :], sq[:, 0, :], sq[:, 2, :], ALU.add).then_inc(S[name("square_ready")], 1)
                            dve.wait_ge(S[name("down_done")], n(i, s, g, DOWN, 0, CREDIT))
                            column = lambda c: k.ps[:, 4:8, c:c + 1].rearrange("p t c -> p (t c)")
                            width = HID * P
                            nc.vector.tensor_scalar_mul(mean[:, :], column(C), 1.0 / width).then_inc(S[name("step")], 1)
                            dve.wait_ge(S[name("step")], step(2))
                            nc.vector.tensor_tensor(msq[:, :], mean[:, :], mean[:, :], ALU.mult).then_inc(S[name("step")], 1)
                            dve.wait_ge(S[name("step")], step(3))
                            nc.vector.scalar_tensor_tensor(out=msq[:, :], in0=column(200), scalar=1.0 / width, in1=msq[:, :],
                                                           op0=ALU.mult, op1=ALU.subtract).then_inc(S[name("step")], 1)
                            dve.wait_ge(S[name("step")], step(4))
                            nc.vector.tensor_scalar_add(vareps[:, :], msq[:, :], LN_EPS).then_inc(S[name("vareps_ready")], 1)
                            dve.wait_ge(S[name("rstd_ready")], n(i, s, g))
                            cw = k.combine[:, 4 * g:4 * g + 4, expert].rearrange("p t e -> p (t e)")
                            nc.vector.tensor_tensor(weight[:, :], rstd[:, :], cw, ALU.mult).then_inc(S[name("weight_ready")], 1)
                            dve.wait_ge(S[name("weight_ready")], n(i, s, g))
                            nc.vector.scalar_tensor_tensor(out=coef[:, 4 * g:4 * g + 4, expert].rearrange("p t e -> p (t e)"),
                                                           in0=weight[:, :], scalar=-1.0, in1=mean[:, :], op0=ALU.mult, op1=ALU.mult)
                        for t in range(GROUP):
                            if layer != 1:
                                dve.wait_ge(S[name("down_done")], n(i, s, g, DOWN, t, CREDIT))
                            acc = k.acc[:, 4 * g + t, :]
                            by = weight[:, t:t + 1] if layer == 1 else k.combine[:, 4 * g + t, expert]
                            nc.vector.scalar_tensor_tensor(out=acc, in0=bank(k, 4 + t)[:, 0:C], scalar=by, in1=acc,
                                                           op0=ALU.mult, op1=ALU.add).then_inc(S[name("acc_done")], 1)
            if layer == 1:
                nc.vector.tensor_copy(coef[:, :, 16:32], k.combine[:, :, :])
                nc.vector.tensor_copy(coef[:, :, 32:48], k.combine[:, :, :]).then_inc(S[name("coef_ready")], 1)
                dve.wait_ge(S[name("combine_turned")], 1)
                nc.vector.tensor_copy(k.expert_rows[0:32, :], bank(k, 0)[0:32, 0:C])
                nc.vector.tensor_copy(k.combine_t[:, :, :].rearrange("p t c -> p (t c)"),
                                      banks(k, 1, 2)[0:48, :]).then_inc(S[name("combine_t_ready")], 1)
                dve.wait_ge(S[name("rows_added")], 1)
                nc.vector.tensor_tensor(k.acc[:, :, :], k.acc[:, :, :], halves, ALU.add)


def close(nc, k, layer, with_x1=False):
    S = k.S
    with ExitStack() as own:
        stats = own.enter_context(nc.sbuf_tensor(f"close{layer}_stats", [P, TILES, 6], F32))
        meanvar = own.enter_context(nc.sbuf_tensor(f"close{layer}_meanvar", [P, TILES, 2], F32))
        rstd = own.enter_context(nc.sbuf_tensor(f"close{layer}_rstd", [P, TILES], F32))
        vareps = own.enter_context(nc.sbuf_tensor(f"close{layer}_vareps", [P, TILES], F32))
        block = own.enter_context(nc.Block())

        @block.gpsimd
        def _(pool):
            pool.wait_ge(S["close_vareps"], S.at("close_vareps") + 1)
            nc.gpsimd.tensor_tensor(rstd[:, :], vareps[:, :], k.minus_half[:, 0:TILES], ALU.pow).then_inc(S["close_rstd"], 1)

        @block.vector
        def _(dve):
            at = [S.at("close_step")]

            def then(ins):
                at[0] += 1
                ins.then_inc(S["close_step"], 1)
                dve.wait_ge(S["close_step"], at[0])

            if with_x1:
                then(nc.vector.tensor_tensor(k.acc[:, :, :], k.acc[:, :, :], k.x1[:, :, :], ALU.add))
            then(nc.vector.tensor_tensor(k.acc[:, :, :], k.acc[:, :, :], k.h[:, :, :], ALU.add))
            for t in range(TILES):
                last = nc.vector.bn_stats(stats[:, t, :], k.acc[:, t, :])
            then(last)
            for t in range(TILES):
                last = nc.vector.bn_aggr(meanvar[:, t, :], stats[:, t, :])
            then(last)
            nc.vector.tensor_scalar_add(vareps[:, :], meanvar[:, :, 1], LN_EPS).then_inc(S["close_vareps"], 1)
            dve.wait_ge(S["close_rstd"], S.at("close_rstd") + 1)
            for t in range(TILES):
                nc.vector.tensor_scalar(k.h[:, t, :], k.acc[:, t, :], meanvar[:, t, 0:1], rstd[:, t:t + 1],
                                        ALU.subtract, ALU.mult)
            close.steps = at[0] - S.at("close_step")
    S.passed(close_vareps=1, close_rstd=1, close_step=close.steps)


def quantised(nc, k, io):
    S = k.S
    two = (0, 1)
    with ExitStack() as own:
        w_int = own.enter_context(nc.sbuf_tensor("w_int", [KH, 2, C], I32))
        wb = own.enter_context(nc.sbuf_tensor("wb", [KH, 2, C], BF16))
        xq = [own.enter_context(nc.sbuf_tensor(f"xq{u}", [KH, 2, P], BF16)) for u in two]
        block = own.enter_context(nc.Block())

        def n(name, i, u, each=1, j=0):
            return i * (2 * each) + (S.at(name) + u * each + j + 1)

        @block.sync
        def _(sp):
            sp.dma_start(w_int[:, :, :], io["l3_w"]).then_inc(S["w_int_loaded"], 16)
            out = io["out"].rearrange("(t p) c -> t p c", p=P)
            with sp.Fori(0, TILES // 2) as i:
                for u in two:
                    sp.wait_ge(S["result_ready"], n("result_ready", i, u))
                    sp.dma_start(out[bass.ds(i * 2 + u, 1), :, :].rearrange("a p c -> p (a c)"),
                                 k.acc[:, bass.ds(i * 2 + u, 1), :].rearrange("p a c -> p (a c)")).then_inc(S["stored"], 16)
            sp.wait_ge(S["stored"], 16 * TILES)

        @block.gpsimd
        def _(pool):
            with pool.Fori(0, TILES // 2) as i:
                ln_power(nc, k, pool, i, "out_")

        @block.tensor
        def _(pe):
            with pe.Fori(0, TILES // 2) as i:
                for u in two:
                    pe.wait_ge(S["x_ready"], n("x_ready", i, u))
                    for f in two:
                        last = nc.tensor.transpose(bank(k, 4 * u)[0:KH, f * P:(f + 1) * P],
                                                   k.xs[u][:, f * KH:(f + 1) * KH], const(k, "ident"))
                    last.then_inc(S["x_turned"], 1)
                for u in two:
                    pe.wait_ge(S["xq_ready"], n("xq_ready", i, u))
                    for f in two:
                        last = nc.tensor.matmul(bank(k, 4 * u + 1)[:, 0:C], xq[u][:, f, :], wb[:, f, :], start=(f == 0), stop=(f == 1))
                    last.then_inc(S["projected"], 1)

        @block.scalar
        def _(act):
            act.wait_ge(S["w_int_loaded"], 16)
            nc.scalar.activation(wb[:, :, :], w_int[:, :, :], ACT.Copy)
            with act.Fori(0, TILES // 2) as i:
                for u in two:
                    act.wait_ge(S["x_turned"], n("x_turned", i, u))
                    nc.scalar.activation(xq[u][:, :, :].rearrange("p f t -> p (f t)"), bank(k, 4 * u)[0:KH, 0:2 * P],
                                         ACT.Copy).then_inc(S["xq_ready"], 1)

        @block.vector
        def _(dve):
            with dve.Fori(0, TILES // 2) as i:
                tile_of = lambda t, u: t[:, bass.ds(i * 2 + u, 1), :].rearrange("p a c -> p (a c)")
                for u in two:
                    nc.vector.tensor_scalar(k.xs[u][:, :], tile_of(k.h, u), float(1.0 / np.float32(0.02)), 127.0,
                                            ALU.mult, ALU.min).then_inc(S["scaled"], 1)
                for u in two:
                    dve.wait_ge(S["scaled"], n("scaled", i, u))
                    nc.vector.tensor_scalar(k.xs[u][:, :], k.xs[u][:, :], -128.0, ROUND, ALU.max, ALU.add).then_inc(S["rounded"], 1)
                for u in two:
                    dve.wait_ge(S["rounded"], n("rounded", i, u))
                    nc.vector.tensor_scalar_add(k.xs[u][:, :], k.xs[u][:, :], -ROUND).then_inc(S["x_ready"], 1)
                for u in two:
                    dve.wait_ge(S["projected"], n("projected", i, u))
                    nc.vector.scalar_tensor_tensor(out=k.ys[u][:, :], in0=bank(k, 4 * u + 1)[:, 0:C], scalar=float(np.float32(0.02 * 0.01)),
                                                   in1=const(k, "l3_bias"), op0=ALU.mult, op1=ALU.add).then_inc(S["masked"], 1)
                for u in two:
                    dve.wait_ge(S["masked"], n("masked", i, u))
                    nc.vector.tensor_tensor(k.ys[u][:, :], k.ys[u][:, :], tile_of(k.h, u), ALU.add).then_inc(S["y_ready"], 1)
                dve.wait_ge(S["y_ready"], n("y_ready", i, 1))
                ln_stats(nc, k, dve, [y[:, :] for y in k.ys], i, "out_")
                for u in two:
                    ln_apply(nc, k, dve, u, tile_of(k.acc, u), k.ys[u][:, :], i, "out_").then_inc(S["result_ready"], 1)


def program(nc, io, until=99, dump=None):
    with ExitStack() as ctx:
        k = allocate(nc, ctx)
        load_constants(nc, k, io)
        embed(nc, k, io)
        allocate_experts(nc, k, ctx)
        with ExitStack() as actx:
            steps = [
                lambda: (allocate_attention(nc, k, actx), clear_attention(nc, k)),
                lambda: attention(nc, k, io, 0, "segments"),
                lambda: attention(nc, k, io, 1, "softmax", pre_ln="ln1", keep=True),
                lambda: (turn(nc, k, k.x1, k.ht, "ln2"), route(nc, k, 0), experts(nc, k, io, 0, k.ht), close(nc, k, 0, with_x1=True)),
                lambda: attention(nc, k, io, 2, "softmax"),
                lambda: (turn(nc, k, k.h, k.ht), route(nc, k, 1), experts(nc, k, io, 1, k.ht), close(nc, k, 1)),
                lambda: (turn(nc, k, k.h, k.ht), gates(nc, k), attention(nc, k, io, 3, "linear", pre_ln="l2")),
                lambda: (turn(nc, k, k.h, k.ht), turn(nc, k, k.h, k.xrt, "rms"), route(nc, k, 2),
                         experts(nc, k, io, 2, k.xrt), close(nc, k, 2)),
                lambda: attention(nc, k, io, 4, "rotary"),
                lambda: quantised(nc, k, io),
            ]
            for n, step in enumerate(steps):
                if n <= until:
                    step()
                if dump is not None and n == until:
                    dump(nc, k)


def _constants(inp):
    f = np.float32
    c = np.zeros((P, CONST_WIDTH), f)

    def put(name, a):
        at, w = CONST_AT[name]
        c[:, at:at + w] = a

    p = np.arange(P)
    t = p % PATCHES
    key = np.arange(PATCHES)
    put("ident", np.eye(P, dtype=f))
    put("fold64", (t[:, None] == key[None, :]).astype(f))
    put("fold128", (t[:, None] == t[None, :]).astype(f))
    put("earlier", (p[:, None] < p[None, :]).astype(f))
    put("ones", np.ones((P, P), f))
    causal = key[None, :] <= t[:, None]
    put("causal_add", np.where(causal, 0, MASKED).astype(f))
    put("causal01", causal.astype(f))
    put("tail01", (causal & (key[None, :] >= t[:, None] // SEG * SEG)).astype(f))
    ends = np.array([15, 31, 47, 63, 31, 63, 63, 0])
    put("seg_add", np.where(t[:, None] >= ends[None, :], 0, MASKED).astype(f))
    freqs = (f(1.0 / 1024.0) ** np.linspace(0, 1, HD // 4, dtype=f)).astype(f)
    theta = t[:, None].astype(f) * np.concatenate([freqs, np.zeros(HD // 4, f)])[None, :]
    put("cos", np.cos(theta).astype(f))
    put("sin", np.sin(theta).astype(f))
    put("nsin", -np.sin(theta).astype(f))
    put("iota", np.arange(16, dtype=f)[None, :])
    put("bv", inp["L0_attn_bv"][None, :])
    put("mn_w", inp["L2_attn_mn_w"][None, :])
    put("mn_b", inp["L2_attn_mn_b"][None, :])
    put("temperature", inp["L2_attn_temperature"][None, :])
    put("l3_bias", inp["L3_ffn_bias"][None, :])
    put("wb2", inp["L2_attn_Wb2"].reshape(128, HEADS, 5).transpose(0, 2, 1).reshape(128, 60))
    return c


def _halves(w, bias=None):
    out = np.zeros((KH + 1, 2, w.shape[1]), np.float32)
    out[0:KH] = w.reshape(2, KH, -1).transpose(1, 0, 2)
    if bias is not None:
        out[KH, 1] = bias
    return out


def _layouts(inp):
    f = np.float32
    x = inp["x"].reshape(IMAGES, 3, 8, 16, 8, 16).transpose(1, 3, 5, 0, 2, 4)
    a = {"patches_t": x.reshape(KT_PATCH, P, TOKENS)}
    a["w_embed"] = inp["L0_tok_W"].T.reshape(KT_PATCH, P, C).transpose(1, 0, 2)
    a["const"] = _constants(inp)
    small = np.zeros((KH + 1, 2, SMALL_WIDTH), f)
    for name, w, b in (("gate0", inp["L0_ffn_w_g"], None), ("gate1", inp["L1_ffn_gate_w"], inp["L1_ffn_gate_b"]),
                       ("gate2", inp["L2_ffn_gate_w"].T, None), ("wb1", inp["L2_attn_Wb1"], None)):
        at, width = SMALL_AT[name]
        small[:, :, at:at + width] = _halves(w, b)
    for name, v in (("ln1_w", "L0_ffn_ln1_w"), ("ln1_b", "L0_ffn_ln1_b"), ("ln2_w", "L0_ffn_ln2_w"),
                    ("ln2_b", "L0_ffn_ln2_b"), ("l2_w", "L2_attn_ln_w"), ("l2_b", "L2_attn_ln_b")):
        at, _ = SMALL_AT[name]
        small[0:KH, :, at] = inp[v].reshape(2, KH).T
    a["small"] = small
    cat = np.concatenate
    z3, z = np.zeros(3 * C, f), np.zeros(C, f)
    a["wattn"] = np.stack([
        _halves(cat([inp["L0_attn_Wqkv"].T, inp["L0_attn_Wproj"].T], 1), cat([z3, z])),
        _halves(cat([inp["L0_ffn_attn_qkv_w"], inp["L0_ffn_attn_proj_w"]], 1),
                cat([inp["L0_ffn_attn_qkv_b"], inp["L0_ffn_attn_proj_b"]])),
        _halves(cat([inp[f"L1_attn_W{c}"].T for c in "qkvo"], 1), cat([inp[f"L1_attn_b{c}"] for c in "qkvo"])),
        _halves(cat([inp["L2_attn_Wqkv"], inp["L2_attn_Wproj"]], 1), cat([inp["L2_attn_bqkv"], inp["L2_attn_bproj"]])),
        _halves(cat([inp["L3_attn_qkv_w"][c].T for c in range(3)] + [inp["L3_attn_c_proj_w"].T], 1), cat([z3, z])),
    ])
    bil = np.zeros((PAIRS, HD, PAIRS, 256), f)
    wv = inp["L0_attn_Wv"].reshape(HD, HD, HD).transpose(1, 0, 2).reshape(HD, 256)
    for h in range(PAIRS):
        bil[h, :, h, :] = wv
    a["bil_w"] = bil.reshape(KH, PAIRS, 256)

    def up(w):
        e, _, n = w.shape
        return w.reshape(e, 2, KH, n).transpose(0, 2, 1, 3).reshape(e, KH, 2 * n)

    def down(w):
        e, h, _ = w.shape
        return w.reshape(e, h // P, P, C).transpose(0, 2, 1, 3).reshape(e, P, -1)

    def side(e, *cols):
        out = np.zeros((e, P, 16), f)
        for at, v in cols:
            out[:, 0:v.shape[1], at:at + v.shape[2]] = v
        return out

    tiles = lambda v: v.reshape(v.shape[0], -1, P).transpose(0, 2, 1)
    a["l0_w1"], a["l0_w2"] = up(inp["L0_ffn_exp_fc_w"]), down(inp["L0_ffn_exp_proj_w"])
    a["l0_side"] = side(8, (0, tiles(inp["L0_ffn_exp_fc_b"][:, 0])))
    a["l0_rows"] = inp["L0_ffn_exp_proj_b"][:, 0]
    a["l1_w1"], a["l1_w2"] = up(inp["L1_ffn_fc1_w"]), down(inp["L1_ffn_fc2_w"])
    a["l1_side"] = side(16, (0, tiles(inp["L1_ffn_fc1_b"])), (4, tiles(inp["L1_ffn_ln_w"])), (7, tiles(inp["L1_ffn_ln_b"])))
    a["l1_rows"] = inp["L1_ffn_fc2_b"]
    w13 = inp["L2_ffn_w13"].transpose(0, 2, 1).reshape(8, C, 2, 4, P).transpose(0, 1, 3, 2, 4).reshape(8, C, 1024)
    a["l2_w1"], a["l2_w2"] = up(w13), down(inp["L2_ffn_w2"].transpose(0, 2, 1))
    a["l2_side"] = side(8, (0, inp["L2_ffn_norm_w"].reshape(8, 2, KH).transpose(0, 2, 1)))
    a["l3_w"] = inp["L3_ffn_weight_t"].reshape(2, KH, C).transpose(1, 0, 2)
    return {n: np.ascontiguousarray(v.astype(np.int32) if v.dtype.kind in "iu" else v) for n, v in a.items()}


def kernel(**inputs):
    import concourse.bacc as bacc
    from concourse.bass_utils import run_bass_kernel_spmd as run

    arrays = _layouts({n: np.asarray(v) for n, v in inputs.items()})
    nc = bacc.Bacc("TRN2", target_bir_lowering=False, num_devices=1)
    io = {n: nc.dram_tensor("in_" + n, v.shape, mybir.dt.from_np(v.dtype), kind="ExternalInput").ap()
          for n, v in arrays.items()}
    io["out"] = nc.dram_tensor("out", (TOKENS, C), F32, kind="ExternalOutput").ap()
    program(nc, io)
    r = run(nc, [{"in_" + n: v for n, v in arrays.items()}], core_ids=[0])
    return r.results[0]["out"].reshape(IMAGES, PATCHES, C)
```

```python
import math
from contextlib import ExitStack

import numpy as np
import concourse.bass as bass
from concourse import mybir

P = 128
IMAGES, PATCHES = 16, 64
TOKENS = IMAGES * PATCHES
TILES = TOKENS // P
C = 192
KH = C // 2
HEADS, HD = 12, 16
BLOCKS = 3
PAIRS = HEADS // 2
PATCH_IN = 768
KT_PATCH = PATCH_IN // P
BANK = 512
LN_EPS = 1e-5
MASKED = -1e30
ROUND = 1.5 * 2 ** 23
SEG = 16

F32 = mybir.dt.float32
BF16 = mybir.dt.bfloat16
I32 = mybir.dt.int32
U32 = mybir.dt.uint32
ALU = mybir.AluOpType
ACT = mybir.ActivationFunctionType
AX = mybir.AxisListType

CONST_COLS = [
    ("ident", 128), ("fold64", 64), ("fold128", 128), ("earlier", 128), ("ones", 128),
    ("causal_add", 64), ("causal01", 64), ("tail01", 64), ("seg_add", 8),
    ("cos", 8), ("sin", 8), ("nsin", 8), ("iota", 16), ("refused", 16),
    ("bv", 16), ("mn_w", 16), ("mn_b", 16), ("temperature", 1), ("l3_bias", C), ("wb2", 60),
]
CONST_AT = {}
_at = 0
for _n, _w in CONST_COLS:
    CONST_AT[_n] = (_at, _w)
    _at += _w
CONST_WIDTH = _at

SMALL_COLS = [("gate0", 8), ("gate1", 16), ("gate2", 8), ("wb1", 128),
              ("ln1_w", 1), ("ln1_b", 1), ("ln2_w", 1), ("ln2_b", 1), ("l2_w", 1), ("l2_b", 1)]
SMALL_AT = {}
_at = 0
for _n, _w in SMALL_COLS:
    SMALL_AT[_n] = (_at, _w)
    _at += _w
SMALL_WIDTH = _at

CAPACITY = TOKENS * 2 * 5 // (4 * 8)
SLOTS = 8 * CAPACITY
ROW_TILES = ((0, P), (P, P), (2 * P, CAPACITY - 2 * P))
MOES = {
    "l0": dict(experts=8, up=6, hid=6, cap=CAPACITY, weight="w_l0"),
    "l1": dict(experts=16, up=3, hid=3, cap=None, weight="w_l1"),
    "l2": dict(experts=8, up=8, hid=4, cap=CAPACITY, weight="w_l2"),
}


class Signals(dict):

    def __init__(self, nc, ctx):
        super().__init__()
        self.nc, self.ctx, self.start = nc, ctx, {}

    def __missing__(self, name):
        self[name] = self.ctx.enter_context(self.nc.semaphore(name))
        self.start[name] = 0
        return self[name]

    def at(self, name):
        self[name]
        return self.start[name]

    def passed(self, **counts):
        for name, n in counts.items():
            self.start[name] = self.at(name) + n


class Core:
    pass


def const(k, name):
    a, w = CONST_AT[name]
    return k.const[:, a:a + w]


def small(k, name):
    a, w = SMALL_AT[name]
    return k.small[:, :, a:a + w]


def bcast(ap, shape):
    return ap.to_broadcast(shape)


def allocate(nc, ctx):
    k = Core()
    k.nc = nc

    def sb(name, shape, dt=F32):
        return ctx.enter_context(nc.sbuf_tensor(name, shape, dt))

    k.S = Signals(nc, ctx)
    k.const = sb("const", [P, CONST_WIDTH])
    k.small = sb("small", [KH + 1, 2, SMALL_WIDTH])
    k.wattn = sb("wattn", [KH + 1, 2, 4 * C])
    k.h = sb("h", [P, TILES, C])
    k.x1 = sb("x1", [P, TILES, C])
    k.ht = sb("ht", [KH + 1, 2, TOKENS])
    k.xs = [sb(f"xs{u}", [P, C]) for u in (0, 1)]
    k.ys = [sb(f"ys{u}", [P, C]) for u in (0, 1)]
    k.ln = {}
    for tag in ("in_", "out_"):
        b = k.ln[tag] = Core()
        b.stats, b.meanvar = sb(tag + "stats", [P, 6]), sb(tag + "meanvar", [P, 2])
        b.vareps, b.rstd, b.pause = sb(tag + "vareps", [P, 1]), sb(tag + "rstd", [P, 1]), sb(tag + "pause", [P, 1])
    k.zeros = sb("zeros", [P, C])
    k.sent = nc.dram_tensor("sent_rows", (SLOTS + 2 * TOKENS, C), F32, kind="Internal").ap()
    k.returned = nc.dram_tensor("returned_rows", (SLOTS, C), F32, kind="Internal").ap()
    k.minus_half = sb("minus_half", [P, 2 * HEADS])
    k.ps = ctx.enter_context(nc.psum_tensor("ps", [P, 8, BANK], F32))
    return k


def bank(k, b):
    return k.ps[:, b, :]


def banks(k, b, n):
    return k.ps[:, b:b + n, :].rearrange("p b c -> p (b c)")


def load_constants(nc, k, io):
    S = k.S
    with nc.Block() as block:
        @block.sync
        def _(sp):
            sp.dma_start(k.const[:, :], io["const"]).then_inc(S["const_loaded"], 16)
            sp.dma_start(k.small[:, :, :], io["small"]).then_inc(S["const_loaded"], 16)
            sp.wait_ge(S["const_loaded"], 32)

        @block.gpsimd
        def _(pool):
            nc.gpsimd.memset(k.minus_half[:, :], -0.5)
            nc.gpsimd.memset(k.zeros[:, :], 0.0)

        @block.vector
        def _(dve):
            nc.vector.memset(k.ht[KH:KH + 1, :, :], 1.0)


def embed(nc, k, io):
    S = k.S
    with ExitStack() as own:
        xt = own.enter_context(nc.sbuf_tensor("patches_t", [P, KT_PATCH, TOKENS], F32))
        w = own.enter_context(nc.sbuf_tensor("w_embed", [P, KT_PATCH, C], F32))
        block = own.enter_context(nc.Block())

        @block.sync
        def _(sp):
            sp.dma_start(w[:, :, :], io["w_embed"]).then_inc(S["w_embed_loaded"], 16)
            for kt in range(0, KT_PATCH, 2):
                sp.dma_start(xt[:, kt, :], io["patches_t"][kt]).then_inc(S[f"patches_loaded{kt}"], 16)

        @block.scalar
        def _(act):
            for kt in range(1, KT_PATCH, 2):
                act.dma_start(xt[:, kt, :], io["patches_t"][kt]).then_inc(S[f"patches_loaded{kt}"], 16)

        @block.tensor
        def _(pe):
            pe.wait_ge(S["w_embed_loaded"], 16)
            for kt in range(KT_PATCH):
                pe.wait_ge(S[f"patches_loaded{kt}"], 16)
                for t in range(TILES):
                    last = nc.tensor.matmul(bank(k, t)[:, 0:C], xt[:, kt, t * P:(t + 1) * P], w[:, kt, :],
                                            start=(kt == 0), stop=(kt == KT_PATCH - 1))
            last.then_inc(S["embedded"], 1)

        @block.vector
        def _(dve):
            dve.wait_ge(S["embedded"], 1)
            nc.vector.tensor_copy(k.h[:, :, :], k.ps[:, :, 0:C])


def ln_stats(nc, k, dve, row, tile, tag, eps=LN_EPS):
    S, b = k.S, k.ln[tag]
    nc.vector.bn_stats(b.stats[:, :], row).then_inc(S[tag + "stats_ready"], 1)
    dve.wait_ge(S[tag + "stats_ready"], tile + (S.at(tag + "stats_ready") + 1))
    nc.vector.memset(b.pause[:, :], 0.0)
    nc.vector.bn_aggr(b.meanvar[:, :], b.stats[:, :]).then_inc(S[tag + "meanvar_ready"], 1)
    dve.wait_ge(S[tag + "meanvar_ready"], tile + (S.at(tag + "meanvar_ready") + 1))
    nc.vector.tensor_scalar_add(b.vareps[:, :], b.meanvar[:, 1:2], eps).then_inc(S[tag + "vareps_ready"], 1)


def ln_power(nc, k, pool, tile, tag):
    S, b = k.S, k.ln[tag]
    pool.wait_ge(S[tag + "vareps_ready"], tile + (S.at(tag + "vareps_ready") + 1))
    nc.gpsimd.tensor_tensor(b.rstd[:, :], b.vareps[:, :], k.minus_half[:, 0:1], ALU.pow).then_inc(S[tag + "rstd_ready"], 1)


def ln_apply(nc, k, dve, dst, src, tile, tag):
    S, b = k.S, k.ln[tag]
    dve.wait_ge(S[tag + "rstd_ready"], tile + (S.at(tag + "rstd_ready") + 1))
    return nc.vector.tensor_scalar(dst, src, b.meanvar[:, 0:1], b.rstd[:, :], ALU.subtract, ALU.mult)


LN_SIGNALS = ("stats_ready", "meanvar_ready", "vareps_ready", "rstd_ready")


def tile_of(t, tile):
    return t[:, bass.ds(tile, 1), :].rearrange("p a c -> p (a c)")


def allocate_attention(nc, k, ctx):
    def two(name, shape):
        return [ctx.enter_context(nc.sbuf_tensor(f"{name}{u}", shape, F32)) for u in (0, 1)]

    a = Core()
    a.xt = two("xt", [KH + 1, 2, P])
    a.qkv = two("qkv", [P, 3, C])
    a.wide = two("wide", [P, 3, HEADS, 2, HD])
    a.qt = two("qt", [P, BLOCKS, P])
    a.kt = two("kt", [P, BLOCKS, 4, PATCHES])
    a.vd = two("vd", [P, PAIRS, 2, 2, HD])
    a.sc = two("sc", [P, HEADS, PATCHES])
    a.pr = two("pr", [P, HEADS, PATCHES])
    a.prt = two("prt", [P, PAIRS, P])
    a.max = two("smax", [P, HEADS])
    a.sum = two("ssum", [P, HEADS])
    a.rsum = two("rsum", [P, HEADS])
    a.seg = two("seg", [P, HEADS, 8])
    a.segp = two("segp", [P, HEADS, 8])
    a.os = two("os", [P, HEADS, HD])
    a.ot = two("ot", [KH + 1, 2, P])
    a.t24 = two("t24", [P, 2 * HEADS])
    a.r24 = two("r24", [P, 2 * HEADS])
    a.tmp = two("tmp", [P, 2, HEADS, HD])
    a.tmp2 = two("tmp2", [P, 2, HEADS, HD])
    a.hs = two("hs", [P, HEADS])
    a.hsq = two("hsq", [P, HEADS, HD])
    a.gate1 = ctx.enter_context(nc.sbuf_tensor("gate1", [P, TILES, HEADS], F32))
    k.a = a


def clear_attention(nc, k):
    a, S = k.a, k.S
    with nc.Block() as block:
        @block.sync
        def _(sp):
            rows = SLOTS // P
            sp.dma_start(k.sent[0:SLOTS, :].rearrange("(p r) c -> p r c", r=rows),
                         bcast(k.zeros[:, :].unsqueeze(1), [P, rows, C])).then_inc(S["slots_cleared"], 16)

        @block.gpsimd
        def _(pool):
            for u in (0, 1):
                nc.gpsimd.memset(a.wide[u][:, :, :, :, :], 0.0)

        @block.vector
        def _(dve):
            for u in (0, 1):
                nc.vector.memset(a.kt[u][:, :, :, :], 0.0)
                nc.vector.memset(a.vd[u][:, :, :, :, :], 0.0)
                nc.vector.memset(a.xt[u][KH:KH + 1, :, :], 1.0)
                nc.vector.memset(a.ot[u][KH:KH + 1, :, :], 1.0)


def in_slots(eng, slot):
    slot(0, 0, True, False, False)
    slot(1, 1, True, True, False)
    with eng.Fori(0, TILES // 2 - 1) as i:
        slot(i * 2 + 2, 0, True, True, True)
        slot(i * 2 + 3, 1, True, True, True)
    slot(TILES, 0, False, True, True)
    slot(TILES + 1, 1, False, False, True)


def attention(nc, k, io, layer, kind, pre_ln=None, keep=False):
    S, a = k.S, k.a
    scale = {"softmax": HD ** -0.5, "segments": HD ** -0.5, "rotary": 0.12, "linear": 1.0}[kind]
    raw = kind == "softmax"
    two = (0, 1)
    score_read = "p_ready" if kind == "linear" else "masked"
    weights_ready = "p_ready" if kind in ("linear", "segments") else "exped"
    scores = banks(k, 3, 2)[:, 0:HEADS * PATCHES]
    turned_p = banks(k, 5, 2)[:, 0:PAIRS * P]

    with ExitStack() as own:
        if kind == "segments":
            bil_w = own.enter_context(nc.sbuf_tensor("bil_w", [KH, PAIRS, 256], F32))
            kft = [own.enter_context(nc.sbuf_tensor(f"kft{u}", [KH, 2, P], F32)) for u in two]
            prod = [own.enter_context(nc.sbuf_tensor(f"prod{u}", [P, HEADS, HD, HD], F32)) for u in two]
        block = own.enter_context(nc.Block())

        def n(name, tile, each=1, more=0):
            return tile * each + (S.at(name) + more + 1)

        @block.sync
        def _(sp):
            sp.dma_start(k.wattn[:, :, :], io["wattn"][layer]).then_inc(S["wattn_loaded"], 16)
            if kind == "segments":
                sp.dma_start(bil_w[:, :, :], io["bil_w"]).then_inc(S["bil_w_loaded"], 16)

        @block.tensor
        def _(pe):
            pe.wait_ge(S["wattn_loaded"], S.at("wattn_loaded") + 16)
            if kind == "segments":
                pe.wait_ge(S["bil_w_loaded"], 16)
            ident = const(k, "ident")

            def slot(s, u, in_a, in_b, in_c):
                if in_b:
                    tile, v = s - 1, 1 - u
                    pe.wait_ge(S["qk_ready"], n("qk_ready", tile))
                    if not (isinstance(tile, int) and tile == 0):
                        pe.wait_ge(S[score_read], n(score_read, tile - 1))
                    for m in range(BLOCKS):
                        last = nc.tensor.matmul(scores[:, m * 256:(m + 1) * 256], a.qt[v][:, m, :],
                                                a.kt[v][:, m, :, :].rearrange("p h t -> p (h t)"),
                                                start=True, stop=True)
                    last.then_inc(S["scored"], 1)
                if in_a:
                    pe.wait_ge(S["x_ready"], n("x_ready", s))
                    for f in two:
                        last = nc.tensor.transpose(bank(k, 0)[0:KH, f * P:(f + 1) * P],
                                                   k.xs[u][:, f * KH:(f + 1) * KH], ident)
                    last.then_inc(S["x_turned"], 1)
                if in_c:
                    tile = s - 2
                    pe.wait_ge(S[weights_ready], n(weights_ready, tile))
                    if not (isinstance(tile, int) and tile == 0):
                        pe.wait_ge(S["y_ready"], n("y_ready", tile - 1))
                    for p in range(PAIRS):
                        last = nc.tensor.transpose(turned_p[:, p * P:(p + 1) * P],
                                                   a.pr[u][:, 2 * p:2 * p + 2, :].rearrange("p h t -> p (h t)"), ident)
                    last.then_inc(S["p_turned"], 1)
                if in_a:
                    pe.wait_ge(S["xt_ready"], n("xt_ready", s))
                    if not (isinstance(s, int) and s == 0):
                        pe.wait_ge(S["vd_ready"], n("vd_ready", s - 1))
                    for c in range(3):
                        for f in two:
                            out = banks(k, 1, 2)[:, c * 256:c * 256 + C]
                            last = nc.tensor.matmul(out, a.xt[u][0:KH + f, f, :],
                                                    k.wattn[0:KH + f, f, c * C:(c + 1) * C],
                                                    start=(f == 0), stop=(f == 1))
                    last.then_inc(S["qkv_projected"], 1)
                if in_c:
                    pe.wait_ge(S["prt_ready"], n("prt_ready", s - 2))
                    for p in range(PAIRS):
                        last = nc.tensor.matmul(bank(k, 7)[:, p * 64:(p + 1) * 64], a.prt[u][:, p, :],
                                                a.vd[u][:, p, :, :, :].rearrange("p a b d -> p (a b d)"),
                                                start=True, stop=True)
                    last.then_inc(S["mixed"], 1)
                if in_a and kind == "segments":
                    pe.wait_ge(S["qkv_ready"], n("qkv_ready", s))
                    for f in two:
                        last = nc.tensor.transpose(bank(k, 0)[0:KH, f * P:(f + 1) * P],
                                                   a.qkv[u][:, 1, f * KH:(f + 1) * KH], ident)
                    last.then_inc(S["k_turned"], 1)
                    pe.wait_ge(S["kft_ready"], n("kft_ready", s))
                    for c in range(6):
                        if c >= 3:
                            pe.wait_ge(S["bil_used"], n("bil_used", s, 6, c - 3))
                        nc.tensor.matmul(bank(k, c % 3), kft[u][:, c // 3, :],
                                         bil_w[:, 2 * (c % 3):2 * (c % 3) + 2, :].rearrange("p a b -> p (a b)"),
                                         start=True, stop=True).then_inc(S["bil_ready"], 1)
                if in_c:
                    pe.wait_ge(S["os_ready"], n("os_ready", s - 2))
                    os = a.os[u][:, :, :].rearrange("p h d -> p (h d)")
                    for f in two:
                        last = nc.tensor.transpose(bank(k, 5)[0:KH, f * P:(f + 1) * P],
                                                   os[:, f * KH:(f + 1) * KH], ident)
                    last.then_inc(S["o_turned"], 1)
                if in_a:
                    pe.wait_ge(S["wide_ready"], n("wide_ready", s))
                    wide = a.wide[u][:, :, :, :, :].rearrange("p c h b d -> p c (h b d)")
                    for m in range(BLOCKS):
                        nc.tensor.transpose(bank(k, 0)[:, m * P:(m + 1) * P],
                                            wide[:, 0, m * P:(m + 1) * P], ident)
                    for m in range(BLOCKS):
                        nc.tensor.matmul(bank(k, 1)[:, m * PATCHES:(m + 1) * PATCHES],
                                         wide[:, 1, m * P:(m + 1) * P], const(k, "fold64"),
                                         start=True, stop=True)
                    nc.tensor.matmul(bank(k, 2)[:, 0:2 * C], const(k, "fold128"), wide[:, 2, :],
                                     start=True, stop=True).then_inc(S["folded"], 1)
                if in_c:
                    pe.wait_ge(S["ot_ready"], n("ot_ready", s - 2))
                    for f in two:
                        last = nc.tensor.matmul(bank(k, 5)[:, 256:256 + C], a.ot[u][0:KH + f, f, :],
                                                k.wattn[0:KH + f, f, 3 * C:4 * C], start=(f == 0), stop=(f == 1))
                    last.then_inc(S["projected"], 1)

            in_slots(pe, slot)

        @block.scalar
        def _(act):
            def slot(s, u, in_a, in_b, in_c):
                if in_a:
                    act.wait_ge(S["x_turned"], n("x_turned", s))
                    if pre_ln:
                        for f in two:
                            last = nc.scalar.activation(a.xt[u][0:KH, f, :], bank(k, 0)[0:KH, f * P:(f + 1) * P],
                                                        ACT.Identity, scale=small(k, pre_ln + "_w")[0:KH, f, :],
                                                        bias=small(k, pre_ln + "_b")[0:KH, f, :])
                    else:
                        last = nc.scalar.activation(a.xt[u][0:KH, :, :].rearrange("p f t -> p (f t)"),
                                                    bank(k, 0)[0:KH, 0:2 * P], ACT.Copy)
                    last.then_inc(S["xt_ready"], 1)
                if in_c:
                    act.wait_ge(S["p_turned"], n("p_turned", s - 2))
                    nc.scalar.activation(a.prt[u][:, :, :].rearrange("p a t -> p (a t)"), turned_p,
                                         ACT.Copy).then_inc(S["prt_ready"], 1)
                if in_a:
                    act.wait_ge(S["qkv_projected"], n("qkv_projected", s))
                    src = k.ps[:, 1:3, :].rearrange("p b (c x) -> p (b c) x", c=2)
                    if raw:
                        for b in two:
                            r = slice(64 * b, 64 * b + 64)
                            last = nc.scalar.activation(a.wide[u][r, :, :, b, :],
                                                        src[r, 0:3, 0:C].rearrange("p c (h d) -> p c h d", d=HD), ACT.Copy)
                        last.then_inc(S["wide_ready"], 1)
                    else:
                        nc.scalar.activation(a.qkv[u][:, :, :], src[:, 0:3, 0:C], ACT.Copy).then_inc(S["qkv_ready"], 1)
                    if kind == "segments":
                        act.wait_ge(S["k_turned"], n("k_turned", s))
                        nc.scalar.activation(kft[u][:, :, :].rearrange("p f t -> p (f t)"), bank(k, 0)[0:KH, 0:2 * P],
                                             ACT.Copy).then_inc(S["kft_ready"], 1)
                    if kind == "linear":
                        act.wait_ge(S["clipped"], n("clipped", s))
                        nc.scalar.activation(a.tmp2[u][:, :, :, :], a.tmp[u][:, :, :, :], ACT.Exp).then_inc(S["elu_exp"], 1)
                if in_b and kind != "linear":
                    act.wait_ge(S["centred"], n("centred", s - 1))
                    src, dst = (a.seg, a.segp) if kind == "segments" else (a.sc, a.pr)
                    nc.scalar.activation(dst[1 - u][:, :, :], src[1 - u][:, :, :], ACT.Exp, scale=scale).then_inc(S["exped"], 1)
                if in_c:
                    act.wait_ge(S["o_turned"], n("o_turned", s - 2))
                    nc.scalar.activation(a.ot[u][0:KH, :, :].rearrange("p f t -> p (f t)"), bank(k, 5)[0:KH, 0:2 * P],
                                         ACT.Copy).then_inc(S["ot_ready"], 1)
                if in_a:
                    act.wait_ge(S["folded"], n("folded", s))
                    nc.scalar.activation(a.qt[u][:, :, :].rearrange("p m t -> p (m t)"), bank(k, 0)[:, 0:3 * P], ACT.Copy)
                    for j in range(4):
                        r = slice(32 * j, 32 * j + 32)
                        last = nc.scalar.activation(a.kt[u][r, :, j, :],
                                                    bank(k, 1)[r, 0:BLOCKS * PATCHES].rearrange("p (m t) -> p m t", m=BLOCKS),
                                                    ACT.Copy)
                    last.then_inc(S["qk_ready"], 1)

            in_slots(act, slot)

        @block.gpsimd
        def _(pool):
            def slot(s, u, in_a, in_b, in_c):
                if in_a and pre_ln:
                    ln_power(nc, k, pool, s, "in_")
                if in_a and kind == "rotary":
                    pool.wait_ge(S["ms_ready"], n("ms_ready", s))
                    nc.gpsimd.tensor_tensor(a.r24[u][:, :], a.t24[u][:, :], k.minus_half[:, :], ALU.pow).then_inc(S["rms_ready"], 1)
                if in_b and kind != "linear":
                    pool.wait_ge(S["max_ready"], n("max_ready", s - 1))
                    t, w = (a.seg, 8) if kind == "segments" else (a.sc, PATCHES)
                    nc.gpsimd.tensor_tensor(t[1 - u][:, :, :], t[1 - u][:, :, :],
                                            bcast(a.max[1 - u][:, :].unsqueeze(2), [P, HEADS, w]),
                                            ALU.subtract).then_inc(S["centred"], 1)
                if in_c and kind == "linear":
                    pool.wait_ge(S["hvar_ready"], n("hvar_ready", s - 2))
                    nc.gpsimd.tensor_tensor(a.r24[u][:, 0:HEADS], a.t24[u][:, 0:HEADS], k.minus_half[:, 0:HEADS],
                                            ALU.pow).then_inc(S["hrstd_ready"], 1)
                if in_c and not keep:
                    ln_power(nc, k, pool, s - 2, "out_")

            if pre_ln or kind != "linear" or not keep:
                in_slots(pool, slot)

        @block.vector
        def _(dve):
            every = [P, HEADS, PATCHES]
            heads = [P, HEADS, HD]
            score = scores.rearrange("p (h t) -> p h t", t=PATCHES)

            def input_rows(s, u):
                if pre_ln:
                    ln_stats(nc, k, dve, tile_of(k.h, s), s, "in_")
                    ln_apply(nc, k, dve, k.xs[u][:, :], tile_of(k.h, s), s, "in_").then_inc(S["x_ready"], 1)
                else:
                    nc.vector.tensor_copy(k.xs[u][:, :], tile_of(k.h, s)).then_inc(S["x_ready"], 1)

            def bilinear_values(s, u):
                dve.wait_ge(S["qkv_ready"], n("qkv_ready", s))
                for c in range(6):
                    dve.wait_ge(S["bil_ready"], n("bil_ready", s, 6, c))
                    v0 = a.qkv[u][:, 2, 32 * c:32 * c + 32].rearrange("p (h d) -> p h d", h=2)
                    nc.vector.tensor_tensor(
                        prod[u][:, 2 * c:2 * c + 2, :, :], bank(k, c % 3).rearrange("p (h e j) -> p h e j", h=2, e=HD),
                        bcast(v0.unsqueeze(2), [P, 2, HD, HD]), ALU.mult).then_inc(S["bil_used"], 1)
                dve.wait_ge(S["bil_used"], n("bil_used", s, 6, 5))
                nc.vector.tensor_reduce(a.tmp[u][:, 0, :, :].rearrange("p h e -> p (h e)"),
                                        prod[u][:, :, :, :].rearrange("p h e j -> p (h e) j"),
                                        AX.X, ALU.add).then_inc(S["v_summed"], 1)
                dve.wait_ge(S["v_summed"], n("v_summed", s))
                for b in two:
                    r = slice(64 * b, 64 * b + 64)
                    nc.vector.tensor_tensor(a.wide[u][r, 2, :, b, :], a.tmp[u][r, 0, :, :],
                                            bcast(const(k, "bv")[r, :].unsqueeze(1), [64, HEADS, HD]), ALU.add)
                    last = nc.vector.tensor_copy(a.wide[u][r, 0:2, :, b, :],
                                                 a.qkv[u][r, 0:2, :].rearrange("p c (h d) -> p c h d", d=HD))
                last.then_inc(S["wide_ready"], 1)

            def positive_keys(s, u):
                dve.wait_ge(S["qkv_ready"], n("qkv_ready", s))
                nc.vector.tensor_scalar_min(a.tmp[u][:, :, :, :].rearrange("p c h d -> p (c h d)"),
                                            a.qkv[u][:, 0:2, :].rearrange("p c x -> p (c x)"), 0.0).then_inc(S["clipped"], 1)
                g = tile_of(a.gate1, s)
                for b in two:
                    r = slice(64 * b, 64 * b + 64)
                    nc.vector.tensor_tensor(a.wide[u][r, 2, :, b, :], a.qkv[u][r, 2, :].rearrange("p (h d) -> p h d", d=HD),
                                            bcast(g[r, :].unsqueeze(2), [64, HEADS, HD]), ALU.mult)
                dve.wait_ge(S["elu_exp"], n("elu_exp", s))
                for b in two:
                    r = slice(64 * b, 64 * b + 64)
                    for c in two:
                        last = nc.vector.scalar_tensor_tensor(
                            out=a.wide[u][r, c, :, b, :], in0=a.qkv[u][r, c, :].rearrange("p (h d) -> p h d", d=HD),
                            scalar=0.0, in1=a.tmp2[u][r, c, :, :], op0=ALU.max, op1=ALU.add)
                last.then_inc(S["wide_ready"], 1)

            def rotated_keys(s, u):
                dve.wait_ge(S["qkv_ready"], n("qkv_ready", s))
                qk = a.qkv[u][:, 0:2, :].rearrange("p c x -> p (c x)")
                x = a.tmp[u][:, :, :, :].rearrange("p c h d -> p (c h) d")
                y = a.tmp2[u][:, :, :, :].rearrange("p c h d -> p (c h) d")
                nc.vector.tensor_tensor(x.rearrange("p h d -> p (h d)"), qk, qk, ALU.mult).then_inc(S["squared"], 1)
                dve.wait_ge(S["squared"], n("squared", s))
                nc.vector.tensor_reduce(a.r24[u][:, :], x, AX.X, ALU.add).then_inc(S["square_sums"], 1)
                dve.wait_ge(S["square_sums"], n("square_sums", s))
                nc.vector.tensor_scalar(a.t24[u][:, :], a.r24[u][:, :], 1.0 / HD, 1.1920928955078125e-07,
                                        ALU.mult, ALU.add).then_inc(S["ms_ready"], 1)
                for b in two:
                    r = slice(64 * b, 64 * b + 64)
                    nc.vector.tensor_copy(a.wide[u][r, 2, :, b, :], a.qkv[u][r, 2, :].rearrange("p (h d) -> p h d", d=HD))
                dve.wait_ge(S["rms_ready"], n("rms_ready", s))
                nc.vector.tensor_tensor(x, a.qkv[u][:, 0:2, :].rearrange("p c (h d) -> p (c h) d", d=HD),
                                        bcast(a.r24[u][:, :].unsqueeze(2), [P, 2 * HEADS, HD]), ALU.mult).then_inc(S["normed"], 1)
                dve.wait_ge(S["normed"], n("normed", s))
                half = [P, 2 * HEADS, HD // 2]
                nc.vector.tensor_tensor(y[:, :, 0:8], x[:, :, 8:16], bcast(const(k, "sin").unsqueeze(1), half), ALU.mult)
                nc.vector.tensor_tensor(y[:, :, 8:16], x[:, :, 0:8], bcast(const(k, "nsin").unsqueeze(1), half),
                                        ALU.mult).then_inc(S["crossed"], 1)
                dve.wait_ge(S["crossed"], n("crossed", s))
                x4 = a.tmp[u][:, :, :, :].rearrange("p c h (s d) -> p (c h s) d", s=2)
                nc.vector.tensor_tensor(x4, x4, bcast(const(k, "cos").unsqueeze(1), [P, 4 * HEADS, HD // 2]),
                                        ALU.mult).then_inc(S["cosined"], 1)
                dve.wait_ge(S["cosined"], n("cosined", s))
                for b in two:
                    r = slice(64 * b, 64 * b + 64)
                    last = nc.vector.tensor_tensor(a.wide[u][r, 0:2, :, b, :], a.tmp[u][r, :, :, :], a.tmp2[u][r, :, :, :], ALU.add)
                last.then_inc(S["wide_ready"], 1)

            def masked_maximum(s, u):
                dve.wait_ge(S["scored"], n("scored", s))
                if kind in ("softmax", "rotary"):
                    nc.vector.tensor_tensor(a.sc[u][:, :, :], score, bcast(const(k, "causal_add").unsqueeze(1), every),
                                            ALU.add).then_inc(S["masked"], 1)
                    dve.wait_ge(S["masked"], n("masked", s))
                    nc.vector.tensor_reduce(a.max[u][:, :], a.sc[u][:, :, :], AX.X, ALU.max).then_inc(S["max_ready"], 1)
                if kind == "linear":
                    nc.vector.tensor_tensor(a.pr[u][:, :, :], score, bcast(const(k, "causal01").unsqueeze(1), every),
                                            ALU.mult).then_inc(S["p_ready"], 1)
                if kind == "segments":
                    nc.vector.tensor_reduce(a.seg[u][:, :, 0:4], score.rearrange("p h (s t) -> p h s t", t=SEG),
                                            AX.X, ALU.add).then_inc(S["seg16"], 1)
                    nc.vector.tensor_tensor(a.sc[u][:, :, :], score, bcast(const(k, "tail01").unsqueeze(1), every),
                                            ALU.mult).then_inc(S["masked"], 1)
                    dve.wait_ge(S["seg16"], n("seg16", s))
                    pairs = a.seg[u][:, :, 0:4].rearrange("p h (s t) -> p h s t", t=2)
                    nc.vector.tensor_tensor(a.seg[u][:, :, 4:6], pairs[:, :, :, 0], pairs[:, :, :, 1],
                                            ALU.add).then_inc(S["seg32"], 1)
                    dve.wait_ge(S["masked"], n("masked", s))
                    nc.vector.tensor_reduce(a.seg[u][:, :, 7:8], a.sc[u][:, :, :], AX.X, ALU.add)
                    dve.wait_ge(S["seg32"], n("seg32", s))
                    nc.vector.tensor_tensor(a.seg[u][:, :, 6:7], a.seg[u][:, :, 4:5], a.seg[u][:, :, 5:6],
                                            ALU.add).then_inc(S["seg64"], 1)
                    dve.wait_ge(S["seg64"], n("seg64", s))
                    nc.vector.tensor_tensor(a.seg[u][:, :, :], a.seg[u][:, :, :],
                                            bcast(const(k, "seg_add").unsqueeze(1), [P, HEADS, 8]), ALU.add).then_inc(S["seg_masked"], 1)
                    dve.wait_ge(S["seg_masked"], n("seg_masked", s))
                    nc.vector.tensor_reduce(a.max[u][:, :], a.seg[u][:, :, :], AX.X, ALU.max).then_inc(S["max_ready"], 1)

            def weights(s, u):
                if kind in ("softmax", "rotary"):
                    dve.wait_ge(S["exped"], n("exped", s))
                    nc.vector.tensor_reduce(a.sum[u][:, :], a.pr[u][:, :, :], AX.X, ALU.add).then_inc(S["sum_ready"], 1)
                    dve.wait_ge(S["sum_ready"], n("sum_ready", s))
                    nc.vector.reciprocal(a.rsum[u][:, :], a.sum[u][:, :]).then_inc(S["rsum_ready"], 1)
                if kind == "linear":
                    dve.wait_ge(S["p_ready"], n("p_ready", s))
                    nc.vector.tensor_reduce(a.sum[u][:, :], a.pr[u][:, :, :], AX.X, ALU.add).then_inc(S["sum_ready"], 1)
                    dve.wait_ge(S["sum_ready"], n("sum_ready", s))
                    nc.vector.tensor_scalar_add(a.max[u][:, :], a.sum[u][:, :], 1e-6).then_inc(S["max_ready"], 1)
                    dve.wait_ge(S["max_ready"], n("max_ready", s))
                    nc.vector.reciprocal(a.rsum[u][:, :], a.max[u][:, :]).then_inc(S["rsum_ready"], 1)
                if kind == "segments":
                    dve.wait_ge(S["exped"], n("exped", s))
                    w4 = a.seg[u][:, :, 0:4].rearrange("p h (s t) -> p h s t", t=2)
                    nc.vector.tensor_tensor(w4, a.segp[u][:, :, 0:4].rearrange("p h (s t) -> p h s t", t=2),
                                            bcast(a.segp[u][:, :, 4:6].unsqueeze(3), [P, HEADS, 2, 2]), ALU.add).then_inc(S["w32"], 1)
                    nc.vector.tensor_tensor(a.sc[u][:, :, :], bcast(const(k, "tail01").unsqueeze(1), every),
                                            bcast(a.segp[u][:, :, 7:8], every), ALU.mult).then_inc(S["tail_ready"], 1)
                    dve.wait_ge(S["w32"], n("w32", s))
                    nc.vector.tensor_tensor(a.seg[u][:, :, 0:4], a.seg[u][:, :, 0:4],
                                            bcast(a.segp[u][:, :, 6:7], [P, HEADS, 4]), ALU.add).then_inc(S["w64"], 1)
                    nc.vector.tensor_reduce(a.sum[u][:, :], a.segp[u][:, :, :], AX.X, ALU.add).then_inc(S["sum_ready"], 1)
                    dve.wait_ge(S["w64"], n("w64", s))
                    dve.wait_ge(S["tail_ready"], n("tail_ready", s))
                    nc.vector.tensor_tensor(a.pr[u][:, :, :].rearrange("p h (s t) -> p h s t", t=SEG),
                                            a.sc[u][:, :, :].rearrange("p h (s t) -> p h s t", t=SEG),
                                            bcast(a.seg[u][:, :, 0:4].unsqueeze(3), [P, HEADS, 4, SEG]),
                                            ALU.add).then_inc(S["p_ready"], 1)
                    dve.wait_ge(S["sum_ready"], n("sum_ready", s))
                    nc.vector.reciprocal(a.rsum[u][:, :], a.sum[u][:, :]).then_inc(S["rsum_ready"], 1)

            def normalised(s, u):
                dve.wait_ge(S["rsum_ready"], n("rsum_ready", s))
                dve.wait_ge(S["mixed"], n("mixed", s))
                o = bank(k, 7)[:, 0:2 * C].rearrange("p (h b d) -> p h b d", b=2, d=HD)
                for b in two:
                    r = slice(64 * b, 64 * b + 64)
                    last = nc.vector.tensor_tensor(a.os[u][r, :, :], o[r, :, b, :],
                                                   bcast(a.rsum[u][r, :].unsqueeze(2), [64, HEADS, HD]), ALU.mult)
                last.then_inc(S["o_scaled" if kind == "linear" else "os_ready"], 1)
                if kind == "linear":
                    dve.wait_ge(S["o_scaled"], n("o_scaled", s))
                    nc.vector.tensor_reduce(a.hs[u][:, :], a.os[u][:, :, :], AX.X, ALU.add).then_inc(S["hsum"], 1)
                    dve.wait_ge(S["hsum"], n("hsum", s))
                    nc.vector.scalar_tensor_tensor(out=a.os[u][:, :, :], in0=a.os[u][:, :, :], scalar=float(HD),
                                                   in1=bcast(a.hs[u][:, :].unsqueeze(2), heads),
                                                   op0=ALU.mult, op1=ALU.subtract).then_inc(S["hcentred"], 1)
                    dve.wait_ge(S["hcentred"], n("hcentred", s))
                    nc.vector.tensor_tensor(a.hsq[u][:, :, :], a.os[u][:, :, :], a.os[u][:, :, :],
                                            ALU.mult).then_inc(S["hsquared"], 1)
                    dve.wait_ge(S["hsquared"], n("hsquared", s))
                    nc.vector.tensor_reduce(a.hs[u][:, :], a.hsq[u][:, :, :], AX.X, ALU.add).then_inc(S["hsqsum"], 1)
                    dve.wait_ge(S["hsqsum"], n("hsqsum", s))
                    nc.vector.tensor_scalar(a.t24[u][:, 0:HEADS], a.hs[u][:, :], 1.0 / HD, LN_EPS * HD * HD,
                                            ALU.mult, ALU.add).then_inc(S["hvar_ready"], 1)
                    dve.wait_ge(S["hrstd_ready"], n("hrstd_ready", s))
                    nc.vector.tensor_tensor(a.os[u][:, :, :], a.os[u][:, :, :],
                                            bcast(a.r24[u][:, 0:HEADS].unsqueeze(2), heads), ALU.mult).then_inc(S["hnormed"], 1)
                    dve.wait_ge(S["hnormed"], n("hnormed", s))
                    nc.vector.tensor_tensor(a.os[u][:, :, :], a.os[u][:, :, :],
                                            bcast(const(k, "mn_w").unsqueeze(1), heads), ALU.mult).then_inc(S["hweighted"], 1)
                    dve.wait_ge(S["hweighted"], n("hweighted", s))
                    nc.vector.tensor_tensor(a.os[u][:, :, :], a.os[u][:, :, :],
                                            bcast(const(k, "mn_b").unsqueeze(1), heads), ALU.add).then_inc(S["os_ready"], 1)

            def slot(s, u, in_a, in_b, in_c):
                if in_a:
                    input_rows(s, u)
                if in_b:
                    masked_maximum(s - 1, 1 - u)
                if in_a and kind == "segments":
                    bilinear_values(s, u)
                if in_a and kind == "linear":
                    positive_keys(s, u)
                if in_a and kind == "rotary":
                    rotated_keys(s, u)
                if in_c:
                    normalised(s - 2, u)
                if in_b:
                    weights(s - 1, 1 - u)
                if in_a:
                    dve.wait_ge(S["folded"], n("folded", s))
                    if not (isinstance(s, int) and s < 2):
                        dve.wait_ge(S["mixed"], n("mixed", s - 2))
                    v = bank(k, 2)[:, 0:2 * C].rearrange("p (a h b d) -> p a h b d", a=PAIRS, h=2, b=2)
                    for h in two:
                        r = slice(64 * h, 64 * h + 64)
                        last = nc.vector.tensor_copy(a.vd[u][r, :, h, :, :].rearrange("p a b d -> p a (b d)"),
                                                     v[r, :, h, :, :].rearrange("p a b d -> p a (b d)"))
                    last.then_inc(S["vd_ready"], 1)
                if in_c:
                    tile = s - 2
                    dve.wait_ge(S["projected"], n("projected", tile))
                    nc.vector.tensor_tensor(tile_of(k.x1, tile) if keep else k.ys[u][:, :], tile_of(k.h, tile),
                                            bank(k, 5)[:, 256:256 + C], ALU.add).then_inc(S["y_ready"], 1)
                    if not keep:
                        dve.wait_ge(S["y_ready"], n("y_ready", tile))
                        ln_stats(nc, k, dve, k.ys[u][:, :], tile, "out_")
                        ln_apply(nc, k, dve, tile_of(k.h, tile), k.ys[u][:, :], tile, "out_")

            in_slots(dve, slot)

    both = ["x_ready", "x_turned", "xt_ready", "qkv_projected", "wide_ready", "folded", "qk_ready", "vd_ready",
            "scored", "p_turned", "prt_ready", "mixed", "os_ready", "o_turned", "ot_ready",
            "projected", "y_ready", "rsum_ready", "sum_ready", "max_ready"]
    both += ["in_" + x for x in LN_SIGNALS if pre_ln] + ["out_" + x for x in LN_SIGNALS if not keep]
    if kind != "softmax":
        both.append("qkv_ready")
    both += ["p_ready"] if kind == "linear" else ["centred", "exped", "masked"]
    if kind == "segments":
        both.append("p_ready")
    S.passed(wattn_loaded=16, **dict.fromkeys(both, TILES))


def turn(nc, k, source, target, kind="raw"):
    S = k.S
    two = (0, 1)
    block_of = k.nc.Block()
    with block_of as block:
        def n(name, i, u):
            return i * 2 + (S.at(name) + u + 1)

        @block.vector
        def _(dve):
            with dve.Fori(0, TILES // 2) as i:
                for u in two:
                    tile = i * 2 + u
                    row = tile_of(source, tile)
                    if kind == "ln2":
                        ln_stats(nc, k, dve, row, tile, "in_")
                        dve.wait_ge(S["x_turned"], n("x_turned", i, u))
                        ln_apply(nc, k, dve, k.xs[u][:, :], row, tile, "in_").then_inc(S["x_ready"], 1)
                        dve.wait_ge(S["x_ready"], n("x_ready", i, u))
                        nc.vector.tensor_copy(tile_of(k.rows, tile), k.xs[u][:, :])
                    else:
                        dve.wait_ge(S["x_turned"], n("x_turned", i, u))
                        nc.vector.tensor_copy(k.xs[u][:, :], row).then_inc(S["x_ready"], 1)
        if kind != "raw":
            @block.gpsimd
            def _(pool):
                with pool.Fori(0, TILES // 2) as i:
                    for u in two:
                        ln_power(nc, k, pool, i * 2 + u, "in_")

        @block.tensor
        def _(pe):
            pe.sem_inc(S["x_turned"], 2)
            with pe.Fori(0, TILES // 2) as i:
                for u in two:
                    pe.wait_ge(S["x_ready"], n("x_ready", i, u))
                    pe.wait_ge(S["turned_free"], n("turned_free", i, u))
                    for f in two:
                        last = nc.tensor.transpose(bank(k, u)[0:KH, f * P:(f + 1) * P],
                                                   k.xs[u][:, f * KH:(f + 1) * KH], const(k, "ident"))
                    last.then_inc(S["x_turned"], 1)

        @block.scalar
        def _(act):
            act.sem_inc(S["turned_free"], 2)
            with act.Fori(0, TILES // 2) as i:
                for u in two:
                    act.wait_ge(S["x_turned"], n("x_turned", i, u + 2))
                    for f in two:
                        dst = target[0:KH, f, bass.ds(i * (2 * P) + u * P, P)]
                        src = bank(k, u)[0:KH, f * P:(f + 1) * P]
                        if kind == "ln2":
                            last = nc.scalar.activation(dst, src, ACT.Identity, scale=small(k, "ln2_w")[0:KH, f, :],
                                                        bias=small(k, "ln2_b")[0:KH, f, :])
                        else:
                            last = nc.scalar.activation(dst, src, ACT.Copy)
                    last.then_inc(S["turned_free"], 1)
    pairs = ["in_" + x for x in LN_SIGNALS] if kind != "raw" else []
    S.passed(**dict.fromkeys(pairs, TILES), x_ready=TILES, x_turned=TILES + 2, turned_free=TILES + 2)


def gates(nc, k):
    S, a = k.S, k.a
    with ExitStack() as own:
        sb = lambda name, shape: own.enter_context(nc.sbuf_tensor(name, shape, F32))
        hidden = sb("gate_hidden", [P, TOKENS])
        params = sb("gate_params", [P, TILES, 5, HEADS])
        amp = sb("gate_amp", [P, 2, TILES, HEADS])
        phase = sb("gate_phase", [P, 2, TILES, HEADS])
        temp = sb("gate_temp", [P, 1])
        block = own.enter_context(nc.Block())

        @block.tensor
        def _(pe):
            for g in range(2):
                for f in range(2):
                    last = nc.tensor.matmul(bank(k, g), small(k, "wb1")[0:KH, f, :], k.ht[0:KH, f, g * BANK:(g + 1) * BANK],
                                            start=(f == 0), stop=(f == 1))
            last.then_inc(S["gate_up"], 1)
            pe.wait_ge(S["gate_hidden_ready"], 1)
            for t in range(TILES):
                last = nc.tensor.matmul(bank(k, 2)[:, t * 60:(t + 1) * 60], hidden[:, t * P:(t + 1) * P],
                                        const(k, "wb2"), start=True, stop=True)
            last.then_inc(S["gate_down"], 1)

        @block.scalar
        def _(act):
            act.wait_ge(S["gate_up"], 1)
            nc.scalar.activation(hidden[:, :], banks(k, 0, 2), ACT.Silu).then_inc(S["gate_hidden_ready"], 1)
            act.wait_ge(S["gate_params_ready"], 1)
            for j in range(2):
                nc.scalar.activation(amp[:, j, :, :], params[:, :, 2 * j, :], ACT.Tanh, scale=0.5)
                last = nc.scalar.activation(phase[:, j, :, :], params[:, :, 2 * j + 1, :], ACT.Tanh)
            last.then_inc(S["gate_tanh"], 1)
            act.wait_ge(S["gate_difference"], 1)
            nc.scalar.activation(phase[:, 1, :, :], phase[:, 0, :, :], ACT.Sin, scale=math.pi / 2).then_inc(S["gate_sine"], 1)
            act.wait_ge(S["gate_angle"], 1)
            nc.scalar.activation(amp[:, 1, :, :], amp[:, 0, :, :], ACT.Tanh).then_inc(S["gate_inter"], 1)
            act.wait_ge(S["gate_scaled"], 1)
            nc.scalar.activation(amp[:, 1, :, :], amp[:, 0, :, :], ACT.Tanh, scale=0.5).then_inc(S["gate_last"], 1)

        @block.vector
        def _(dve):
            steps = [0]

            def then(ins):
                steps[0] += 1
                ins.then_inc(S["gate_step"], 1)
                dve.wait_ge(S["gate_step"], steps[0])

            then(nc.vector.tensor_scalar(temp[:, :], const(k, "temperature"), 0.1, 2.0, ALU.max, ALU.min))
            dve.wait_ge(S["gate_down"], 1)
            nc.vector.tensor_copy(params[:, :, :, :].rearrange("p t j h -> p (t j h)"),
                                  bank(k, 2)[:, 0:TILES * 60]).then_inc(S["gate_params_ready"], 1)
            dve.wait_ge(S["gate_tanh"], 1)
            then(nc.vector.tensor_scalar(amp[:, :, :, :], amp[:, :, :, :], 0.5, 0.5, ALU.mult, ALU.add))
            nc.vector.tensor_tensor(phase[:, 0, :, :], phase[:, 0, :, :], phase[:, 1, :, :],
                                    ALU.subtract).then_inc(S["gate_difference"], 1)
            then(nc.vector.tensor_tensor(amp[:, 0, :, :], amp[:, 0, :, :], amp[:, 1, :, :], ALU.mult))
            dve.wait_ge(S["gate_sine"], 1)
            then(nc.vector.tensor_tensor(phase[:, 0, :, :], phase[:, 1, :, :], phase[:, 1, :, :], ALU.mult))
            then(nc.vector.tensor_scalar(phase[:, 1, :, :], phase[:, 0, :, :], -2.0, 1.0, ALU.mult, ALU.add))
            nc.vector.tensor_tensor(amp[:, 0, :, :], amp[:, 0, :, :], phase[:, 1, :, :], ALU.mult).then_inc(S["gate_angle"], 1)
            dve.wait_ge(S["gate_inter"], 1)
            nc.vector.tensor_scalar(amp[:, 0, :, :], amp[:, 1, :, :], temp[:, :], None, ALU.mult).then_inc(S["gate_scaled"], 1)
            dve.wait_ge(S["gate_last"], 1)
            nc.vector.tensor_scalar(a.gate1[:, :, :], amp[:, 1, :, :], 0.5, 1.5, ALU.mult, ALU.add)


def route(nc, k, layer):
    S = k.S
    E = MOES[f"l{layer}"]["experts"]
    cap = MOES[f"l{layer}"]["cap"]
    top = 3 if layer == 1 else 2
    tag = f"route{layer}_"
    with ExitStack() as own:
        sb = lambda name, shape, dt=F32: own.enter_context(nc.sbuf_tensor(tag + name, shape, dt))
        logits = sb("logits", [P, TILES, E])
        probs = sb("probs", [P, TILES, E])
        best = sb("best", [P, TILES, 8])
        index = sb("index", [P, TILES, 8], U32)
        indexf = sb("indexf", [P, TILES, 8])
        hot = sb("hot", [P, top, TILES, E])
        weight = sb("weight", [P, top, TILES])
        small1 = sb("small1", [P, TILES])
        prefix = sb("prefix", [P, 2, TILES, E])
        counted = sb("counted", [P, 2, TILES, E])
        kept = sb("kept", [P, 2, TILES, E])
        place, has_room, slot = [sb(nm, [P, 2, TILES]) for nm in ("place", "has_room", "slot")]
        block = own.enter_context(nc.Block())
        shape = [P, TILES, E]

        @block.tensor
        def _(pe):
            for t in range(TILES):
                for f in range(2):
                    last = nc.tensor.matmul(bank(k, 0)[:, t * E:(t + 1) * E], k.ht[0:KH + f, f, t * P:(t + 1) * P],
                                            small(k, f"gate{layer}")[0:KH + f, f, :], start=(f == 0), stop=(f == 1))
            last.then_inc(S["logits_done"], 1)
            if cap:
                width = 2 if layer == 0 else 1
                pe.wait_ge(S["prefix_ready"], S.at("prefix_ready") + 1)
                src = hot if layer == 0 else counted
                out = bank(k, 1)[:, 0:width * TILES * E]
                nc.tensor.matmul(out, const(k, "earlier"), src[:, 0:width, :, :].rearrange("p c t e -> p (c t e)"),
                                 start=True, stop=False)
                nc.tensor.matmul(out, const(k, "ones"), prefix[:, 0:width, :, :].rearrange("p c t e -> p (c t e)"),
                                 start=False, stop=True).then_inc(S["ranked"], 1)

        if cap:
            @block.gpsimd
            def _(pool):
                pool.wait_ge(S["slots_cleared"], 16)
                pool.wait_ge(S["slots_ready"], S.at("slots_ready") + 1)
                for c in range(2):
                    for t in range(TILES):
                        nc.gpsimd.indirect_dma_start(k.sent, bass.IndirectOffsetOnAxis(ap=k.slot[:, c, t:t + 1], axis=0),
                                                     k.rows[:, t, :], None).then_inc(S["rows_sent"], 16)
                pool.wait_ge(S["rows_sent"], S.at("rows_sent") + 16 * 2 * TILES)

        @block.scalar
        def _(act):
            if layer == 0:
                act.wait_ge(S["route_gap"], 1)
                nc.scalar.activation(weight[:, 1, :], small1[:, :], ACT.Exp).then_inc(S["route_exp"], 1)
            else:
                act.wait_ge(S["route_gap"], S.at("route_gap") + 1)
                nc.scalar.activation(probs[:, :, :], logits[:, :, :], ACT.Exp).then_inc(S["route_exp"], 1)

        @block.vector
        def _(dve):
            at = [S.at("route_step")]

            def then(ins):
                at[0] += 1
                ins.then_inc(S["route_step"], 1)
                dve.wait_ge(S["route_step"], at[0])

            dve.wait_ge(S["logits_done"], S.at("logits_done") + 1)
            then(nc.vector.tensor_copy(logits[:, :, :], bank(k, 0)[:, 0:TILES * E].rearrange("p (t e) -> p t e", e=E)))
            source = logits
            if layer > 0:
                if layer == 1:
                    then(nc.vector.memset(logits[:, :, 0:1], -1e9))
                then(nc.vector.tensor_reduce(small1[:, :], logits[:, :, :], AX.X, ALU.max))
                nc.vector.tensor_tensor(logits[:, :, :], logits[:, :, :], bcast(small1[:, :].unsqueeze(2), shape),
                                        ALU.subtract).then_inc(S["route_gap"], 1)
                dve.wait_ge(S["route_exp"], S.at("route_exp") + 1)
                then(nc.vector.tensor_reduce(small1[:, :], probs[:, :, :], AX.X, ALU.add))
                then(nc.vector.reciprocal(small1[:, :], small1[:, :]))
                then(nc.vector.tensor_tensor(probs[:, :, :], probs[:, :, :], bcast(small1[:, :].unsqueeze(2), shape), ALU.mult))
                source = probs
            for t in range(TILES):
                last = nc.vector.max(best[:, t, :], source[:, t, :])
            then(last)
            for t in range(TILES):
                last = nc.vector.max_index(index[:, t, :], best[:, t, :], source[:, t, :])
            then(last)
            then(nc.vector.tensor_copy(indexf[:, :, :], index[:, :, :]))
            for c in range(top):
                last = nc.vector.tensor_tensor(hot[:, c, :, :], bcast(const(k, "iota")[:, 0:E].unsqueeze(1), shape),
                                               bcast(indexf[:, :, c:c + 1], shape), ALU.is_equal)
            then(last)
            if layer == 0:
                nc.vector.tensor_tensor(small1[:, :], best[:, :, 1], best[:, :, 0], ALU.subtract).then_inc(S["route_gap"], 1)
                dve.wait_ge(S["route_exp"], 1)
                then(nc.vector.tensor_scalar_add(small1[:, :], weight[:, 1, :], 1.0))
                then(nc.vector.reciprocal(weight[:, 0, :], small1[:, :]))
                then(nc.vector.tensor_tensor(weight[:, 1, :], weight[:, 1, :], weight[:, 0, :], ALU.mult))
            elif layer == 1:
                for c in range(top):
                    last = nc.vector.tensor_copy(weight[:, c, :], best[:, :, c])
                then(last)
            else:
                then(nc.vector.tensor_tensor(small1[:, :], best[:, :, 0], best[:, :, 1], ALU.add))
                then(nc.vector.reciprocal(small1[:, :], small1[:, :]))
                for c in range(top):
                    last = nc.vector.tensor_tensor(weight[:, c, :], best[:, :, c], small1[:, :], ALU.mult)
                then(last)
            if cap:
                if layer == 0:
                    order = [(c, t) for c in range(2) for t in range(TILES)]
                    tokens = hot
                else:
                    then(nc.vector.tensor_tensor(counted[:, 0, :, :], hot[:, 0, :, :], hot[:, 1, :, :], ALU.add))
                    order = [(0, t) for t in range(TILES)]
                    tokens = counted
                last = nc.vector.memset(prefix[:, 0, 0, :], 0.0)
                for (c0, t0), (c1, t1) in zip(order, order[1:]):
                    then(last)
                    last = nc.vector.tensor_tensor(prefix[:, c1, t1, :], prefix[:, c0, t0, :], tokens[:, c0, t0, :], ALU.add)
                last.then_inc(S["prefix_ready"], 1)
                dve.wait_ge(S["ranked"], S.at("ranked") + 1)
                width = 2 * TILES * E if layer == 0 else TILES * E
                rank = bank(k, 1)[:, 0:width].rearrange("p (c t e) -> p c t e", t=TILES, e=E)
                for c in range(2):
                    last = nc.vector.tensor_tensor(kept[:, c, :, :], hot[:, c, :, :], rank[:, c if layer == 0 else 0, :, :], ALU.mult)
                then(last)
                then(nc.vector.tensor_reduce(place[:, :, :], kept[:, :, :, :], AX.X, ALU.add))
                nc.vector.tensor_scalar(has_room[:, :, :], place[:, :, :], float(cap), None, ALU.is_lt)
                then(nc.vector.scalar_tensor_tensor(out=slot[:, :, :], in0=indexf[:, :, 0:2].rearrange("p t c -> p c t"),
                                                    scalar=float(cap), in1=place[:, :, :], op0=ALU.mult, op1=ALU.add))
                refused = const(k, "refused").rearrange("p (c t) -> p c t", c=2)
                then(nc.vector.tensor_tensor(slot[:, :, :], slot[:, :, :], refused, ALU.subtract))
                then(nc.vector.tensor_tensor(slot[:, :, :], slot[:, :, :], has_room[:, :, :], ALU.mult))
                then(nc.vector.tensor_tensor(slot[:, :, :], slot[:, :, :], refused, ALU.add))
                nc.vector.tensor_copy(k.slot[:, :, :], slot[:, :, :]).then_inc(S["slots_ready"], 1)
                then(nc.vector.tensor_scalar(slot[:, :, :], slot[:, :, :], float(SLOTS - 1), None, ALU.min))
                nc.vector.tensor_copy(k.back[:, :, :], slot[:, :, :])
                then(nc.vector.tensor_tensor(k.share[:, :, :], weight[:, :, :], has_room[:, :, :], ALU.mult))
                if layer == 0:
                    nc.vector.tensor_tensor(k.acc[:, :, :], k.h[:, :, :], k.x1[:, :, :], ALU.add)
                else:
                    then(nc.vector.tensor_tensor(small1[:, :], k.share[:, 0, :], k.share[:, 1, :], ALU.add))
                    then(nc.vector.tensor_scalar_add(small1[:, :], small1[:, :], 1.0))
                    nc.vector.tensor_tensor(k.acc[:, :, :], k.h[:, :, :], bcast(small1[:, :].unsqueeze(2), [P, TILES, C]), ALU.mult)
            else:
                for c in range(top):
                    last = nc.vector.tensor_tensor(hot[:, c, :, :], hot[:, c, :, :], bcast(weight[:, c, :].unsqueeze(2), shape), ALU.mult)
                then(last)
                dst = k.combine[:, :, 0:E]
                then(nc.vector.tensor_tensor(dst, hot[:, 0, :, :], hot[:, 1, :, :], ALU.add))
                then(nc.vector.tensor_tensor(dst, dst, hot[:, 2, :, :], ALU.add))
                then(nc.vector.tensor_scalar_add(k.combine[:, :, 0:1], k.combine[:, :, 0:1], 1.0))
            route.steps = at[0] - S.at("route_step")
    S.passed(logits_done=1, route_gap=1, route_exp=1, route_step=route.steps,
             **(dict(prefix_ready=1, ranked=1, slots_ready=1, rows_sent=16 * 2 * TILES) if cap else {}))


def allocate_experts(nc, k, ctx):
    def sb(name, shape):
        return ctx.enter_context(nc.sbuf_tensor(name, shape, F32))

    k.combine = sb("combine", [P, TILES, 16])
    k.combine_t = sb("combine_t", [48, TILES, P])
    k.expert_rows = sb("expert_rows", [48, C])
    k.acc = sb("acc", [P, TILES, C])
    k.rows = sb("rows", [P, TILES, C])
    k.share = sb("share", [P, 2, TILES])
    k.slot = ctx.enter_context(nc.sbuf_tensor("slot", [P, 2, TILES], U32))
    k.back = ctx.enter_context(nc.sbuf_tensor("back", [P, 2, TILES], U32))


def experts(nc, k, io, layer, x):
    S = k.S
    M = MOES[f"l{layer}"]
    E, UP, HID = M["experts"], M["up"], M["hid"]
    W2 = C + 1 if layer == 1 else C
    GROUP = 4
    RING = {0: 4, 1: 3, 2: 2}[layer]
    DOWN = 1 if layer == 1 else GROUP
    CREDIT = 2 * DOWN + 1
    tag = f"l{layer}_"
    name = lambda x: tag + x
    two = (0, 1)
    with ExitStack() as own:
        sb = lambda nm, shape: own.enter_context(nc.sbuf_tensor(tag + nm, shape, F32))
        w1 = [sb(f"w1_{s}", [KH, 2, UP * P]) for s in two]
        w2 = [sb(f"w2_{s}", [P, HID, C]) for s in two]
        side = [sb(f"side{s}", [P, 16]) for s in two]
        hid = [sb(f"hid{g}", [P, HID, BANK]) for g in two]
        if layer == 1:
            w2s = [sb(f"w2s{s}", [P, HID, W2]) for s in two]
            square = [sb(f"square{g}", [P, HID, BANK]) for g in two]
            mean, msq, vareps, rstd, weight = [sb(nm, [P, GROUP]) for nm in ("mean", "msq", "vareps", "rstd", "weight")]
            coef = sb("coef", [P, TILES, 48])
            fixed_t = sb("fixed_t", [KH, 2, 2, 16])
        if layer == 2:
            silu = [sb(f"silu{b}", [P, BANK]) for b in two]
            kept_sum = sb("kept_sum", [P, TILES])
        block = own.enter_context(nc.Block())
        halves = banks(k, 4, 4).rearrange("p (t c) -> p t c", t=TILES)[:, :, 0:C]

        def n(i, s, g, each=1, j=0, credit=0):
            return i * (4 * each) + ((2 * s + g) * each + j + 1 + credit)

        def e(i, s, more=1):
            return i * 2 + (s + more)

        @block.sync
        def _(sp):
            with sp.Fori(0, E // 2) as i:
                for s in two:
                    sp.wait_ge(S[name("down_done")], i * (4 * DOWN) + (2 * DOWN * s + 1))
                    at = bass.ds(e(i, s, 0), 1)
                    sp.dma_start(w1[s][:, :, :].rearrange("p f h -> p (f h)"),
                                 io[tag + "w1"][at, :, :].rearrange("a p x -> p (a x)")).then_inc(S[name(f"w{s}_loaded")], 16)
                    sp.dma_start(w2[s][:, :, :].rearrange("p f h -> p (f h)"),
                                 io[tag + "w2"][at, :, :].rearrange("a p x -> p (a x)")).then_inc(S[name(f"w{s}_loaded")], 16)
                    sp.dma_start(side[s][:, :],
                                 io[tag + "side"][at, :, :].rearrange("a p x -> p (a x)")).then_inc(S[name(f"w{s}_loaded")], 16)

        if layer == 1:
            @block.gpsimd
            def _(pool):
                nc.gpsimd.memset(w2s[0][:, :, C:C + 1], 1.0)
                nc.gpsimd.memset(w2s[1][:, :, C:C + 1], 1.0)
                with pool.Fori(0, E // 2) as i:
                    for s in two:
                        pool.wait_ge(S[name(f"w{s}_loaded")], i * 48 + 48)
                        pool.wait_ge(S[name("down_done")], i * (4 * DOWN) + (2 * DOWN * s + 1))
                        nc.gpsimd.tensor_tensor(w2s[s][:, :, 0:C], w2[s][:, :, :],
                                                bcast(side[s][:, 4:4 + HID].unsqueeze(2), [P, HID, C]),
                                                ALU.mult).then_inc(S[name("w2s_ready")], 1)
                        for g in two:
                            pool.wait_ge(S[name("vareps_ready")], n(i, s, g))
                            nc.gpsimd.tensor_tensor(rstd[:, :], vareps[:, :], k.minus_half[:, 0:GROUP],
                                                    ALU.pow).then_inc(S[name("rstd_ready")], 1)

        @block.tensor
        def _(pe):
            pe.sem_inc(S[name("down_done")], CREDIT)
            ident = const(k, "ident")
            if layer == 0:
                for t in range(TILES):
                    last = nc.tensor.transpose(banks(k, 0, 2)[0:8, t * P:(t + 1) * P], k.combine[:, t, 0:8], ident)
                last.then_inc(S[name("combine_turned")], 1)
                pe.wait_ge(S[name("rows_loaded")], 16)
                pe.wait_ge(S[name("combine_t_ready")], 1)
                for t in range(TILES):
                    last = nc.tensor.matmul(halves[:, t, :], k.combine_t[0:8, t, :], k.expert_rows[0:8, :],
                                            start=True, stop=True)
                last.then_inc(S[name("rows_added")], 1)
            with pe.Fori(0, E // 2) as i:
                for s in two:
                    pe.wait_ge(S[name(f"w{s}_loaded")], i * 48 + 48)
                    if layer == 1:
                        pe.wait_ge(S[name("fixed_read")], e(i, s))
                        for f in two:
                            for m in range(HID):
                                last = nc.tensor.matmul(bank(k, 3)[0:KH, 2 * f:2 * f + 2], w2[s][:, m, f * KH:(f + 1) * KH],
                                                        side[s][:, 4 + m:8 + m:3], start=(m == 0), stop=(m == HID - 1))
                        last.then_inc(S[name("fixed_done")], 1)
                    if layer == 2:
                        pe.wait_ge(S[name("w1_scaled")], e(i, s))
                    for g in two:
                        for m in range(UP):
                            if layer == 2:
                                if m % 2 == 0:
                                    pe.wait_ge(S[name("hid_ready")], n(i, s, g, HID, m // 2))
                                b = m % 4
                            else:
                                pe.wait_ge(S[name("hid_ready")], n(i, s, g, HID, m))
                                b = m if layer == 1 else (UP * g + m) % 4
                            for f in two:
                                last = nc.tensor.matmul(bank(k, b), w1[s][:, f, m * P:(m + 1) * P],
                                                        x[0:KH, f, g * BANK:(g + 1) * BANK], start=(f == 0), stop=(f == 1))
                            last.then_inc(S[name("up_done")], 1)
                        if layer == 1:
                            pe.wait_ge(S[name("w2s_ready")], e(i, s))
                        pe.wait_ge(S[name("hid_ready")], n(i, s, g, HID, HID - 1, RING))
                        for t in range(GROUP):
                            pe.wait_ge(S[name("acc_done")], n(i, s, g, GROUP, t))
                            for m in range(HID):
                                rhs = w2s[s][:, m, :] if layer == 1 else w2[s][:, m, :]
                                last = nc.tensor.matmul(bank(k, 4 + t)[:, 0:W2], hid[g][:, m, t * P:(t + 1) * P], rhs,
                                                        start=(m == 0), stop=(m == HID - 1))
                            if layer != 1:
                                last.then_inc(S[name("down_done")], 1)
                        if layer == 1:
                            pe.wait_ge(S[name("square_ready")], n(i, s, g))
                            for t in range(GROUP):
                                last = nc.tensor.matmul(bank(k, 4 + t)[:, 200:201], square[g][:, 0, t * P:(t + 1) * P],
                                                        const(k, "ones")[:, 0:1], start=True, stop=True)
                            last.then_inc(S[name("down_done")], 1)
            if layer == 1:
                pe.wait_ge(S[name("coef_ready")], 1)
                for f in two:
                    nc.tensor.transpose(bank(k, 0)[0:32, f * KH:(f + 1) * KH],
                                        fixed_t[:, f, :, :].rearrange("p j e -> p (j e)"), ident[0:KH, 0:KH])
                for t in range(TILES):
                    last = nc.tensor.transpose(banks(k, 1, 2)[0:48, t * P:(t + 1) * P], coef[:, t, :], ident)
                last.then_inc(S[name("combine_turned")], 1)
                pe.wait_ge(S[name("rows_loaded")], 16)
                pe.wait_ge(S[name("combine_t_ready")], 1)
                for t in range(TILES):
                    last = nc.tensor.matmul(halves[:, t, :], k.combine_t[0:48, t, :], k.expert_rows[0:48, :],
                                            start=True, stop=True)
                last.then_inc(S[name("rows_added")], 1)

        @block.scalar
        def _(act):
            if layer == 0:
                act.dma_start(k.expert_rows[0:8, :], io["l0_rows"]).then_inc(S[name("rows_loaded")], 16)
            if layer == 1:
                act.dma_start(k.expert_rows[32:48, :], io["l1_rows"]).then_inc(S[name("rows_loaded")], 16)
            if layer != 2:
                act.sem_inc(S[name("hid_ready")], RING)
            with act.Fori(0, E // 2) as i:
                for s in two:
                    act.wait_ge(S[name(f"w{s}_loaded")], i * 48 + 48)
                    if layer == 2:
                        for f in two:
                            last = nc.scalar.activation(w1[s][:, f, :], w1[s][:, f, :], ACT.Copy, scale=side[s][0:KH, f:f + 1])
                        last.then_inc(S[name("w1_scaled")], 1)
                    for g in two:
                        if layer == 2:
                            for j in range(HID):
                                act.wait_ge(S[name("up_done")], n(i, s, g, UP, 2 * j))
                                act.wait_ge(S[name("hid_ready")], n(i, s, g, HID, j))
                                nc.scalar.activation(silu[j % 2][:, :], bank(k, (2 * j) % 4), ACT.Silu).then_inc(S[name("silu_ready")], 1)
                        else:
                            act.wait_ge(S[name("down_done")], i * (4 * DOWN) + ((2 * s + g + 1) * DOWN + 1))
                            for m in range(UP):
                                b = m if layer == 1 else (UP * g + m) % 4
                                act.wait_ge(S[name("up_done")], n(i, s, g, UP, m))
                                nc.scalar.activation(hid[g][:, m, :], bank(k, b), ACT.Gelu,
                                                     bias=side[s][:, m:m + 1]).then_inc(S[name("hid_ready")], 1)

        @block.vector
        def _(dve):
            if layer == 0:
                dve.wait_ge(S[name("combine_turned")], 1)
                nc.vector.tensor_copy(k.combine_t[0:8, :, :].rearrange("p t c -> p (t c)"),
                                      banks(k, 0, 2)[0:8, :]).then_inc(S[name("combine_t_ready")], 1)
                dve.wait_ge(S[name("rows_added")], 1)
                nc.vector.tensor_copy(k.acc[:, :, :], halves).then_inc(S[name("acc_started")], 1)
            if layer == 1:
                nc.vector.memset(k.acc[:, :, :], 0.0).then_inc(S[name("acc_started")], 1)
                dve.sem_inc(S[name("fixed_read")], 1)
            if layer == 2:
                nc.vector.tensor_reduce(kept_sum[:, :], k.combine[:, :, 0:E], AX.X, ALU.add).then_inc(S[name("kept_summed")], 1)
                dve.wait_ge(S[name("kept_summed")], 1)
                nc.vector.tensor_tensor(k.acc[:, :, :], k.h[:, :, :], bcast(kept_sum[:, :].unsqueeze(2), [P, TILES, C]),
                                        ALU.mult).then_inc(S[name("acc_started")], 1)
                dve.sem_inc(S[name("hid_ready")], RING)
            dve.wait_ge(S[name("acc_started")], 1)
            dve.sem_inc(S[name("acc_done")], GROUP)
            with dve.Fori(0, E // 2) as i:
                for s in two:
                    expert = bass.ds(e(i, s, 0), 1)
                    if layer == 1:
                        dve.wait_ge(S[name("fixed_done")], e(i, s))
                        nc.vector.tensor_copy(fixed_t[:, :, :, expert].rearrange("p f j e -> p f (j e)"),
                                              bank(k, 3)[0:KH, 0:4].rearrange("p (f j) -> p f j", f=2)).then_inc(S[name("fixed_read")], 1)
                    for g in two:
                        if layer == 2:
                            dve.wait_ge(S[name("down_done")], i * (4 * DOWN) + ((2 * s + g + 1) * DOWN + 1))
                            for j in range(HID):
                                dve.wait_ge(S[name("silu_ready")], n(i, s, g, HID, j))
                                dve.wait_ge(S[name("up_done")], n(i, s, g, UP, 2 * j + 1))
                                nc.vector.tensor_tensor(hid[g][:, j, :], silu[j % 2][:, :], bank(k, (2 * j + 1) % 4),
                                                        ALU.mult).then_inc(S[name("hid_ready")], 1)
                        if layer == 1:
                            h, sq = hid[g], square[g]
                            step = lambda j: n(i, s, g, 5, j)
                            dve.wait_ge(S[name("hid_ready")], n(i, s, g, HID, HID - 1, RING))
                            nc.vector.tensor_tensor(sq[:, :, :], h[:, :, :], h[:, :, :], ALU.mult).then_inc(S[name("step")], 1)
                            dve.wait_ge(S[name("step")], step(0))
                            nc.vector.tensor_tensor(sq[:, 0, :], sq[:, 0, :], sq[:, 1, :], ALU.add).then_inc(S[name("step")], 1)
                            dve.wait_ge(S[name("step")], step(1))
                            nc.vector.tensor_tensor(sq[:, 0, :], sq[:, 0, :], sq[:, 2, :], ALU.add).then_inc(S[name("square_ready")], 1)
                            dve.wait_ge(S[name("down_done")], n(i, s, g, DOWN, 0, CREDIT))
                            column = lambda c: k.ps[:, 4:8, c:c + 1].rearrange("p t c -> p (t c)")
                            width = HID * P
                            nc.vector.tensor_scalar_mul(mean[:, :], column(C), 1.0 / width).then_inc(S[name("step")], 1)
                            dve.wait_ge(S[name("step")], step(2))
                            nc.vector.tensor_tensor(msq[:, :], mean[:, :], mean[:, :], ALU.mult).then_inc(S[name("step")], 1)
                            dve.wait_ge(S[name("step")], step(3))
                            nc.vector.scalar_tensor_tensor(out=msq[:, :], in0=column(200), scalar=1.0 / width, in1=msq[:, :],
                                                           op0=ALU.mult, op1=ALU.subtract).then_inc(S[name("step")], 1)
                            dve.wait_ge(S[name("step")], step(4))
                            nc.vector.tensor_scalar_add(vareps[:, :], msq[:, :], LN_EPS).then_inc(S[name("vareps_ready")], 1)
                            dve.wait_ge(S[name("rstd_ready")], n(i, s, g))
                            cw = k.combine[:, 4 * g:4 * g + 4, expert].rearrange("p t e -> p (t e)")
                            nc.vector.tensor_tensor(weight[:, :], rstd[:, :], cw, ALU.mult).then_inc(S[name("weight_ready")], 1)
                            dve.wait_ge(S[name("weight_ready")], n(i, s, g))
                            nc.vector.scalar_tensor_tensor(out=coef[:, 4 * g:4 * g + 4, expert].rearrange("p t e -> p (t e)"),
                                                           in0=weight[:, :], scalar=-1.0, in1=mean[:, :], op0=ALU.mult, op1=ALU.mult)
                        for t in range(GROUP):
                            if layer != 1:
                                dve.wait_ge(S[name("down_done")], n(i, s, g, DOWN, t, CREDIT))
                            acc = k.acc[:, 4 * g + t, :]
                            by = weight[:, t:t + 1] if layer == 1 else k.combine[:, 4 * g + t, expert]
                            nc.vector.scalar_tensor_tensor(out=acc, in0=bank(k, 4 + t)[:, 0:C], scalar=by, in1=acc,
                                                           op0=ALU.mult, op1=ALU.add).then_inc(S[name("acc_done")], 1)
            if layer == 1:
                nc.vector.tensor_copy(coef[:, :, 16:32], k.combine[:, :, :])
                nc.vector.tensor_copy(coef[:, :, 32:48], k.combine[:, :, :]).then_inc(S[name("coef_ready")], 1)
                dve.wait_ge(S[name("combine_turned")], 1)
                nc.vector.tensor_copy(k.expert_rows[0:32, :], bank(k, 0)[0:32, 0:C])
                nc.vector.tensor_copy(k.combine_t[:, :, :].rearrange("p t c -> p (t c)"),
                                      banks(k, 1, 2)[0:48, :]).then_inc(S[name("combine_t_ready")], 1)
                dve.wait_ge(S[name("rows_added")], 1)
                nc.vector.tensor_tensor(k.acc[:, :, :], k.acc[:, :, :], halves, ALU.add)


def rms_rows(nc, k):
    S = k.S
    with ExitStack() as own:
        sums = own.enter_context(nc.sbuf_tensor("rms_sums", [P, TILES], F32))
        rstd = own.enter_context(nc.sbuf_tensor("rms_rstd", [P, TILES], F32))
        block = own.enter_context(nc.Block())

        @block.gpsimd
        def _(pool):
            pool.wait_ge(S["rms_sums_ready"], 3)
            nc.gpsimd.tensor_tensor(rstd[:, :], sums[:, :], k.minus_half[:, 0:TILES], ALU.pow).then_inc(S["rms_rstd_ready"], 1)

        @block.vector
        def _(dve):
            nc.vector.tensor_tensor(k.rows[:, :, :], k.h[:, :, :], k.h[:, :, :], ALU.mult).then_inc(S["rms_sums_ready"], 1)
            dve.wait_ge(S["rms_sums_ready"], 1)
            nc.vector.tensor_reduce(sums[:, :], k.rows[:, :, :], AX.X, ALU.add).then_inc(S["rms_sums_ready"], 1)
            dve.wait_ge(S["rms_sums_ready"], 2)
            nc.vector.tensor_scalar(sums[:, :], sums[:, :], 4.0 / C, 1e-6, ALU.mult, ALU.add).then_inc(S["rms_sums_ready"], 1)
            dve.wait_ge(S["rms_rstd_ready"], 1)
            for t in range(TILES):
                nc.vector.tensor_scalar(k.rows[:, t, :], k.h[:, t, :], rstd[:, t:t + 1], 2.0, ALU.mult, ALU.mult)


def sent_experts(nc, k, io, layer):
    S = k.S
    M = MOES[f"l{layer}"]
    E, UP, HID = M["experts"], M["up"], M["hid"]
    W2 = HID * C + (C if layer == 0 else 0)
    RING = {0: 4, 2: 2}[layer]
    tag = f"l{layer}_"
    name = lambda x: "sent_" + x
    two = (0, 1)
    with ExitStack() as own:
        sb = lambda nm, shape: own.enter_context(nc.sbuf_tensor(tag + nm, shape, F32))
        w1 = [sb(f"w1_{s}", [KH, 2, UP * P]) for s in two]
        w2 = [sb(f"w2_{s}", [P, W2]) for s in two]
        side = [sb(f"side{s}", [P, 16]) for s in two]
        rows = [sb(f"rows{s}", [P, len(ROW_TILES), C]) for s in two]
        xt = [sb(f"xt{s}", [KH, 2, CAPACITY]) for s in two]
        hid = [sb(f"hid{s}", [P, HID, CAPACITY]) for s in two]
        out = [sb(f"out{s}", [P, len(ROW_TILES), C]) for s in two]
        silu = [sb(f"silu{b}", [P, CAPACITY]) for b in two] if layer == 2 else None
        block = own.enter_context(nc.Block())

        def n(what, i, s, each=1, j=0, credit=0):
            return i * (2 * each) + (S.at(name(what)) + s * each + j + 1 + credit)

        def in_pairs(eng, expert):
            with eng.Fori(0, E // 2 - 1) as i:
                expert(i, 0, True)
                expert(i, 1, True)
            expert(E // 2 - 1, 0, True)
            expert(E // 2 - 1, 1, False)

        def slots_of(t, i, s):
            part = t[0:SLOTS, :].rearrange("(e r) c -> e r c", r=CAPACITY)[bass.ds(i * 2 + s, 1), :, :]
            return (part[:, 0:2 * P, :].rearrange("e (j p) c -> p (e j) c", p=P),
                    part[:, 2 * P:CAPACITY, :].rearrange("e p c -> p (e c)"))

        @block.sync
        def _(sp):
            def load(i, s):
                at = bass.ds(i * 2 + s, 1)
                whole, rest = slots_of(k.sent, i, s)
                sp.dma_start(rows[s][:, 0:2, :], whole).then_inc(S[name(f"rows{s}_loaded")], 16)
                sp.dma_start(rows[s][0:ROW_TILES[2][1], 2, :], rest).then_inc(S[name(f"rows{s}_loaded")], 16)
                sp.dma_start(w1[s][:, :, :].rearrange("p f h -> p (f h)"),
                             io[tag + "w1"][at, :, :].rearrange("a p x -> p (a x)")).then_inc(S[name(f"w{s}_loaded")], 16)
                sp.dma_start(side[s][:, :], io[tag + "side"][at, :, :].rearrange("a p x -> p (a x)")).then_inc(S[name(f"w{s}_loaded")], 16)
                sp.dma_start(w2[s][:, :], io[tag + "w2"][at, :, :].rearrange("a p x -> p (a x)")).then_inc(S[name(f"w{s}_loaded")], 16)

            def expert(i, s, more):
                sp.wait_ge(S[name("out_ready")], n("out_ready", i, s, 3, 2, 2))
                whole, rest = slots_of(k.returned, i, s)
                sp.dma_start(whole, out[s][:, 0:2, :]).then_inc(S[name("out_stored")], 16)
                sp.dma_start(rest, out[s][0:ROW_TILES[2][1], 2, :]).then_inc(S[name("out_stored")], 16)
                if more:
                    load(i + 1, s)
                sp.wait_ge(S[name("out_stored")], n("out_stored", i, s, 32, 31))
                sp.sem_inc(S[name("out_free")], 1)

            load(0, 0)
            load(0, 1)
            sp.sem_inc(S[name("out_free")], 2)
            with sp.Fori(0, E // 2 - 1) as i:
                for s in two:
                    expert(i, s, True)
            for s in two:
                expert(E // 2 - 1, s, False)

        @block.tensor
        def _(pe):
            def turn_rows(i, s, first=False):
                pe.wait_ge(S[name(f"rows{s}_loaded")], n(f"rows{s}_loaded", i, 0, 16, 31))
                if not first:
                    pe.wait_ge(S[name("xt_ready")], n("xt_ready", i, s - 1))
                for j, (at, size) in enumerate(ROW_TILES):
                    for f in two:
                        last = nc.tensor.transpose(bank(k, 4 + f)[0:KH, at:at + size], rows[s][0:size, j, f * KH:(f + 1) * KH],
                                                   const(k, "ident")[0:size, 0:size])
                last.then_inc(S[name("rows_turned")], 1)

            def expert(i, s, more):
                pe.wait_ge(S[name("xt_ready")], n("xt_ready", i, s))
                pe.wait_ge(S[name(f"w{s}_loaded")], n(f"w{s}_loaded", i, 0, 24, 47))
                for m in range(UP):
                    if layer == 0:
                        pe.wait_ge(S[name("hid_ready")], n("hid_ready", i, s, HID, m))
                    elif m % 2 == 0:
                        pe.wait_ge(S[name("hid_ready")], n("hid_ready", i, s, HID, m // 2))
                    b = (UP * s + m) % 4
                    for f in two:
                        last = nc.tensor.matmul(bank(k, b)[:, 0:CAPACITY], w1[s][:, f, m * P:(m + 1) * P], xt[s][:, f, :],
                                                start=(f == 0), stop=(f == 1))
                    last.then_inc(S[name("up_done")], 1)
                if more:
                    turn_rows(i + s, 1 - s)
                for j, (at, size) in enumerate(ROW_TILES):
                    if j == 0:
                        pe.wait_ge(S[name("hid_ready")], n("hid_ready", i, s, HID, HID - 1, RING))
                    pe.wait_ge(S[name("out_ready")], n("out_ready", i, s, 3, j))
                    for m in range(HID):
                        last = nc.tensor.matmul(bank(k, 6 + (3 * s + j) % 2)[0:size, 0:C], hid[s][:, m, at:at + size],
                                                w2[s][:, m * C:(m + 1) * C], start=(m == 0), stop=(m == HID - 1))
                    last.then_inc(S[name("down_done")], 1)

            pe.sem_inc(S[name("down_done")], 2 * 3)
            turn_rows(0, 0, first=True)
            in_pairs(pe, expert)

        @block.scalar
        def _(act):
            if layer == 0:
                act.sem_inc(S[name("hid_ready")], RING)
            with act.Fori(0, E // 2) as i:
                for s in two:
                    act.wait_ge(S[name(f"w{s}_loaded")], n(f"w{s}_loaded", i, 0, 24, 47))
                    if layer == 0:
                        act.wait_ge(S[name("down_done")], n("down_done", i, s, 3, 2))
                        for m in range(UP):
                            act.wait_ge(S[name("up_done")], n("up_done", i, s, UP, m))
                            nc.scalar.activation(hid[s][:, m, :], bank(k, (UP * s + m) % 4)[:, 0:CAPACITY], ACT.Gelu,
                                                 bias=side[s][:, m:m + 1]).then_inc(S[name("hid_ready")], 1)
                    else:
                        for j in range(HID):
                            act.wait_ge(S[name("up_done")], n("up_done", i, s, UP, 2 * j))
                            act.wait_ge(S[name("hid_ready")], n("hid_ready", i, s, HID, j))
                            nc.scalar.activation(silu[j % 2][:, :], bank(k, (2 * j) % 4)[:, 0:CAPACITY],
                                                 ACT.Silu).then_inc(S[name("silu_ready")], 1)

        @block.vector
        def _(dve):
            def take_rows(i, s, first=False):
                dve.wait_ge(S[name("rows_turned")], n("rows_turned", i, s))
                for f in two:
                    src = bank(k, 4 + f)[0:KH, 0:CAPACITY]
                    if layer == 0:
                        last = nc.vector.tensor_scalar(xt[s][:, f, :], src, small(k, "ln2_w")[0:KH, f, :],
                                                       small(k, "ln2_b")[0:KH, f, :], ALU.mult, ALU.add)
                    else:
                        if f == 0:
                            dve.wait_ge(S[name(f"w{s}_loaded")], n(f"w{s}_loaded", i, 0, 24, 47))
                        last = nc.vector.tensor_scalar(xt[s][:, f, :], src, side[s][0:KH, f:f + 1], None, ALU.mult)
                last.then_inc(S[name("xt_ready")], 1)

            def expert(i, s, more):
                if layer == 2:
                    dve.wait_ge(S[name("down_done")], n("down_done", i, s, 3, 2))
                    for j in range(HID):
                        dve.wait_ge(S[name("silu_ready")], n("silu_ready", i, s, HID, j))
                        dve.wait_ge(S[name("up_done")], n("up_done", i, s, UP, 2 * j + 1))
                        nc.vector.tensor_tensor(hid[s][:, j, :], silu[j % 2][:, :], bank(k, (2 * j + 1) % 4)[:, 0:CAPACITY],
                                                ALU.mult).then_inc(S[name("hid_ready")], 1)
                if more:
                    take_rows(i + s, 1 - s)
                for j, (at, size) in enumerate(ROW_TILES):
                    dve.wait_ge(S[name("down_done")], n("down_done", i, s, 3, j, 6))
                    if j == 0:
                        dve.wait_ge(S[name("out_free")], n("out_free", i, s))
                    src = bank(k, 6 + (3 * s + j) % 2)[0:size, 0:C]
                    if layer == 0:
                        last = nc.vector.tensor_tensor(out[s][0:size, j, :], src, w2[s][0:size, HID * C:], ALU.add)
                    else:
                        last = nc.vector.tensor_copy(out[s][0:size, j, :], src)
                    last.then_inc(S[name("out_ready")], 1)

            if layer == 2:
                dve.sem_inc(S[name("hid_ready")], RING)
            dve.sem_inc(S[name("out_ready")], 2)
            take_rows(0, 0)
            in_pairs(dve, expert)
    counts = dict(up_done=UP * E, hid_ready=HID * E + RING, down_done=3 * E + 6, out_ready=3 * E + 2, out_stored=32 * E,
                  out_free=E + 2, rows_turned=E, xt_ready=E, silu_ready=HID * E if layer == 2 else 0,
                  w0_loaded=24 * E, w1_loaded=24 * E, rows0_loaded=16 * E, rows1_loaded=16 * E)
    S.passed(**{name(x): c for x, c in counts.items()})


def collect(nc, k):
    S = k.S
    two = (0, 1)
    with ExitStack() as own:
        came = [own.enter_context(nc.sbuf_tensor(f"came{c}_{S.at('rows_back0')}", [P, TILES, C], F32)) for c in two]
        block = own.enter_context(nc.Block())

        @block.gpsimd
        def _(pool):
            for t in range(TILES):
                for c in two:
                    nc.gpsimd.indirect_dma_start(came[c][:, t, :], None, k.returned,
                                                 bass.IndirectOffsetOnAxis(ap=k.back[:, c, t:t + 1], axis=0)).then_inc(S[f"rows_back{t}"], 16)
            for t in range(TILES):
                ln_power(nc, k, pool, t, "out_")

        @block.vector
        def _(dve):
            for t in range(TILES):
                acc = k.acc[:, t, :]
                dve.wait_ge(S[f"rows_back{t}"], S.at(f"rows_back{t}") + 32)
                for c in two:
                    nc.vector.scalar_tensor_tensor(out=acc, in0=came[c][:, t, :], scalar=k.share[:, c, t:t + 1], in1=acc,
                                                   op0=ALU.mult, op1=ALU.add).then_inc(S["y_ready"], 1)
                    dve.wait_ge(S["y_ready"], S.at("y_ready") + 2 * t + c + 1)
                ln_stats(nc, k, dve, acc, t, "out_")
                ln_apply(nc, k, dve, k.h[:, t, :], acc, t, "out_")
    S.passed(**dict.fromkeys(["out_" + x for x in LN_SIGNALS], TILES), y_ready=2 * TILES,
             **{f"rows_back{t}": 32 for t in range(TILES)})


def close(nc, k, layer, with_x1=False):
    S = k.S
    with ExitStack() as own:
        stats = own.enter_context(nc.sbuf_tensor(f"close{layer}_stats", [P, TILES, 6], F32))
        meanvar = own.enter_context(nc.sbuf_tensor(f"close{layer}_meanvar", [P, TILES, 2], F32))
        rstd = own.enter_context(nc.sbuf_tensor(f"close{layer}_rstd", [P, TILES], F32))
        vareps = own.enter_context(nc.sbuf_tensor(f"close{layer}_vareps", [P, TILES], F32))
        block = own.enter_context(nc.Block())

        @block.gpsimd
        def _(pool):
            pool.wait_ge(S["close_vareps"], S.at("close_vareps") + 1)
            nc.gpsimd.tensor_tensor(rstd[:, :], vareps[:, :], k.minus_half[:, 0:TILES], ALU.pow).then_inc(S["close_rstd"], 1)

        @block.vector
        def _(dve):
            at = [S.at("close_step")]

            def then(ins):
                at[0] += 1
                ins.then_inc(S["close_step"], 1)
                dve.wait_ge(S["close_step"], at[0])

            if with_x1:
                then(nc.vector.tensor_tensor(k.acc[:, :, :], k.acc[:, :, :], k.x1[:, :, :], ALU.add))
            then(nc.vector.tensor_tensor(k.acc[:, :, :], k.acc[:, :, :], k.h[:, :, :], ALU.add))
            for t in range(TILES):
                last = nc.vector.bn_stats(stats[:, t, :], k.acc[:, t, :])
            then(last)
            for t in range(TILES):
                last = nc.vector.bn_aggr(meanvar[:, t, :], stats[:, t, :])
            then(last)
            nc.vector.tensor_scalar_add(vareps[:, :], meanvar[:, :, 1], LN_EPS).then_inc(S["close_vareps"], 1)
            dve.wait_ge(S["close_rstd"], S.at("close_rstd") + 1)
            for t in range(TILES):
                nc.vector.tensor_scalar(k.h[:, t, :], k.acc[:, t, :], meanvar[:, t, 0:1], rstd[:, t:t + 1],
                                        ALU.subtract, ALU.mult)
            close.steps = at[0] - S.at("close_step")
    S.passed(close_vareps=1, close_rstd=1, close_step=close.steps)


def quantised(nc, k, io):
    S = k.S
    two = (0, 1)
    with ExitStack() as own:
        w_int = own.enter_context(nc.sbuf_tensor("w_int", [KH, 2, C], I32))
        wb = own.enter_context(nc.sbuf_tensor("wb", [KH, 2, C], BF16))
        xq = [own.enter_context(nc.sbuf_tensor(f"xq{u}", [KH, 2, P], BF16)) for u in two]
        block = own.enter_context(nc.Block())

        def n(name, i, u, each=1, j=0):
            return i * (2 * each) + (S.at(name) + u * each + j + 1)

        @block.sync
        def _(sp):
            sp.dma_start(w_int[:, :, :], io["l3_w"]).then_inc(S["w_int_loaded"], 16)
            out = io["out"].rearrange("(t p) c -> t p c", p=P)
            with sp.Fori(0, TILES // 2) as i:
                for u in two:
                    sp.wait_ge(S["result_ready"], n("result_ready", i, u))
                    sp.dma_start(out[bass.ds(i * 2 + u, 1), :, :].rearrange("a p c -> p (a c)"),
                                 k.acc[:, bass.ds(i * 2 + u, 1), :].rearrange("p a c -> p (a c)")).then_inc(S["stored"], 16)
            sp.wait_ge(S["stored"], 16 * TILES)

        @block.gpsimd
        def _(pool):
            with pool.Fori(0, TILES // 2) as i:
                for u in two:
                    ln_power(nc, k, pool, i * 2 + u, "out_")

        @block.tensor
        def _(pe):
            with pe.Fori(0, TILES // 2) as i:
                for u in two:
                    pe.wait_ge(S["x_ready"], n("x_ready", i, u))
                    for f in two:
                        last = nc.tensor.transpose(bank(k, 4 * u)[0:KH, f * P:(f + 1) * P],
                                                   k.xs[u][:, f * KH:(f + 1) * KH], const(k, "ident"))
                    last.then_inc(S["x_turned"], 1)
                for u in two:
                    pe.wait_ge(S["xq_ready"], n("xq_ready", i, u))
                    for f in two:
                        last = nc.tensor.matmul(bank(k, 4 * u + 1)[:, 0:C], xq[u][:, f, :], wb[:, f, :], start=(f == 0), stop=(f == 1))
                    last.then_inc(S["projected"], 1)

        @block.scalar
        def _(act):
            act.wait_ge(S["w_int_loaded"], 16)
            nc.scalar.activation(wb[:, :, :], w_int[:, :, :], ACT.Copy)
            with act.Fori(0, TILES // 2) as i:
                for u in two:
                    act.wait_ge(S["x_turned"], n("x_turned", i, u))
                    nc.scalar.activation(xq[u][:, :, :].rearrange("p f t -> p (f t)"), bank(k, 4 * u)[0:KH, 0:2 * P],
                                         ACT.Copy).then_inc(S["xq_ready"], 1)

        @block.vector
        def _(dve):
            with dve.Fori(0, TILES // 2) as i:
                for u in two:
                    nc.vector.tensor_scalar(k.xs[u][:, :], tile_of(k.h, i * 2 + u), float(1.0 / np.float32(0.02)), 127.0,
                                            ALU.mult, ALU.min).then_inc(S["scaled"], 1)
                for u in two:
                    dve.wait_ge(S["scaled"], n("scaled", i, u))
                    nc.vector.tensor_scalar(k.xs[u][:, :], k.xs[u][:, :], -128.0, ROUND, ALU.max, ALU.add).then_inc(S["rounded"], 1)
                for u in two:
                    dve.wait_ge(S["rounded"], n("rounded", i, u))
                    nc.vector.tensor_scalar_add(k.xs[u][:, :], k.xs[u][:, :], -ROUND).then_inc(S["x_ready"], 1)
                for u in two:
                    dve.wait_ge(S["projected"], n("projected", i, u))
                    nc.vector.scalar_tensor_tensor(out=k.ys[u][:, :], in0=bank(k, 4 * u + 1)[:, 0:C], scalar=float(np.float32(0.02 * 0.01)),
                                                   in1=const(k, "l3_bias"), op0=ALU.mult, op1=ALU.add).then_inc(S["masked"], 1)
                for u in two:
                    dve.wait_ge(S["masked"], n("masked", i, u))
                    nc.vector.tensor_tensor(k.ys[u][:, :], k.ys[u][:, :], tile_of(k.h, i * 2 + u), ALU.add).then_inc(S["y_ready"], 1)
                for u in two:
                    tile = i * 2 + u
                    dve.wait_ge(S["y_ready"], n("y_ready", i, u))
                    ln_stats(nc, k, dve, k.ys[u][:, :], tile, "out_")
                    ln_apply(nc, k, dve, tile_of(k.acc, tile), k.ys[u][:, :], tile, "out_").then_inc(S["result_ready"], 1)


def program(nc, io, until=99, dump=None):
    with ExitStack() as ctx:
        k = allocate(nc, ctx)
        load_constants(nc, k, io)
        embed(nc, k, io)
        allocate_experts(nc, k, ctx)
        with ExitStack() as actx:
            steps = [
                lambda: (allocate_attention(nc, k, actx), clear_attention(nc, k)),
                lambda: attention(nc, k, io, 0, "segments"),
                lambda: attention(nc, k, io, 1, "softmax", pre_ln="ln1", keep=True),
                lambda: (turn(nc, k, k.x1, k.ht, "ln2"), route(nc, k, 0), sent_experts(nc, k, io, 0), collect(nc, k)),
                lambda: attention(nc, k, io, 2, "softmax"),
                lambda: (turn(nc, k, k.h, k.ht), route(nc, k, 1), experts(nc, k, io, 1, k.ht), close(nc, k, 1)),
                lambda: (turn(nc, k, k.h, k.ht), gates(nc, k), attention(nc, k, io, 3, "linear", pre_ln="l2")),
                lambda: (turn(nc, k, k.h, k.ht), rms_rows(nc, k), route(nc, k, 2),
                         sent_experts(nc, k, io, 2), collect(nc, k)),
                lambda: attention(nc, k, io, 4, "rotary"),
                lambda: quantised(nc, k, io),
            ]
            for n, step in enumerate(steps):
                if n <= until:
                    step()
                if dump is not None and n == until:
                    dump(nc, k)


def _constants(inp):
    f = np.float32
    c = np.zeros((P, CONST_WIDTH), f)

    def put(name, a):
        at, w = CONST_AT[name]
        c[:, at:at + w] = a

    p = np.arange(P)
    t = p % PATCHES
    key = np.arange(PATCHES)
    put("ident", np.eye(P, dtype=f))
    put("fold64", (t[:, None] == key[None, :]).astype(f))
    put("fold128", (t[:, None] == t[None, :]).astype(f))
    put("earlier", (p[:, None] < p[None, :]).astype(f))
    put("ones", np.ones((P, P), f))
    causal = key[None, :] <= t[:, None]
    put("causal_add", np.where(causal, 0, MASKED).astype(f))
    put("causal01", causal.astype(f))
    put("tail01", (causal & (key[None, :] >= t[:, None] // SEG * SEG)).astype(f))
    ends = np.array([15, 31, 47, 63, 31, 63, 63, 0])
    put("seg_add", np.where(t[:, None] >= ends[None, :], 0, MASKED).astype(f))
    freqs = (f(1.0 / 1024.0) ** np.linspace(0, 1, HD // 4, dtype=f)).astype(f)
    theta = t[:, None].astype(f) * np.concatenate([freqs, np.zeros(HD // 4, f)])[None, :]
    put("cos", np.cos(theta).astype(f))
    put("sin", np.sin(theta).astype(f))
    put("nsin", -np.sin(theta).astype(f))
    put("iota", np.arange(16, dtype=f)[None, :])
    put("refused", (SLOTS + np.arange(16)[None, :] * P + p[:, None]).astype(f))
    put("bv", inp["L0_attn_bv"][None, :])
    put("mn_w", inp["L2_attn_mn_w"][None, :])
    put("mn_b", inp["L2_attn_mn_b"][None, :])
    put("temperature", inp["L2_attn_temperature"][None, :])
    put("l3_bias", inp["L3_ffn_bias"][None, :])
    put("wb2", inp["L2_attn_Wb2"].reshape(128, HEADS, 5).transpose(0, 2, 1).reshape(128, 60))
    return c


def _halves(w, bias=None):
    out = np.zeros((KH + 1, 2, w.shape[1]), np.float32)
    out[0:KH] = w.reshape(2, KH, -1).transpose(1, 0, 2)
    if bias is not None:
        out[KH, 1] = bias
    return out


def _layouts(inp):
    f = np.float32
    x = inp["x"].reshape(IMAGES, 3, 8, 16, 8, 16).transpose(1, 3, 5, 0, 2, 4)
    a = {"patches_t": x.reshape(KT_PATCH, P, TOKENS)}
    a["w_embed"] = inp["L0_tok_W"].T.reshape(KT_PATCH, P, C).transpose(1, 0, 2)
    a["const"] = _constants(inp)
    small = np.zeros((KH + 1, 2, SMALL_WIDTH), f)
    for name, w, b in (("gate0", inp["L0_ffn_w_g"], None), ("gate1", inp["L1_ffn_gate_w"], inp["L1_ffn_gate_b"]),
                       ("gate2", inp["L2_ffn_gate_w"].T, None), ("wb1", inp["L2_attn_Wb1"], None)):
        at, width = SMALL_AT[name]
        small[:, :, at:at + width] = _halves(w, b)
    for name, v in (("ln1_w", "L0_ffn_ln1_w"), ("ln1_b", "L0_ffn_ln1_b"), ("ln2_w", "L0_ffn_ln2_w"),
                    ("ln2_b", "L0_ffn_ln2_b"), ("l2_w", "L2_attn_ln_w"), ("l2_b", "L2_attn_ln_b")):
        at, _ = SMALL_AT[name]
        small[0:KH, :, at] = inp[v].reshape(2, KH).T
    a["small"] = small
    cat = np.concatenate
    z3, z = np.zeros(3 * C, f), np.zeros(C, f)
    a["wattn"] = np.stack([
        _halves(cat([inp["L0_attn_Wqkv"].T, inp["L0_attn_Wproj"].T], 1), cat([z3, z])),
        _halves(cat([inp["L0_ffn_attn_qkv_w"], inp["L0_ffn_attn_proj_w"]], 1),
                cat([inp["L0_ffn_attn_qkv_b"], inp["L0_ffn_attn_proj_b"]])),
        _halves(cat([inp[f"L1_attn_W{c}"].T for c in "qkvo"], 1), cat([inp[f"L1_attn_b{c}"] for c in "qkvo"])),
        _halves(cat([inp["L2_attn_Wqkv"], inp["L2_attn_Wproj"]], 1), cat([inp["L2_attn_bqkv"], inp["L2_attn_bproj"]])),
        _halves(cat([inp["L3_attn_qkv_w"][c].T for c in range(3)] + [inp["L3_attn_c_proj_w"].T], 1), cat([z3, z])),
    ])
    bil = np.zeros((PAIRS, HD, PAIRS, 256), f)
    wv = inp["L0_attn_Wv"].reshape(HD, HD, HD).transpose(1, 0, 2).reshape(HD, 256)
    for h in range(PAIRS):
        bil[h, :, h, :] = wv
    a["bil_w"] = bil.reshape(KH, PAIRS, 256)

    def up(w):
        e, _, n = w.shape
        return w.reshape(e, 2, KH, n).transpose(0, 2, 1, 3).reshape(e, KH, 2 * n)

    def down(w):
        e, h, _ = w.shape
        return w.reshape(e, h // P, P, C).transpose(0, 2, 1, 3).reshape(e, P, -1)

    def side(e, *cols):
        out = np.zeros((e, P, 16), f)
        for at, v in cols:
            out[:, 0:v.shape[1], at:at + v.shape[2]] = v
        return out

    tiles = lambda v: v.reshape(v.shape[0], -1, P).transpose(0, 2, 1)
    a["l0_w1"], a["l0_w2"] = up(inp["L0_ffn_exp_fc_w"]), cat([down(inp["L0_ffn_exp_proj_w"]),
                                                                       np.broadcast_to(inp["L0_ffn_exp_proj_b"], (8, P, C))], 2)
    a["l0_side"] = side(8, (0, tiles(inp["L0_ffn_exp_fc_b"][:, 0])))
    a["l1_w1"], a["l1_w2"] = up(inp["L1_ffn_fc1_w"]), down(inp["L1_ffn_fc2_w"])
    a["l1_side"] = side(16, (0, tiles(inp["L1_ffn_fc1_b"])), (4, tiles(inp["L1_ffn_ln_w"])), (7, tiles(inp["L1_ffn_ln_b"])))
    a["l1_rows"] = inp["L1_ffn_fc2_b"]
    w13 = inp["L2_ffn_w13"].transpose(0, 2, 1).reshape(8, C, 2, 4, P).transpose(0, 1, 3, 2, 4).reshape(8, C, 1024)
    a["l2_w1"], a["l2_w2"] = up(w13), down(inp["L2_ffn_w2"].transpose(0, 2, 1))
    a["l2_side"] = side(8, (0, inp["L2_ffn_norm_w"].reshape(8, 2, KH).transpose(0, 2, 1)))
    a["l3_w"] = inp["L3_ffn_weight_t"].reshape(2, KH, C).transpose(1, 0, 2)
    return {n: np.ascontiguousarray(v.astype(np.int32) if v.dtype.kind in "iu" else v) for n, v in a.items()}


def kernel(**inputs):
    import concourse.bacc as bacc
    from concourse.bass_utils import run_bass_kernel_spmd as run

    arrays = _layouts({n: np.asarray(v) for n, v in inputs.items()})
    nc = bacc.Bacc("TRN2", target_bir_lowering=False, num_devices=1)
    io = {n: nc.dram_tensor("in_" + n, v.shape, mybir.dt.from_np(v.dtype), kind="ExternalInput").ap()
          for n, v in arrays.items()}
    io["out"] = nc.dram_tensor("out", (TOKENS, C), F32, kind="ExternalOutput").ap()
    program(nc, io)
    r = run(nc, [{"in_" + n: v for n, v in arrays.items()}], core_ids=[0])
    return r.results[0]["out"].reshape(IMAGES, PATCHES, C)
```

```python
import math
from contextlib import ExitStack

import numpy as np
import concourse.bass as bass
from concourse import mybir

P = 128
IMAGES, PATCHES = 16, 64
TOKENS = IMAGES * PATCHES
TILES = TOKENS // P
ATTENTIONS = 5
C = 192
KH = C // 2
HEADS, HD = 12, 16
BLOCKS = 3
PAIRS = HEADS // 2
PATCH_IN = 768
KT_PATCH = PATCH_IN // P
BANK = 512
LN_EPS = 1e-5
MASKED = -1e30
ROUND = 1.5 * 2 ** 23
SEG = 16

F32 = mybir.dt.float32
BF16 = mybir.dt.bfloat16
I32 = mybir.dt.int32
U32 = mybir.dt.uint32
ALU = mybir.AluOpType
ACT = mybir.ActivationFunctionType
AX = mybir.AxisListType

CONST_COLS = [
    ("ident", 128), ("fold64", 64), ("fold128", 128), ("earlier", 128), ("ones", 128),
    ("causal_add", 64), ("causal01", 64), ("tail01", 64), ("seg_add", 8),
    ("cos", 8), ("sin", 8), ("nsin", 8), ("iota", 16), ("refused", 16), ("tile_start", 48),
    ("bv", 16), ("mn_w", 16), ("mn_b", 16), ("temperature", 1), ("l3_bias", C), ("wb2", 60),
]
CONST_AT = {}
_at = 0
for _n, _w in CONST_COLS:
    CONST_AT[_n] = (_at, _w)
    _at += _w
CONST_WIDTH = _at

SMALL_COLS = [("gate0", 8), ("gate1", 16), ("gate2", 8), ("wb1", 128),
              ("ln1_w", 1), ("ln1_b", 1), ("ln2_w", 1), ("ln2_b", 1), ("l2_w", 1), ("l2_b", 1)]
SMALL_AT = {}
_at = 0
for _n, _w in SMALL_COLS:
    SMALL_AT[_n] = (_at, _w)
    _at += _w
SMALL_WIDTH = _at

CAPACITY = TOKENS * 2 * 5 // (4 * 8)
SLOTS = 8 * CAPACITY
ROW_TILES = ((0, P), (P, P), (2 * P, CAPACITY - 2 * P))
CHOICES = 3
SORTED = TILES + (TOKENS * CHOICES + 15 * (P - 1)) // P
MOES = {
    "l0": dict(experts=8, up=6, hid=6, cap=CAPACITY),
    "l1": dict(experts=16, up=3, hid=3, cap=None),
    "l2": dict(experts=8, up=8, hid=4, cap=CAPACITY),
}


class Signals(dict):

    def __init__(self, nc, ctx):
        super().__init__()
        self.nc, self.ctx, self.start = nc, ctx, {}

    def __missing__(self, name):
        self[name] = self.ctx.enter_context(self.nc.semaphore(name))
        self.start[name] = 0
        return self[name]

    def at(self, name):
        self[name]
        return self.start[name]

    def passed(self, **counts):
        for name, n in counts.items():
            self.start[name] = self.at(name) + n


class Core:
    pass


def const(k, name):
    a, w = CONST_AT[name]
    return k.const[:, a:a + w]


def small(k, name):
    a, w = SMALL_AT[name]
    return k.small[:, :, a:a + w]


def bcast(ap, shape):
    return ap.to_broadcast(shape)


def allocate(nc, ctx):
    k = Core()
    k.nc = nc

    def sb(name, shape, dt=F32):
        return ctx.enter_context(nc.sbuf_tensor(name, shape, dt))

    k.S = Signals(nc, ctx)
    k.const = sb("const", [P, CONST_WIDTH])
    k.small = sb("small", [KH + 1, 2, SMALL_WIDTH])
    k.wattns = [sb(f"wattn{u}", [KH + 1, 2, 4 * C]) for u in (0, 1)]
    k.h = sb("h", [P, TILES, C])
    k.x1 = sb("x1", [P, TILES, C])
    k.ht = sb("ht", [KH + 1, 2, TOKENS])
    k.xs = [sb(f"xs{u}", [P, C]) for u in (0, 1)]
    k.ys = [sb(f"ys{u}", [P, C]) for u in (0, 1)]
    k.ln = {}
    for tag in ("in_", "out_"):
        b = k.ln[tag] = Core()
        b.stats, b.meanvar = sb(tag + "stats", [P, 6]), sb(tag + "meanvar", [P, 2])
        b.vareps, b.rstd, b.pause = sb(tag + "vareps", [P, 1]), sb(tag + "rstd", [P, 1]), sb(tag + "pause", [P, 1])
    k.zeros = sb("zeros", [P, C])
    k.sent = nc.dram_tensor("sent_rows", (max(SLOTS + 2 * TOKENS, SORTED * P), C), F32, kind="Internal").ap()
    k.returned = nc.dram_tensor("returned_rows", (max(SLOTS, SORTED * P), C), F32, kind="Internal").ap()
    k.minus_half = sb("minus_half", [P, 2 * HEADS])
    k.ps = ctx.enter_context(nc.psum_tensor("ps", [P, 8, BANK], F32))
    return k


def bank(k, b):
    return k.ps[:, b, :]


def banks(k, b, n):
    return k.ps[:, b:b + n, :].rearrange("p b c -> p (b c)")


def load_constants(nc, k, io):
    S = k.S
    with nc.Block() as block:
        @block.sync
        def _(sp):
            sp.dma_start(k.const[:, :], io["const"]).then_inc(S["const_loaded"], 16)
            sp.dma_start(k.small[:, :, :], io["small"]).then_inc(S["const_loaded"], 16)
            sp.dma_start(k.wattns[0][:, :, :], io["wattn"][0]).then_inc(S["wattn_loaded0"], 16)
            sp.wait_ge(S["const_loaded"], 32)

        @block.gpsimd
        def _(pool):
            nc.gpsimd.memset(k.minus_half[:, :], -0.5)
            nc.gpsimd.memset(k.zeros[:, :], 0.0)

        @block.vector
        def _(dve):
            nc.vector.memset(k.ht[KH:KH + 1, :, :], 1.0)


def embed(nc, k, io):
    S = k.S
    with ExitStack() as own:
        xt = own.enter_context(nc.sbuf_tensor("patches_t", [P, KT_PATCH, TOKENS], F32))
        w = own.enter_context(nc.sbuf_tensor("w_embed", [P, KT_PATCH, C], F32))
        block = own.enter_context(nc.Block())

        @block.sync
        def _(sp):
            sp.dma_start(w[:, :, :], io["w_embed"]).then_inc(S["w_embed_loaded"], 16)
            for kt in range(0, KT_PATCH, 2):
                sp.dma_start(xt[:, kt, :], io["patches_t"][kt]).then_inc(S[f"patches_loaded{kt}"], 16)

        @block.scalar
        def _(act):
            for kt in range(1, KT_PATCH, 2):
                act.dma_start(xt[:, kt, :], io["patches_t"][kt]).then_inc(S[f"patches_loaded{kt}"], 16)

        @block.tensor
        def _(pe):
            pe.wait_ge(S["w_embed_loaded"], 16)
            for kt in range(KT_PATCH):
                pe.wait_ge(S[f"patches_loaded{kt}"], 16)
                for t in range(TILES):
                    last = nc.tensor.matmul(bank(k, t)[:, 0:C], xt[:, kt, t * P:(t + 1) * P], w[:, kt, :],
                                            start=(kt == 0), stop=(kt == KT_PATCH - 1))
            last.then_inc(S["embedded"], 1)

        @block.vector
        def _(dve):
            dve.wait_ge(S["embedded"], 1)
            nc.vector.tensor_copy(k.h[:, :, :], k.ps[:, :, 0:C])


def ln_stats(nc, k, dve, row, tile, tag, eps=LN_EPS):
    S, b = k.S, k.ln[tag]
    nc.vector.bn_stats(b.stats[:, :], row).then_inc(S[tag + "stats_ready"], 1)
    dve.wait_ge(S[tag + "stats_ready"], tile + (S.at(tag + "stats_ready") + 1))
    nc.vector.memset(b.pause[:, :], 0.0)
    nc.vector.bn_aggr(b.meanvar[:, :], b.stats[:, :]).then_inc(S[tag + "meanvar_ready"], 1)
    dve.wait_ge(S[tag + "meanvar_ready"], tile + (S.at(tag + "meanvar_ready") + 1))
    nc.vector.tensor_scalar_add(b.vareps[:, :], b.meanvar[:, 1:2], eps).then_inc(S[tag + "vareps_ready"], 1)


def ln_power(nc, k, pool, tile, tag):
    S, b = k.S, k.ln[tag]
    pool.wait_ge(S[tag + "vareps_ready"], tile + (S.at(tag + "vareps_ready") + 1))
    nc.gpsimd.tensor_tensor(b.rstd[:, :], b.vareps[:, :], k.minus_half[:, 0:1], ALU.pow).then_inc(S[tag + "rstd_ready"], 1)


def ln_apply(nc, k, dve, dst, src, tile, tag):
    S, b = k.S, k.ln[tag]
    dve.wait_ge(S[tag + "rstd_ready"], tile + (S.at(tag + "rstd_ready") + 1))
    return nc.vector.tensor_scalar(dst, src, b.meanvar[:, 0:1], b.rstd[:, :], ALU.subtract, ALU.mult)


LN_SIGNALS = ("stats_ready", "meanvar_ready", "vareps_ready", "rstd_ready")


def tile_of(t, tile):
    return t[:, bass.ds(tile, 1), :].rearrange("p a c -> p (a c)")


def allocate_attention(nc, k, ctx, tag):
    def two(name, shape):
        return [ctx.enter_context(nc.sbuf_tensor(f"{tag}{name}{u}", shape, F32)) for u in (0, 1)]

    a = Core()
    a.xt = two("xt", [KH + 1, 2, P])
    a.qkv = two("qkv", [P, 3, C])
    a.wide = two("wide", [P, 3, HEADS, 2, HD])
    a.qt = two("qt", [P, BLOCKS, P])
    a.kt = two("kt", [P, BLOCKS, 4, PATCHES])
    a.vd = two("vd", [P, PAIRS, 2, 2, HD])
    a.sc = two("sc", [P, HEADS, PATCHES])
    a.pr = two("pr", [P, HEADS, PATCHES])
    a.prt = two("prt", [P, PAIRS, P])
    a.max = two("smax", [P, HEADS])
    a.sum = two("ssum", [P, HEADS])
    a.rsum = two("rsum", [P, HEADS])
    a.seg = two("seg", [P, HEADS, 8])
    a.segp = two("segp", [P, HEADS, 8])
    a.os = two("os", [P, HEADS, HD])
    a.ot = two("ot", [KH + 1, 2, P])
    a.t24 = two("t24", [P, 2 * HEADS])
    a.r24 = two("r24", [P, 2 * HEADS])
    a.tmp = two("tmp", [P, 2, HEADS, HD])
    a.tmp2 = two("tmp2", [P, 2, HEADS, HD])
    a.hs = two("hs", [P, HEADS])
    a.hsq = two("hsq", [P, HEADS, HD])
    a.gate1 = ctx.enter_context(nc.sbuf_tensor(tag + "gate1", [P, TILES, HEADS], F32))
    k.a = a


def clear_attention(nc, k, slots=False):
    a, S = k.a, k.S
    with nc.Block() as block:
        if slots:
            @block.sync
            def _(sp):
                rows = max(SLOTS // P, SORTED)
                sp.dma_start(k.sent[0:rows * P, :].rearrange("(p r) c -> p r c", r=rows),
                             bcast(k.zeros[:, :].unsqueeze(1), [P, rows, C])).then_inc(S["slots_cleared"], 16)

        @block.gpsimd
        def _(pool):
            for u in (0, 1):
                nc.gpsimd.memset(a.wide[u][:, :, :, :, :], 0.0)

        @block.vector
        def _(dve):
            for u in (0, 1):
                nc.vector.memset(a.kt[u][:, :, :, :], 0.0)
                nc.vector.memset(a.vd[u][:, :, :, :, :], 0.0)
                nc.vector.memset(a.xt[u][KH:KH + 1, :, :], 1.0)
                nc.vector.memset(a.ot[u][KH:KH + 1, :, :], 1.0)


def in_slots(eng, slot):
    slot(0, 0, True, False, False, True)
    slot(1, 1, True, True, False, True)
    with eng.Fori(0, TILES // 2 - 2) as i:
        slot(i * 2 + 2, 0, True, True, True, True)
        slot(i * 2 + 3, 1, True, True, True, True)
    slot(TILES - 2, 0, True, True, True, True)
    slot(TILES - 1, 1, True, True, True, False)
    slot(TILES, 0, False, True, True, False)
    slot(TILES + 1, 1, False, False, True, False)


def keep_awake(nc, k, products):
    for _ in range(products):
        nc.tensor.transpose(bank(k, 6)[:, 256:256 + P], const(k, "ident"), const(k, "ident"))


AWAKE_FIRST = 20
AWAKE = {"softmax": 0, "segments": 34, "rotary": 16, "linear": 16}


def attention(nc, k, io, layer, kind, pre_ln=None, keep=False, ahead=None):
    S, a = k.S, k.a
    scale = {"softmax": HD ** -0.5, "segments": HD ** -0.5, "rotary": 0.12, "linear": 1.0}[kind]
    raw = kind == "softmax"
    wattn = k.wattns[layer % 2]
    two = (0, 1)
    score_read = "p_ready" if kind == "linear" else "masked"
    weights_ready = "p_ready" if kind in ("linear", "segments") else "exped"
    scores = banks(k, 3, 2)[:, 0:HEADS * PATCHES]
    turned_p = banks(k, 5, 2)[:, 0:PAIRS * P]
    turned_x = bank(k, 4)[0:KH, 256:512]

    with ExitStack() as own:
        if kind == "segments":
            bil_w = own.enter_context(nc.sbuf_tensor("bil_w", [KH, PAIRS, 256], F32))
            kft = [own.enter_context(nc.sbuf_tensor(f"kft{u}", [KH, 2, P], F32)) for u in two]
            prod = [own.enter_context(nc.sbuf_tensor(f"prod{u}", [P, HEADS, HD, HD], F32)) for u in two]
        block = own.enter_context(nc.Block())

        def n(name, tile, each=1, more=0):
            return tile * each + (S.at(name) + more + 1)

        @block.sync
        def _(sp):
            if layer + 1 < ATTENTIONS:
                sp.dma_start(k.wattns[(layer + 1) % 2][:, :, :], io["wattn"][layer + 1]).then_inc(S[f"wattn_loaded{(layer + 1) % 2}"], 16)
            if ahead is not None:
                ahead(sp)
            if kind == "segments":
                sp.dma_start(bil_w[:, :, :], io["bil_w"]).then_inc(S["bil_w_loaded"], 16)

        @block.tensor
        def _(pe):
            pe.wait_ge(S[f"wattn_loaded{layer % 2}"], 16 * (layer // 2 + 1))
            if kind == "segments":
                pe.wait_ge(S["bil_w_loaded"], 16)
            ident = const(k, "ident")

            def score(s, u, in_a, in_b):
                if not in_b:
                    return
                tile, v = s - 1, 1 - u
                pe.wait_ge(S["qk_ready"], n("qk_ready", tile))
                if not (isinstance(tile, int) and tile == 0):
                    pe.wait_ge(S[score_read], n(score_read, tile - 1))
                for m in range(BLOCKS):
                    last = nc.tensor.matmul(scores[:, m * 256:(m + 1) * 256], a.qt[v][:, m, :],
                                            a.kt[v][:, m, :, :].rearrange("p h t -> p (h t)"),
                                            start=True, stop=True)
                last.then_inc(S["scored"], 1)

            def project_in(s, u, in_a, in_b):
                if not in_a:
                    return
                if not (isinstance(s, int) and s == 0):
                    pe.wait_ge(S["vd_ready"], n("vd_ready", s - 1))
                for c in range(3):
                    for f in two:
                        out = banks(k, 1, 2)[:, c * 256:c * 256 + C]
                        last = nc.tensor.matmul(out, a.xt[u][0:KH + f, f, :],
                                                wattn[0:KH + f, f, c * C:(c + 1) * C],
                                                start=(f == 0), stop=(f == 1))
                last.then_inc(S["qkv_projected"], 1)

            def turn_out(s, u):
                pe.wait_ge(S["os_ready"], n("os_ready", s - 2))
                os = a.os[u][:, :, :].rearrange("p h d -> p (h d)")
                for f in two:
                    last = nc.tensor.transpose(bank(k, 5)[0:KH, f * P:(f + 1) * P],
                                               os[:, f * KH:(f + 1) * KH], ident)
                last.then_inc(S["o_turned"], 1)

            def project_out(s, u):
                pe.wait_ge(S["ot_ready"], n("ot_ready", s - 2))
                for f in two:
                    last = nc.tensor.matmul(bank(k, 5)[:, 256:256 + C], a.ot[u][0:KH + f, f, :],
                                            wattn[0:KH + f, f, 3 * C:4 * C], start=(f == 0), stop=(f == 1))
                last.then_inc(S["projected"], 1)

            def slot(s, u, in_a, in_b, in_c, in_x):
                if in_a:
                    pe.wait_ge(S["x_ready"], n("x_ready", s))
                    for f in two:
                        last = nc.tensor.transpose(turned_x[:, f * P:(f + 1) * P],
                                                   k.xs[u][:, f * KH:(f + 1) * KH], ident)
                    last.then_inc(S["x_turned"], 1)
                if in_c:
                    tile = s - 2
                    pe.wait_ge(S[weights_ready], n(weights_ready, tile))
                    if not (isinstance(tile, int) and tile == 0):
                        pe.wait_ge(S["y_ready"], n("y_ready", tile - 1))
                    for p in range(PAIRS):
                        last = nc.tensor.transpose(turned_p[:, p * P:(p + 1) * P],
                                                   a.pr[u][:, 2 * p:2 * p + 2, :].rearrange("p h t -> p (h t)"), ident)
                    last.then_inc(S["p_turned"], 1)
                if in_a:
                    pe.wait_ge(S["xt_ready"], n("xt_ready", s))
                score(s, u, in_a, in_b)
                project_in(s, u, in_a, in_b)
                if in_c:
                    pe.wait_ge(S["prt_ready"], n("prt_ready", s - 2))
                    for p in range(PAIRS):
                        last = nc.tensor.matmul(bank(k, 7)[:, p * 64:(p + 1) * 64], a.prt[u][:, p, :],
                                                a.vd[u][:, p, :, :, :].rearrange("p a b d -> p (a b d)"),
                                                start=True, stop=True)
                    last.then_inc(S["mixed"], 1)
                if in_c and kind not in ("linear", "segments"):
                    if in_a and kind == "rotary":
                        keep_awake(nc, k, AWAKE[kind])
                    turn_out(s, u)
                if in_a and kind == "segments":
                    pe.wait_ge(S["qkv_ready"], n("qkv_ready", s))
                    for f in two:
                        last = nc.tensor.transpose(bank(k, 0)[0:KH, f * P:(f + 1) * P],
                                                   a.qkv[u][:, 1, f * KH:(f + 1) * KH], ident)
                    last.then_inc(S["k_turned"], 1)
                if in_c and kind == "segments":
                    turn_out(s, u)
                if in_a and kind == "segments":
                    pe.wait_ge(S["kft_ready"], n("kft_ready", s))
                    for c in range(6):
                        if c >= 3:
                            pe.wait_ge(S["bil_used"], n("bil_used", s, 6, c - 3))
                        nc.tensor.matmul(bank(k, c % 3), kft[u][:, c // 3, :],
                                         bil_w[:, 2 * (c % 3):2 * (c % 3) + 2, :].rearrange("p a b -> p (a b)"),
                                         start=True, stop=True).then_inc(S["bil_ready"], 1)
                if in_c and kind != "linear":
                    project_out(s, u)
                if in_a:
                    if kind != "rotary":
                        keep_awake(nc, k, AWAKE[kind])
                    pe.wait_ge(S["wide_ready"], n("wide_ready", s))
                    if kind == "segments":
                        pe.wait_ge(S["qk_spread"], n("qk_spread", s))
                    wide = a.wide[u][:, :, :, :, :].rearrange("p c h b d -> p c (h b d)")
                    for m in range(BLOCKS):
                        nc.tensor.transpose(bank(k, 0)[:, m * P:(m + 1) * P],
                                            wide[:, 0, m * P:(m + 1) * P], ident)
                    for m in range(BLOCKS):
                        nc.tensor.matmul(bank(k, 1)[:, m * PATCHES:(m + 1) * PATCHES],
                                         wide[:, 1, m * P:(m + 1) * P], const(k, "fold64"),
                                         start=True, stop=True)
                    nc.tensor.matmul(bank(k, 2)[:, 0:2 * C], const(k, "fold128"), wide[:, 2, :],
                                     start=True, stop=True).then_inc(S["folded"], 1)
                if in_c and kind == "linear":
                    turn_out(s, u)
                    project_out(s, u)

            keep_awake(nc, k, AWAKE_FIRST)
            in_slots(pe, slot)

        @block.scalar
        def _(act):
            def take_qk(s, u):
                act.wait_ge(S["folded"], n("folded", s))
                nc.scalar.activation(a.qt[u][:, :, :].rearrange("p m t -> p (m t)"), bank(k, 0)[:, 0:3 * P], ACT.Copy)
                for j in range(4):
                    r = slice(32 * j, 32 * j + 32)
                    last = nc.scalar.activation(a.kt[u][r, :, j, :],
                                                bank(k, 1)[r, 0:BLOCKS * PATCHES].rearrange("p (m t) -> p m t", m=BLOCKS),
                                                ACT.Copy)
                last.then_inc(S["qk_ready"], 1)

            def slot(s, u, in_a, in_b, in_c, in_x):
                if in_a:
                    act.wait_ge(S["x_turned"], n("x_turned", s))
                    if pre_ln:
                        for f in two:
                            last = nc.scalar.activation(a.xt[u][0:KH, f, :], turned_x[:, f * P:(f + 1) * P],
                                                        ACT.Identity, scale=small(k, pre_ln + "_w")[0:KH, f, :],
                                                        bias=small(k, pre_ln + "_b")[0:KH, f, :])
                    else:
                        last = nc.scalar.activation(a.xt[u][0:KH, :, :].rearrange("p f t -> p (f t)"), turned_x, ACT.Copy)
                    last.then_inc(S["xt_ready"], 1)
                if in_c:
                    act.wait_ge(S["p_turned"], n("p_turned", s - 2))
                    nc.scalar.activation(a.prt[u][:, :, :].rearrange("p a t -> p (a t)"), turned_p,
                                         ACT.Copy).then_inc(S["prt_ready"], 1)
                if in_a:
                    act.wait_ge(S["qkv_projected"], n("qkv_projected", s))
                    src = k.ps[:, 1:3, :].rearrange("p b (c x) -> p (b c) x", c=2)
                    if raw:
                        for b in two:
                            r = slice(64 * b, 64 * b + 64)
                            last = nc.scalar.activation(a.wide[u][r, :, :, b, :],
                                                        src[r, 0:3, 0:C].rearrange("p c (h d) -> p c h d", d=HD), ACT.Copy)
                        last.then_inc(S["wide_ready"], 1)
                    else:
                        nc.scalar.activation(a.qkv[u][:, :, :], src[:, 0:3, 0:C], ACT.Copy).then_inc(S["qkv_ready"], 1)
                    if kind == "segments":
                        act.wait_ge(S["k_turned"], n("k_turned", s))
                        nc.scalar.activation(kft[u][:, :, :].rearrange("p f t -> p (f t)"), bank(k, 0)[0:KH, 0:2 * P],
                                             ACT.Copy).then_inc(S["kft_ready"], 1)
                        for b in two:
                            r = slice(64 * b, 64 * b + 64)
                            last = nc.scalar.activation(a.wide[u][r, 0:2, :, b, :],
                                                        a.qkv[u][r, 0:2, :].rearrange("p c (h d) -> p c h d", d=HD), ACT.Copy)
                        last.then_inc(S["qk_spread"], 1)
                    if kind == "linear":
                        act.wait_ge(S["clipped"], n("clipped", s))
                        nc.scalar.activation(a.tmp2[u][:, :, :, :], a.tmp[u][:, :, :, :], ACT.Exp).then_inc(S["elu_exp"], 1)
                if in_b and kind != "linear":
                    act.wait_ge(S["centred"], n("centred", s - 1))
                    src, dst = (a.seg, a.segp) if kind == "segments" else (a.sc, a.pr)
                    nc.scalar.activation(dst[1 - u][:, :, :], src[1 - u][:, :, :], ACT.Exp, scale=scale).then_inc(S["exped"], 1)
                if in_a and kind == "linear":
                    take_qk(s, u)
                if in_c:
                    act.wait_ge(S["o_turned"], n("o_turned", s - 2))
                    nc.scalar.activation(a.ot[u][0:KH, :, :].rearrange("p f t -> p (f t)"), bank(k, 5)[0:KH, 0:2 * P],
                                         ACT.Copy).then_inc(S["ot_ready"], 1)
                if in_a and kind != "linear":
                    take_qk(s, u)

            in_slots(act, slot)

        @block.gpsimd
        def _(pool):
            def slot(s, u, in_a, in_b, in_c, in_x):
                if in_b and kind != "linear":
                    pool.wait_ge(S["max_ready"], n("max_ready", s - 1))
                    t, w = (a.seg, 8) if kind == "segments" else (a.sc, PATCHES)
                    nc.gpsimd.tensor_tensor(t[1 - u][:, :, :], t[1 - u][:, :, :],
                                            bcast(a.max[1 - u][:, :].unsqueeze(2), [P, HEADS, w]),
                                            ALU.subtract).then_inc(S["centred"], 1)
                if in_b and kind == "segments":
                    pool.wait_ge(S["exped"], n("exped", s - 1))
                    nc.gpsimd.tensor_tensor(a.sc[1 - u][:, :, :], bcast(const(k, "tail01").unsqueeze(1), [P, HEADS, PATCHES]),
                                            bcast(a.segp[1 - u][:, :, 7:8], [P, HEADS, PATCHES]),
                                            ALU.mult).then_inc(S["tail_ready"], 1)
                if in_a and kind == "rotary":
                    pool.wait_ge(S["ms_ready"], n("ms_ready", s))
                    nc.gpsimd.tensor_tensor(a.r24[u][:, :], a.t24[u][:, :], k.minus_half[:, :], ALU.pow).then_inc(S["rms_ready"], 1)
                if in_c and kind == "linear":
                    pool.wait_ge(S["hvar_ready"], n("hvar_ready", s - 2))
                    nc.gpsimd.tensor_tensor(a.r24[u][:, 0:HEADS], a.t24[u][:, 0:HEADS], k.minus_half[:, 0:HEADS],
                                            ALU.pow).then_inc(S["hrstd_ready"], 1)
                if in_x and pre_ln:
                    ln_power(nc, k, pool, s + 1, "in_")
                if in_c and not keep:
                    ln_power(nc, k, pool, s - 2, "out_")

            if pre_ln:
                ln_power(nc, k, pool, 0, "in_")
            in_slots(pool, slot)

        @block.vector
        def _(dve):
            every = [P, HEADS, PATCHES]
            heads = [P, HEADS, HD]
            score = scores.rearrange("p (h t) -> p h t", t=PATCHES)

            def input_rows(s, u):
                if pre_ln:
                    ln_stats(nc, k, dve, tile_of(k.h, s), s, "in_")
                    ln_apply(nc, k, dve, k.xs[u][:, :], tile_of(k.h, s), s, "in_").then_inc(S["x_ready"], 1)
                else:
                    nc.vector.tensor_copy(k.xs[u][:, :], tile_of(k.h, s)).then_inc(S["x_ready"], 1)

            def bilinear_values(s, u):
                dve.wait_ge(S["qkv_ready"], n("qkv_ready", s))
                for c in range(6):
                    dve.wait_ge(S["bil_ready"], n("bil_ready", s, 6, c))
                    v0 = a.qkv[u][:, 2, 32 * c:32 * c + 32].rearrange("p (h d) -> p h d", h=2)
                    nc.vector.tensor_tensor(
                        prod[u][:, 2 * c:2 * c + 2, :, :], bank(k, c % 3).rearrange("p (h e j) -> p h e j", h=2, e=HD),
                        bcast(v0.unsqueeze(2), [P, 2, HD, HD]), ALU.mult).then_inc(S["bil_used"], 1)
                dve.wait_ge(S["bil_used"], n("bil_used", s, 6, 5))
                nc.vector.tensor_reduce(a.tmp[u][:, 0, :, :].rearrange("p h e -> p (h e)"),
                                        prod[u][:, :, :, :].rearrange("p h e j -> p (h e) j"),
                                        AX.X, ALU.add).then_inc(S["v_summed"], 1)
                dve.wait_ge(S["v_summed"], n("v_summed", s))
                for b in two:
                    r = slice(64 * b, 64 * b + 64)
                    last = nc.vector.tensor_tensor(a.wide[u][r, 2, :, b, :], a.tmp[u][r, 0, :, :],
                                            bcast(const(k, "bv")[r, :].unsqueeze(1), [64, HEADS, HD]), ALU.add)
                last.then_inc(S["wide_ready"], 1)

            def positive_keys(s, u):
                dve.wait_ge(S["qkv_ready"], n("qkv_ready", s))
                nc.vector.tensor_scalar_min(a.tmp[u][:, :, :, :].rearrange("p c h d -> p (c h d)"),
                                            a.qkv[u][:, 0:2, :].rearrange("p c x -> p (c x)"), 0.0).then_inc(S["clipped"], 1)
                g = tile_of(a.gate1, s)
                for b in two:
                    r = slice(64 * b, 64 * b + 64)
                    nc.vector.tensor_tensor(a.wide[u][r, 2, :, b, :], a.qkv[u][r, 2, :].rearrange("p (h d) -> p h d", d=HD),
                                            bcast(g[r, :].unsqueeze(2), [64, HEADS, HD]), ALU.mult)

            def positive_keys_spread(s, u):
                dve.wait_ge(S["elu_exp"], n("elu_exp", s))
                for b in two:
                    r = slice(64 * b, 64 * b + 64)
                    for c in two:
                        last = nc.vector.scalar_tensor_tensor(
                            out=a.wide[u][r, c, :, b, :], in0=a.qkv[u][r, c, :].rearrange("p (h d) -> p h d", d=HD),
                            scalar=0.0, in1=a.tmp2[u][r, c, :, :], op0=ALU.max, op1=ALU.add)
                last.then_inc(S["wide_ready"], 1)

            def rotated_keys(s, u):
                dve.wait_ge(S["qkv_ready"], n("qkv_ready", s))
                qk = a.qkv[u][:, 0:2, :].rearrange("p c x -> p (c x)")
                x = a.tmp[u][:, :, :, :].rearrange("p c h d -> p (c h) d")
                y = a.tmp2[u][:, :, :, :].rearrange("p c h d -> p (c h) d")
                nc.vector.tensor_tensor(x.rearrange("p h d -> p (h d)"), qk, qk, ALU.mult).then_inc(S["squared"], 1)
                dve.wait_ge(S["squared"], n("squared", s))
                nc.vector.tensor_reduce(a.r24[u][:, :], x, AX.X, ALU.add).then_inc(S["square_sums"], 1)
                dve.wait_ge(S["square_sums"], n("square_sums", s))
                nc.vector.tensor_scalar(a.t24[u][:, :], a.r24[u][:, :], 1.0 / HD, 1.1920928955078125e-07,
                                        ALU.mult, ALU.add).then_inc(S["ms_ready"], 1)
                for b in two:
                    r = slice(64 * b, 64 * b + 64)
                    nc.vector.tensor_copy(a.wide[u][r, 2, :, b, :], a.qkv[u][r, 2, :].rearrange("p (h d) -> p h d", d=HD))

            def rotated_keys_turn(s, u):
                x = a.tmp[u][:, :, :, :].rearrange("p c h d -> p (c h) d")
                y = a.tmp2[u][:, :, :, :].rearrange("p c h d -> p (c h) d")
                half = [P, 2 * HEADS, HD // 2]
                raw_x = a.qkv[u][:, 0:2, :].rearrange("p c (h d) -> p (c h) d", d=HD)
                nc.vector.tensor_tensor(y[:, :, 0:8], raw_x[:, :, 8:16], bcast(const(k, "sin").unsqueeze(1), half), ALU.mult)
                nc.vector.tensor_tensor(y[:, :, 8:16], raw_x[:, :, 0:8], bcast(const(k, "nsin").unsqueeze(1), half), ALU.mult)
                nc.vector.tensor_tensor(a.tmp[u][:, :, :, :].rearrange("p c h (s d) -> p (c h s) d", s=2),
                                        a.qkv[u][:, 0:2, :].rearrange("p c (h s d) -> p (c h s) d", s=2, d=HD // 2),
                                        bcast(const(k, "cos").unsqueeze(1), [P, 4 * HEADS, HD // 2]), ALU.mult).then_inc(S["cosined"], 1)
                dve.wait_ge(S["cosined"], n("cosined", s))
                nc.vector.tensor_tensor(x, x, y, ALU.add).then_inc(S["turned_by_angle"], 1)

            def rotated_keys_spread(s, u):
                dve.wait_ge(S["rms_ready"], n("rms_ready", s))
                dve.wait_ge(S["turned_by_angle"], n("turned_by_angle", s))
                r24 = a.r24[u][:, :].rearrange("p (c h) -> p c h", c=2).unsqueeze(3)
                for b in two:
                    r = slice(64 * b, 64 * b + 64)
                    last = nc.vector.tensor_tensor(a.wide[u][r, 0:2, :, b, :], a.tmp[u][r, :, :, :],
                                                   bcast(r24[r], [64, 2, HEADS, HD]), ALU.mult)
                last.then_inc(S["wide_ready"], 1)

            def masked_maximum(s, u):
                dve.wait_ge(S["scored"], n("scored", s))
                if kind in ("softmax", "rotary"):
                    nc.vector.tensor_tensor(a.sc[u][:, :, :], score, bcast(const(k, "causal_add").unsqueeze(1), every),
                                            ALU.add).then_inc(S["masked"], 1)
                    dve.wait_ge(S["masked"], n("masked", s))
                    nc.vector.tensor_reduce(a.max[u][:, :], a.sc[u][:, :, :], AX.X, ALU.max).then_inc(S["max_ready"], 1)
                if kind == "linear":
                    nc.vector.tensor_tensor(a.pr[u][:, :, :], score, bcast(const(k, "causal01").unsqueeze(1), every),
                                            ALU.mult).then_inc(S["p_ready"], 1)
                if kind == "segments":
                    nc.vector.tensor_reduce(a.seg[u][:, :, 0:4], score.rearrange("p h (s t) -> p h s t", t=SEG),
                                            AX.X, ALU.add).then_inc(S["seg16"], 1)
                    nc.vector.tensor_tensor(a.sc[u][:, :, :], score, bcast(const(k, "tail01").unsqueeze(1), every),
                                            ALU.mult).then_inc(S["masked"], 1)
                    dve.wait_ge(S["seg16"], n("seg16", s))
                    pairs = a.seg[u][:, :, 0:4].rearrange("p h (s t) -> p h s t", t=2)
                    nc.vector.tensor_tensor(a.seg[u][:, :, 4:6], pairs[:, :, :, 0], pairs[:, :, :, 1],
                                            ALU.add).then_inc(S["seg32"], 1)
                    dve.wait_ge(S["masked"], n("masked", s))
                    nc.vector.tensor_reduce(a.seg[u][:, :, 7:8], a.sc[u][:, :, :], AX.X, ALU.add)
                    dve.wait_ge(S["seg32"], n("seg32", s))
                    nc.vector.tensor_tensor(a.seg[u][:, :, 6:7], a.seg[u][:, :, 4:5], a.seg[u][:, :, 5:6],
                                            ALU.add).then_inc(S["seg64"], 1)
                    dve.wait_ge(S["seg64"], n("seg64", s))
                    nc.vector.tensor_tensor(a.seg[u][:, :, :], a.seg[u][:, :, :],
                                            bcast(const(k, "seg_add").unsqueeze(1), [P, HEADS, 8]), ALU.add).then_inc(S["seg_masked"], 1)
                    dve.wait_ge(S["seg_masked"], n("seg_masked", s))
                    nc.vector.tensor_reduce(a.max[u][:, :], a.seg[u][:, :, :], AX.X, ALU.max).then_inc(S["max_ready"], 1)

            def weights(s, u):
                if kind in ("softmax", "rotary"):
                    dve.wait_ge(S["exped"], n("exped", s))
                    nc.vector.tensor_reduce(a.sum[u][:, :], a.pr[u][:, :, :], AX.X, ALU.add).then_inc(S["sum_ready"], 1)
                    dve.wait_ge(S["sum_ready"], n("sum_ready", s))
                    nc.vector.reciprocal(a.rsum[u][:, :], a.sum[u][:, :]).then_inc(S["rsum_ready"], 1)
                if kind == "linear":
                    dve.wait_ge(S["p_ready"], n("p_ready", s))
                    nc.vector.tensor_reduce(a.sum[u][:, :], a.pr[u][:, :, :], AX.X, ALU.add).then_inc(S["sum_ready"], 1)
                    dve.wait_ge(S["sum_ready"], n("sum_ready", s))
                    nc.vector.tensor_scalar_add(a.max[u][:, :], a.sum[u][:, :], 1e-6).then_inc(S["max_ready"], 1)
                    dve.wait_ge(S["max_ready"], n("max_ready", s))
                    nc.vector.reciprocal(a.rsum[u][:, :], a.max[u][:, :]).then_inc(S["rsum_ready"], 1)
                if kind == "segments":
                    dve.wait_ge(S["exped"], n("exped", s))
                    w4 = a.seg[u][:, :, 0:4].rearrange("p h (s t) -> p h s t", t=2)
                    nc.vector.tensor_tensor(w4, a.segp[u][:, :, 0:4].rearrange("p h (s t) -> p h s t", t=2),
                                            bcast(a.segp[u][:, :, 4:6].unsqueeze(3), [P, HEADS, 2, 2]), ALU.add).then_inc(S["w32"], 1)
                    dve.wait_ge(S["w32"], n("w32", s))
                    nc.vector.tensor_tensor(a.seg[u][:, :, 0:4], a.seg[u][:, :, 0:4],
                                            bcast(a.segp[u][:, :, 6:7], [P, HEADS, 4]), ALU.add).then_inc(S["w64"], 1)
                    nc.vector.tensor_reduce(a.sum[u][:, :], a.segp[u][:, :, :], AX.X, ALU.add).then_inc(S["sum_ready"], 1)
                    dve.wait_ge(S["w64"], n("w64", s))
                    dve.wait_ge(S["tail_ready"], n("tail_ready", s))
                    nc.vector.tensor_tensor(a.pr[u][:, :, :].rearrange("p h (s t) -> p h s t", t=SEG),
                                            a.sc[u][:, :, :].rearrange("p h (s t) -> p h s t", t=SEG),
                                            bcast(a.seg[u][:, :, 0:4].unsqueeze(3), [P, HEADS, 4, SEG]),
                                            ALU.add).then_inc(S["p_ready"], 1)
                    dve.wait_ge(S["sum_ready"], n("sum_ready", s))
                    nc.vector.reciprocal(a.rsum[u][:, :], a.sum[u][:, :]).then_inc(S["rsum_ready"], 1)

            def normalised(s, u):
                dve.wait_ge(S["rsum_ready"], n("rsum_ready", s))
                dve.wait_ge(S["mixed"], n("mixed", s))
                o = bank(k, 7)[:, 0:2 * C].rearrange("p (h b d) -> p h b d", b=2, d=HD)
                for b in two:
                    r = slice(64 * b, 64 * b + 64)
                    last = nc.vector.tensor_tensor(a.os[u][r, :, :], o[r, :, b, :],
                                                   bcast(a.rsum[u][r, :].unsqueeze(2), [64, HEADS, HD]), ALU.mult)
                last.then_inc(S["o_scaled" if kind == "linear" else "os_ready"], 1)
                if kind == "linear":
                    dve.wait_ge(S["o_scaled"], n("o_scaled", s))
                    nc.vector.tensor_reduce(a.hs[u][:, :], a.os[u][:, :, :], AX.X, ALU.add).then_inc(S["hsum"], 1)
                    dve.wait_ge(S["hsum"], n("hsum", s))
                    nc.vector.scalar_tensor_tensor(out=a.os[u][:, :, :], in0=a.os[u][:, :, :], scalar=float(HD),
                                                   in1=bcast(a.hs[u][:, :].unsqueeze(2), heads),
                                                   op0=ALU.mult, op1=ALU.subtract).then_inc(S["hcentred"], 1)
                    dve.wait_ge(S["hcentred"], n("hcentred", s))
                    nc.vector.tensor_tensor(a.hsq[u][:, :, :], a.os[u][:, :, :], a.os[u][:, :, :],
                                            ALU.mult).then_inc(S["hsquared"], 1)
                    dve.wait_ge(S["hsquared"], n("hsquared", s))
                    nc.vector.tensor_reduce(a.hs[u][:, :], a.hsq[u][:, :, :], AX.X, ALU.add).then_inc(S["hsqsum"], 1)
                    dve.wait_ge(S["hsqsum"], n("hsqsum", s))
                    nc.vector.tensor_scalar(a.t24[u][:, 0:HEADS], a.hs[u][:, :], 1.0 / HD, LN_EPS * HD * HD,
                                            ALU.mult, ALU.add).then_inc(S["hvar_ready"], 1)

            def normalised_heads(s, u):
                if kind == "linear":
                    dve.wait_ge(S["hrstd_ready"], n("hrstd_ready", s))
                    nc.vector.tensor_tensor(a.os[u][:, :, :], a.os[u][:, :, :],
                                            bcast(a.r24[u][:, 0:HEADS].unsqueeze(2), heads), ALU.mult).then_inc(S["hnormed"], 1)
                    dve.wait_ge(S["hnormed"], n("hnormed", s))
                    nc.vector.tensor_tensor(a.os[u][:, :, :], a.os[u][:, :, :],
                                            bcast(const(k, "mn_w").unsqueeze(1), heads), ALU.mult).then_inc(S["hweighted"], 1)
                    dve.wait_ge(S["hweighted"], n("hweighted", s))
                    nc.vector.tensor_tensor(a.os[u][:, :, :], a.os[u][:, :, :],
                                            bcast(const(k, "mn_b").unsqueeze(1), heads), ALU.add).then_inc(S["os_ready"], 1)

            def take_values(s, u):
                dve.wait_ge(S["folded"], n("folded", s))
                if not (isinstance(s, int) and s < 2):
                    dve.wait_ge(S["mixed"], n("mixed", s - 2))
                v = bank(k, 2)[:, 0:2 * C].rearrange("p (a h b d) -> p a h b d", a=PAIRS, h=2, b=2)
                for h in two:
                    r = slice(64 * h, 64 * h + 64)
                    last = nc.vector.tensor_copy(a.vd[u][r, :, h, :, :].rearrange("p a b d -> p a (b d)"),
                                                 v[r, :, h, :, :].rearrange("p a b d -> p a (b d)"))
                last.then_inc(S["vd_ready"], 1)

            def residual(tile, u):
                dve.wait_ge(S["projected"], n("projected", tile))
                nc.vector.tensor_tensor(tile_of(k.x1, tile) if keep else k.ys[u][:, :], tile_of(k.h, tile),
                                        bank(k, 5)[:, 256:256 + C], ALU.add).then_inc(S["y_ready"], 1)
                if not keep:
                    dve.wait_ge(S["y_ready"], n("y_ready", tile))
                    ln_stats(nc, k, dve, k.ys[u][:, :], tile, "out_")

            def slot(s, u, in_a, in_b, in_c, in_x):
                if in_b:
                    masked_maximum(s - 1, 1 - u)
                    if kind == "linear":
                        weights(s - 1, 1 - u)
                if in_a and kind == "linear":
                    positive_keys(s, u)
                if in_a and kind == "rotary":
                    rotated_keys(s, u)
                if in_c:
                    normalised(s - 2, u)
                if in_a and kind == "segments":
                    bilinear_values(s, u)
                if in_a and kind == "rotary":
                    rotated_keys_turn(s, u)
                if in_a and kind == "linear":
                    positive_keys_spread(s, u)
                if in_c:
                    normalised_heads(s - 2, u)
                if in_b and kind != "linear":
                    weights(s - 1, 1 - u)
                if in_x:
                    input_rows(s + 1, 1 - u)
                if in_a and kind == "rotary":
                    rotated_keys_spread(s, u)
                early = kind != "linear"
                if in_c and early:
                    residual(s - 2, u)
                if in_a:
                    take_values(s, u)
                if in_c and not early:
                    residual(s - 2, u)
                if in_c and not keep:
                    ln_apply(nc, k, dve, tile_of(k.h, s - 2), k.ys[u][:, :], s - 2, "out_")

            input_rows(0, 0)
            in_slots(dve, slot)

    both = ["x_ready", "x_turned", "xt_ready", "qkv_projected", "wide_ready", "folded", "qk_ready", "vd_ready",
            "scored", "p_turned", "prt_ready", "mixed", "os_ready", "o_turned", "ot_ready",
            "projected", "y_ready", "rsum_ready", "sum_ready", "max_ready"]
    both += ["in_" + x for x in LN_SIGNALS if pre_ln] + ["out_" + x for x in LN_SIGNALS if not keep]
    if kind != "softmax":
        both.append("qkv_ready")
    both += ["p_ready"] if kind == "linear" else ["centred", "exped", "masked"]
    if kind == "segments":
        both.append("p_ready")
    S.passed(**dict.fromkeys(both, TILES))


def turn(nc, k, source, ln2=False):
    S = k.S
    with ExitStack() as own:
        if ln2:
            sb = lambda name, shape: own.enter_context(nc.sbuf_tensor("ln2_" + name, shape, F32))
            stats, meanvar = sb("stats", [P, TILES, 6]), sb("meanvar", [P, TILES, 2])
            vareps, rstd = sb("vareps", [P, TILES]), sb("rstd", [P, TILES])
        rows = k.rows if ln2 else source
        block = own.enter_context(nc.Block())

        def take(eng, t):
            dst, src = k.ht[0:KH, :, t * P:(t + 1) * P], bank(k, t)[0:KH, 0:2 * P].rearrange("p (f t) -> p f t", f=2)
            eng.wait_ge(S["x_turned"], S.at("x_turned") + t + 1)
            for f in range(2) if ln2 else ():
                nc.scalar.activation(dst[:, f, :], src[:, f, :], ACT.Identity, scale=small(k, "ln2_w")[0:KH, f, :],
                                     bias=small(k, "ln2_b")[0:KH, f, :])
            return dst, src

        if ln2:
            @block.gpsimd
            def _(pool):
                pool.wait_ge(S["ln2_ready"], 3)
                nc.gpsimd.tensor_tensor(rstd[:, :], vareps[:, :], k.minus_half[:, 0:TILES], ALU.pow).then_inc(S["ln2_ready"], 1)

        @block.tensor
        def _(pe):
            for t in range(TILES):
                if ln2:
                    pe.wait_ge(S["ln2_ready"], 4 + t + 1)
                for f in range(2):
                    last = nc.tensor.transpose(bank(k, t)[0:KH, f * P:(f + 1) * P], rows[:, t, f * KH:(f + 1) * KH],
                                               const(k, "ident"))
                last.then_inc(S["x_turned"], 1)

        @block.scalar
        def _(act):
            for t in range(0, TILES, 1 if ln2 else 2):
                dst, src = take(act, t)
                if not ln2:
                    nc.scalar.activation(dst, src, ACT.Copy)

        @block.vector
        def _(dve):
            if ln2:
                for t in range(TILES):
                    last = nc.vector.bn_stats(stats[:, t, :], source[:, t, :])
                last.then_inc(S["ln2_ready"], 1)
                dve.wait_ge(S["ln2_ready"], 1)
                for t in range(TILES):
                    last = nc.vector.bn_aggr(meanvar[:, t, :], stats[:, t, :])
                last.then_inc(S["ln2_ready"], 1)
                dve.wait_ge(S["ln2_ready"], 2)
                nc.vector.tensor_scalar_add(vareps[:, :], meanvar[:, :, 1], LN_EPS).then_inc(S["ln2_ready"], 1)
                dve.wait_ge(S["ln2_ready"], 4)
                for t in range(TILES):
                    nc.vector.tensor_scalar(k.rows[:, t, :], source[:, t, :], meanvar[:, t, 0:1], rstd[:, t:t + 1],
                                            ALU.subtract, ALU.mult).then_inc(S["ln2_ready"], 1)
            else:
                for t in range(1, TILES, 2):
                    dst, src = take(dve, t)
                    nc.vector.tensor_copy(dst, src)
    S.passed(x_turned=TILES)


def gates(nc, k):
    S, a = k.S, k.a
    with ExitStack() as own:
        sb = lambda name, shape: own.enter_context(nc.sbuf_tensor(name, shape, F32))
        hidden = sb("gate_hidden", [P, TOKENS])
        params = sb("gate_params", [P, TILES, 5, HEADS])
        amp = sb("gate_amp", [P, 2, TILES, HEADS])
        phase = sb("gate_phase", [P, 2, TILES, HEADS])
        temp = sb("gate_temp", [P, 1])
        block = own.enter_context(nc.Block())

        @block.tensor
        def _(pe):
            for g in range(2):
                for f in range(2):
                    last = nc.tensor.matmul(bank(k, g), small(k, "wb1")[0:KH, f, :], k.ht[0:KH, f, g * BANK:(g + 1) * BANK],
                                            start=(f == 0), stop=(f == 1))
            last.then_inc(S["gate_up"], 1)
            pe.wait_ge(S["gate_hidden_ready"], 1)
            for t in range(TILES):
                last = nc.tensor.matmul(bank(k, 2)[:, t * 60:(t + 1) * 60], hidden[:, t * P:(t + 1) * P],
                                        const(k, "wb2"), start=True, stop=True)
            last.then_inc(S["gate_down"], 1)

        @block.scalar
        def _(act):
            act.wait_ge(S["gate_up"], 1)
            nc.scalar.activation(hidden[:, :], banks(k, 0, 2), ACT.Silu).then_inc(S["gate_hidden_ready"], 1)
            act.wait_ge(S["gate_params_ready"], 1)
            for j in range(2):
                nc.scalar.activation(amp[:, j, :, :], params[:, :, 2 * j, :], ACT.Tanh, scale=0.5)
                last = nc.scalar.activation(phase[:, j, :, :], params[:, :, 2 * j + 1, :], ACT.Tanh)
            last.then_inc(S["gate_by_act"], 1)
            act.wait_ge(S["gate_by_dve"], 1)
            nc.scalar.activation(phase[:, 1, :, :], phase[:, 0, :, :], ACT.Sin, scale=math.pi / 2).then_inc(S["gate_by_act"], 1)
            act.wait_ge(S["gate_by_dve"], 2)
            nc.scalar.activation(amp[:, 1, :, :], amp[:, 0, :, :], ACT.Tanh).then_inc(S["gate_by_act"], 1)
            act.wait_ge(S["gate_by_dve"], 3)
            nc.scalar.activation(amp[:, 1, :, :], amp[:, 0, :, :], ACT.Tanh, scale=0.5).then_inc(S["gate_by_act"], 1)

        @block.vector
        def _(dve):
            steps = [0]

            def then(ins):
                steps[0] += 1
                ins.then_inc(S["gate_step"], 1)
                dve.wait_ge(S["gate_step"], steps[0])

            then(nc.vector.tensor_scalar(temp[:, :], const(k, "temperature"), 0.1, 2.0, ALU.max, ALU.min))
            dve.wait_ge(S["gate_down"], 1)
            nc.vector.tensor_copy(params[:, :, :, :].rearrange("p t j h -> p (t j h)"),
                                  bank(k, 2)[:, 0:TILES * 60]).then_inc(S["gate_params_ready"], 1)
            dve.wait_ge(S["gate_by_act"], 1)
            then(nc.vector.tensor_scalar(amp[:, :, :, :], amp[:, :, :, :], 0.5, 0.5, ALU.mult, ALU.add))
            nc.vector.tensor_tensor(phase[:, 0, :, :], phase[:, 0, :, :], phase[:, 1, :, :],
                                    ALU.subtract).then_inc(S["gate_by_dve"], 1)
            then(nc.vector.tensor_tensor(amp[:, 0, :, :], amp[:, 0, :, :], amp[:, 1, :, :], ALU.mult))
            dve.wait_ge(S["gate_by_act"], 2)
            then(nc.vector.tensor_tensor(phase[:, 0, :, :], phase[:, 1, :, :], phase[:, 1, :, :], ALU.mult))
            then(nc.vector.tensor_scalar(phase[:, 1, :, :], phase[:, 0, :, :], -2.0, 1.0, ALU.mult, ALU.add))
            nc.vector.tensor_tensor(amp[:, 0, :, :], amp[:, 0, :, :], phase[:, 1, :, :], ALU.mult).then_inc(S["gate_by_dve"], 1)
            dve.wait_ge(S["gate_by_act"], 3)
            nc.vector.tensor_scalar(amp[:, 0, :, :], amp[:, 1, :, :], temp[:, :], None, ALU.mult).then_inc(S["gate_by_dve"], 1)
            dve.wait_ge(S["gate_by_act"], 4)
            nc.vector.tensor_scalar(a.gate1[:, :, :], amp[:, 1, :, :], 0.5, 1.5, ALU.mult, ALU.add)


def send_rows(nc, k, rows, choice, tile):
    nc.gpsimd.indirect_dma_start(k.sent, bass.IndirectOffsetOnAxis(ap=k.slot[:, choice, tile:tile + 1], axis=0),
                                 rows[:, tile, :], None).then_inc(k.S["rows_sent"], 16)


def route(nc, k, layer, io):
    S = k.S
    E = MOES[f"l{layer}"]["experts"]
    cap = MOES[f"l{layer}"]["cap"]
    top = 3 if layer == 1 else 2
    tag = f"route{layer}_"
    with ExitStack() as own:
        sb = lambda name, shape, dt=F32: own.enter_context(nc.sbuf_tensor(tag + name, shape, dt))
        logits = sb("logits", [P, TILES, E])
        probs = sb("probs", [P, TILES, E])
        best = sb("best", [P, TILES, 8])
        index = sb("index", [P, TILES, 8], U32)
        indexf = sb("indexf", [P, TILES, 8])
        hot = sb("hot", [P, top, TILES, E])
        weight = sb("weight", [P, top, TILES])
        small1 = sb("small1", [P, TILES])
        prefix = sb("prefix", [P, 2, TILES + 1, E])
        counted = sb("counted", [P, 2, TILES, E])
        kept = sb("kept", [P, top, TILES, E])
        place, has_room, slot = [sb(nm, [P, top, TILES]) for nm in ("place", "has_room", "slot")]
        if layer == 1:
            tiles_of = sb("tiles_of", [E, 1])
            tiles_row = sb("tiles_row", [E, P])
            start = sb("start", [P, E])
            behind = sb("behind", [1, SORTED, E])
            tile_expert = sb("tile_expert", [1, SORTED])
            lnb = sb("lnb", [P, 3, E * (E + 1)])
        block = own.enter_context(nc.Block())
        shape = [P, TILES, E]

        @block.tensor
        def _(pe):
            def expert_row_products(first, end):
                for e in range(first, end):
                    for m in range(3):
                        last = nc.tensor.matmul(bank(k, 2)[0:E, 0:C], lnb[:, m, e * E:(e + 1) * E], k.w2_sorted[:, e, m, :],
                                                start=(e == 0 and m == 0), stop=(e == E - 1 and m == 2))
                    last.then_inc(S["expert_row_done"], 1)

            for t in range(TILES):
                for f in range(2):
                    last = nc.tensor.matmul(bank(k, 0)[:, t * E:(t + 1) * E], k.ht[0:KH + f, f, t * P:(t + 1) * P],
                                            small(k, f"gate{layer}")[0:KH + f, f, :], start=(f == 0), stop=(f == 1))
            last.then_inc(S["logits_done"], 1)
            if layer == 1:
                pe.wait_ge(S["lnb_ready"], 1)
                pe.wait_ge(S["w_sorted_loaded"], 16 * W_SORTED_PARTS)
                expert_row_products(0, 5)
            width = 2 if layer == 0 else 1
            pe.wait_ge(S["prefix_ready"], S.at("prefix_ready") + 1)
            src = hot if layer == 0 else counted
            out = bank(k, 1)[:, 0:width * TILES * E].rearrange("p (c x) -> p c x", c=width)
            nc.tensor.matmul(out, const(k, "earlier"), src[:, 0:width, 0:TILES, :].rearrange("p c t e -> p c (t e)"),
                             start=True, stop=False)
            last = nc.tensor.matmul(out, const(k, "ones"), prefix[:, 0:width, 0:TILES, :].rearrange("p c t e -> p c (t e)"),
                                    start=False, stop=True)
            if layer == 1:
                last = nc.tensor.matmul(bank(k, 3)[0:E, 0:1], prefix[:, 0, TILES, :], const(k, "ones")[:, 0:1],
                                        start=True, stop=True)
            last.then_inc(S["ranked"], 1)
            if layer == 1:
                expert_row_products(5, 6)
                pe.wait_ge(S["tiles_ready"], 1)
                nc.tensor.matmul(bank(k, 3)[:, 16:16 + E], tiles_row[:, :], const(k, "earlier")[0:E, 0:E],
                                 start=True, stop=True).then_inc(S["started"], 1)
                expert_row_products(6, E)
                pe.wait_ge(S["combine_ready"], 1)
                for t in range(TILES):
                    last = nc.tensor.transpose(banks(k, 0, 2)[0:E, t * P:(t + 1) * P], k.combine[:, t, :], const(k, "ident"))
                last.then_inc(S["combine_turned"], 1)
                pe.wait_ge(S["combine_t_ready"], 1)
                for t in range(TILES):
                    last = nc.tensor.matmul(banks(k, 4, 4).rearrange("p (t c) -> p t c", t=TILES)[:, t, 0:C],
                                            k.combine_t[:, t, :], k.expert_rows[:, :], start=True, stop=True)
                last.then_inc(S["rows_added"], 1)

        @block.gpsimd
        def _(pool):
            pool.wait_ge(S["slots_cleared"], 16)
            pool.wait_ge(S["slots_ready"], S.at("slots_ready") + 1)
            for t in range(TILES):
                send_rows(nc, k, k.h if layer == 1 else k.rows, 0, t)

        if layer == 1:
            @block.sync
            def _(sp):
                sp.dma_start(k.sent[0:TOKENS, :].rearrange("(t p) c -> p t c", p=P), k.h[:, :, :]).then_inc(S["shared_sent"], 16)
                sp.dma_start(k.expert_rows[:, :], io["l1_rows"]).then_inc(S["rows_loaded"], 16)
                sp.wait_ge(S["shared_sent"], 16)

        @block.scalar
        def _(act):
            if layer == 0:
                act.wait_ge(S["route_gap"], 1)
                nc.scalar.activation(weight[:, 1, :], small1[:, :], ACT.Exp).then_inc(S["route_exp"], 1)
            else:
                act.wait_ge(S["route_gap"], S.at("route_gap") + 1)
                nc.scalar.activation(probs[:, :, :], logits[:, :, :], ACT.Exp).then_inc(S["route_exp"], 1)
            if layer == 1:
                for e in range(E):
                    act.wait_ge(S["expert_row_done"], e + 1)
                    for m in range(3):
                        nc.scalar.activation(k.w2_sorted[:, e, m, :], k.w2_sorted[:, e, m, :], ACT.Copy,
                                             scale=k.side_sorted[:, 0, m, e:e + 1])

        @block.vector
        def _(dve):
            at = [S.at("route_step")]

            def then(ins):
                at[0] += 1
                ins.then_inc(S["route_step"], 1)
                dve.wait_ge(S["route_step"], at[0])

            if layer == 1:
                then(nc.vector.memset(lnb[:, :, :], 0.0))
                dve.wait_ge(S["w_sorted_loaded"], 16 * W_SORTED_PARTS)
                nc.vector.tensor_copy(lnb[:, :, 0:E * (E + 1):E + 1], k.side_sorted[:, 1, :, :]).then_inc(S["lnb_ready"], 1)
            dve.wait_ge(S["logits_done"], S.at("logits_done") + 1)
            then(nc.vector.tensor_copy(logits[:, :, :], bank(k, 0)[:, 0:TILES * E].rearrange("p (t e) -> p t e", e=E)))
            source = logits
            if layer > 0:
                if layer == 1:
                    then(nc.vector.memset(logits[:, :, 0:1], -1e9))
                then(nc.vector.tensor_reduce(small1[:, :], logits[:, :, :], AX.X, ALU.max))
                nc.vector.tensor_tensor(logits[:, :, :], logits[:, :, :], bcast(small1[:, :].unsqueeze(2), shape),
                                        ALU.subtract).then_inc(S["route_gap"], 1)
                dve.wait_ge(S["route_exp"], S.at("route_exp") + 1)
                then(nc.vector.tensor_reduce(small1[:, :], probs[:, :, :], AX.X, ALU.add))
                then(nc.vector.reciprocal(small1[:, :], small1[:, :]))
                then(nc.vector.tensor_tensor(probs[:, :, :], probs[:, :, :], bcast(small1[:, :].unsqueeze(2), shape), ALU.mult))
                source = probs
            for t in range(TILES):
                last = nc.vector.max(best[:, t, :], source[:, t, :])
            then(last)
            for t in range(TILES):
                last = nc.vector.max_index(index[:, t, :], best[:, t, :], source[:, t, :])
            then(last)
            then(nc.vector.tensor_copy(indexf[:, :, :], index[:, :, :]))
            for c in range(top):
                last = nc.vector.tensor_tensor(hot[:, c, :, :], bcast(const(k, "iota")[:, 0:E].unsqueeze(1), shape),
                                               bcast(indexf[:, :, c:c + 1], shape), ALU.is_equal)
            then(last)
            if layer == 0:
                nc.vector.tensor_tensor(small1[:, :], best[:, :, 1], best[:, :, 0], ALU.subtract).then_inc(S["route_gap"], 1)
                dve.wait_ge(S["route_exp"], 1)
                then(nc.vector.tensor_scalar_add(small1[:, :], weight[:, 1, :], 1.0))
                then(nc.vector.reciprocal(weight[:, 0, :], small1[:, :]))
                then(nc.vector.tensor_tensor(weight[:, 1, :], weight[:, 1, :], weight[:, 0, :], ALU.mult))
            elif layer == 1:
                for c in range(top):
                    last = nc.vector.tensor_copy(weight[:, c, :], best[:, :, c])
                then(last)
            else:
                then(nc.vector.tensor_tensor(small1[:, :], best[:, :, 0], best[:, :, 1], ALU.add))
                then(nc.vector.reciprocal(small1[:, :], small1[:, :]))
                for c in range(top):
                    last = nc.vector.tensor_tensor(weight[:, c, :], best[:, :, c], small1[:, :], ALU.mult)
                then(last)
            if layer == 0:
                order = [(c, t) for c in range(2) for t in range(TILES)]
                tokens = hot
            else:
                then(nc.vector.tensor_tensor(counted[:, 0, :, :], hot[:, 0, :, :], hot[:, 1, :, :], ALU.add))
                if layer == 1:
                    then(nc.vector.tensor_tensor(counted[:, 0, :, :], counted[:, 0, :, :], hot[:, 2, :, :], ALU.add))
                order = [(0, t) for t in range(TILES + (layer == 1))]
                tokens = counted
            last = nc.vector.memset(prefix[:, 0, 0, :], 0.0)
            for (c0, t0), (c1, t1) in zip(order, order[1:]):
                then(last)
                last = nc.vector.tensor_tensor(prefix[:, c1, t1, :], prefix[:, c0, t0, :], tokens[:, c0, t0, :], ALU.add)
            last.then_inc(S["prefix_ready"], 1)
            dve.wait_ge(S["ranked"], S.at("ranked") + 1)
            width = 2 * TILES * E if layer == 0 else TILES * E
            rank = bank(k, 1)[:, 0:width].rearrange("p (c t e) -> p c t e", t=TILES, e=E)
            if layer == 1:
                then(nc.vector.tensor_scalar(tiles_of[:, :], bank(k, 3)[0:E, 0:1], 1.0 / P, (P - 1.0) / P - 0.5 + 0.5 / P,
                                             ALU.mult, ALU.add))
                then(nc.vector.tensor_scalar_add(tiles_of[:, :], tiles_of[:, :], ROUND))
                then(nc.vector.tensor_scalar_add(tiles_of[:, :], tiles_of[:, :], -ROUND))
                nc.vector.tensor_scalar(tiles_row[:, :], const(k, "ones")[0:E, :], tiles_of[:, :], None,
                                        ALU.mult).then_inc(S["tiles_ready"], 1)
                dve.wait_ge(S["started"], 1)
                then(nc.vector.tensor_scalar(start[:, :], bank(k, 3)[:, 16:16 + E], float(P), float(TOKENS), ALU.mult, ALU.add))
                nc.vector.tensor_tensor(prefix[:, 0, 0:TILES, :], rank[:, 0, :, :], bcast(start[:, :].unsqueeze(1), shape),
                                        ALU.add)
                wide = [1, SORTED, E - 1]
                then(nc.vector.tensor_tensor(behind[:, :, 1:E], bcast(const(k, "tile_start")[0:1, 0:SORTED].unsqueeze(2), wide),
                                             bcast(start[0:1, 1:E].unsqueeze(1), wide), ALU.is_ge))
                nc.vector.tensor_reduce(tile_expert[:, :], behind[:, :, 1:E], AX.X, ALU.add)
                for c in range(top):
                    last = nc.vector.tensor_tensor(kept[:, c, :, :], hot[:, c, :, :], prefix[:, 0, 0:TILES, :], ALU.mult)
                then(last)
                nc.vector.tensor_copy(k.tile_expert[:, :], tile_expert[:, :])
                then(nc.vector.tensor_reduce(slot[:, :, :], kept[:, :, :, :], AX.X, ALU.add))
                nc.vector.tensor_copy(k.slot[:, :, :], slot[:, :, :]).then_inc(S["slots_ready"], 1)
                nc.vector.tensor_copy(k.back[:, :, :], slot[:, :, :])
                nc.vector.tensor_copy(k.share[:, :, :], weight[:, :, :])
                for c in range(top):
                    last = nc.vector.tensor_tensor(hot[:, c, :, :], hot[:, c, :, :], bcast(weight[:, c, :].unsqueeze(2), shape), ALU.mult)
                then(last)
                dst = k.combine[:, :, :]
                then(nc.vector.tensor_tensor(dst, hot[:, 0, :, :], hot[:, 1, :, :], ALU.add))
                then(nc.vector.tensor_tensor(dst, dst, hot[:, 2, :, :], ALU.add))
                nc.vector.tensor_scalar_add(k.combine[:, :, 0:1], k.combine[:, :, 0:1], 1.0).then_inc(S["combine_ready"], 1)
                dve.wait_ge(S["rows_loaded"], 16)
                dve.wait_ge(S["expert_row_done"], E)
                nc.vector.tensor_tensor(k.expert_rows[:, :], k.expert_rows[:, :], bank(k, 2)[0:E, 0:C], ALU.add)
                dve.wait_ge(S["combine_turned"], 1)
                nc.vector.tensor_copy(k.combine_t[:, :, :].rearrange("p t c -> p (t c)"),
                                      banks(k, 0, 2)[0:E, :]).then_inc(S["combine_t_ready"], 1)
                dve.wait_ge(S["rows_added"], 1)
                nc.vector.tensor_tensor(k.acc[:, :, :], k.h[:, :, :],
                                        banks(k, 4, 4).rearrange("p (t c) -> p t c", t=TILES)[:, :, 0:C], ALU.add)
            else:
                for c in range(2):
                    last = nc.vector.tensor_tensor(kept[:, c, :, :], hot[:, c, :, :], rank[:, c if layer == 0 else 0, :, :], ALU.mult)
                then(last)
                then(nc.vector.tensor_reduce(place[:, :, :], kept[:, :, :, :], AX.X, ALU.add))
                nc.vector.tensor_scalar(has_room[:, :, :], place[:, :, :], float(cap), None, ALU.is_lt)
                then(nc.vector.scalar_tensor_tensor(out=slot[:, :, :], in0=indexf[:, :, 0:2].rearrange("p t c -> p c t"),
                                                    scalar=float(cap), in1=place[:, :, :], op0=ALU.mult, op1=ALU.add))
                refused = const(k, "refused").rearrange("p (c t) -> p c t", c=2)
                then(nc.vector.tensor_tensor(slot[:, :, :], slot[:, :, :], refused, ALU.subtract))
                then(nc.vector.tensor_tensor(slot[:, :, :], slot[:, :, :], has_room[:, :, :], ALU.mult))
                then(nc.vector.tensor_tensor(slot[:, :, :], slot[:, :, :], refused, ALU.add))
                nc.vector.tensor_copy(k.slot[:, 0:2, :], slot[:, 0:2, :]).then_inc(S["slots_ready"], 1)
                then(nc.vector.tensor_scalar(slot[:, :, :], slot[:, :, :], float(SLOTS - 1), None, ALU.min))
                nc.vector.tensor_copy(k.back[:, 0:2, :], slot[:, 0:2, :])
                then(nc.vector.tensor_tensor(k.share[:, 0:2, :], weight[:, :, :], has_room[:, :, :], ALU.mult))
                if layer == 0:
                    nc.vector.tensor_tensor(k.acc[:, :, :], k.h[:, :, :], k.x1[:, :, :], ALU.add)
                else:
                    then(nc.vector.tensor_tensor(small1[:, :], k.share[:, 0, :], k.share[:, 1, :], ALU.add))
                    then(nc.vector.tensor_scalar_add(small1[:, :], small1[:, :], 1.0))
                    nc.vector.tensor_tensor(k.acc[:, :, :], k.h[:, :, :], bcast(small1[:, :].unsqueeze(2), [P, TILES, C]), ALU.mult)
            route.steps = at[0] - S.at("route_step")
    S.passed(logits_done=1, route_gap=1, route_exp=1, route_step=route.steps,
             prefix_ready=1, ranked=1, slots_ready=1, rows_sent=16 * top * TILES)


def allocate_experts(nc, k, ctx):
    def sb(name, shape):
        return ctx.enter_context(nc.sbuf_tensor(name, shape, F32))

    k.combine = sb("combine", [P, TILES, 16])
    k.combine_t = sb("combine_t", [16, TILES, P])
    k.expert_rows = sb("expert_rows", [16, C])
    k.acc = sb("acc", [P, TILES, C])
    k.rows = sb("rows", [P, TILES, C])
    k.share = sb("share", [P, CHOICES, TILES])
    k.tile_expert = ctx.enter_context(nc.sbuf_tensor("tile_expert", [1, SORTED], I32))
    k.slot = ctx.enter_context(nc.sbuf_tensor("slot", [P, CHOICES, TILES], U32))
    k.back = ctx.enter_context(nc.sbuf_tensor("back", [P, CHOICES, TILES], U32))


def allocate_sorted(nc, k, ctx):
    M = MOES["l1"]
    sb = lambda nm, shape: ctx.enter_context(nc.sbuf_tensor(nm, shape, F32))
    k.w1_sorted = sb("w1_sorted", [KH + 1, 2, M["experts"], M["up"] * P])
    k.w2_sorted = sb("w2_sorted", [P, M["experts"], M["hid"], C])
    k.side_sorted = sb("side_sorted", [P, 2, M["hid"], M["experts"]])


W_SORTED_PARTS = 13


def load_sorted(k, io, sp):
    for f in range(2):
        for e in range(0, 16, 4):
            sp.dma_start(k.w1_sorted[:, f, e:e + 4, :], io["l1_w1"][:, f, e:e + 4, :]).then_inc(k.S["w_sorted_loaded"], 16)
    for e in range(0, 16, 4):
        sp.dma_start(k.w2_sorted[:, e:e + 4, :, :], io["l1_w2"][:, e:e + 4, :, :]).then_inc(k.S["w_sorted_loaded"], 16)
    sp.dma_start(k.side_sorted[:, :, :, :], io["l1_side"]).then_inc(k.S["w_sorted_loaded"], 16)


def sorted_experts(nc, k):
    S = k.S
    H = MOES["l1"]["up"] * P
    N = SORTED
    two = (0, 1)

    def in_time(eng, step, first, last):
        for s in range(first):
            step(s, s % 2, s)
        with eng.Fori(0, (last - first) // 2) as i:
            step(i * 2 + first, 0, first)
            step(i * 2 + (first + 1), 1, first)
        for s in range(last, N + 2):
            step(s, s % 2, s)

    with ExitStack() as own:
        sb = lambda nm, shape: own.enter_context(nc.sbuf_tensor("sorted_" + nm, shape, F32))
        rows = [sb(f"rows{u}", [P, C]) for u in two]
        xt = [sb(f"xt{u}", [KH + 1, 2, P]) for u in two]
        hid = [sb(f"hid{u}", [P, H]) for u in two]
        normed = [sb(f"normed{u}", [P, H]) for u in two]
        hidt = [sb(f"hidt{u}", [P, H]) for u in two]
        out = [sb(f"out{u}", [P, C]) for u in two]
        stats, meanvar = [[sb(f"{nm}{u}", [P, w]) for u in two] for nm, w in (("stats", 6), ("meanvar", 2))]
        vareps, rstd = [[sb(f"{nm}{u}", [P, 1]) for u in two] for nm in ("vareps", "rstd")]
        pause = sb("pause", [P, 1])
        block = own.enter_context(nc.Block())

        def at(tile, each=1):
            return tile * each + each

        def each_rows(t, tile):
            return t[0:N * P, :].rearrange("(t p) c -> t p c", p=P)[bass.ds(tile, 1), :, :].rearrange("t p c -> p (t c)")

        @block.sync
        def _(sp):
            def load(tile, u):
                sp.dma_start(rows[u][:, :], each_rows(k.sent, tile)).then_inc(S[f"tile_loaded{u}"], 16)

            def step(s, u, low):
                if low + 3 < N:
                    if low == TILES - 3:
                        sp.wait_ge(S["rows_sent"], S.at("rows_sent"))
                    sp.wait_ge(S["tile_turned"], at(s + 1))
                    load(s + 3, 1 - u)
                if low >= 2:
                    sp.wait_ge(S["tile_out"], at(s - 2))
                    sp.dma_start(each_rows(k.returned, s - 2), out[u][:, :]).then_inc(S[f"tile_stored{u}"], 16)

            for t in range(3):
                if t == 2:
                    sp.wait_ge(S["tile_turned"], at(0))
                load(t, t % 2)
            in_time(sp, step, 6, N - 4)
            for u in two:
                sp.wait_ge(S[f"tile_stored{u}"], 16 * N // 2)

        @block.gpsimd
        def _(pool):
            def step(s, u, low):
                if low < N:
                    pool.wait_ge(S["tile_vareps"], at(s))
                    nc.gpsimd.tensor_tensor(rstd[u][:, :], vareps[u][:, :], k.minus_half[:, 0:1], ALU.pow).then_inc(S["tile_rstd"], 1)
                if low < TILES:
                    for c in range(1, CHOICES):
                        send_rows(nc, k, k.h, c, s)
            in_time(pool, step, TILES, N - 2)

        @block.tensor
        def _(pe):
            def expert_of(tile):
                return nc.values_load(k.tile_expert[0:1, bass.ds(tile, 1)], engines=[mybir.EngineType.PE], min_val=0, max_val=15,
                                      skip_runtime_bounds_check_because="it counts experts 1 to 15")

            def turn_tile(tile, u, low):
                pe.wait_ge(S[f"tile_loaded{u}"], (tile - u) * 8 + 16)
                if low >= 2:
                    pe.wait_ge(S["tile_xt"], at(tile - 2))
                for f in two:
                    last = nc.tensor.transpose(bank(k, u)[0:KH, f * P:(f + 1) * P], rows[u][:, f * KH:(f + 1) * KH], const(k, "ident"))
                last.then_inc(S["tile_turned"], 1)

            def step(s, u, low):
                up_of = expert_of(s) if low < N else None
                down_of = expert_of(s - 2) if low >= 2 else None
                if low >= 2:
                    pe.wait_ge(S["tile_normed"], at(s - 2))
                    if low >= 4:
                        pe.wait_ge(S["tile_hidt"], at(s - 4))
                    for m in range(3):
                        last = nc.tensor.transpose(bank(k, 4 + u)[:, m * P:(m + 1) * P], normed[u][:, m * P:(m + 1) * P], const(k, "ident"))
                    last.then_inc(S["tile_hid_turned"], 1)
                if low < N:
                    pe.wait_ge(S["tile_xt"], at(s))
                    if low >= 2:
                        pe.wait_ge(S["tile_hid"], at(s - 2))
                    for f in two:
                        last = nc.tensor.matmul(bank(k, 2 + u)[:, 0:H], xt[u][0:KH + f, f, :],
                                                k.w1_sorted[0:KH + f, f, bass.ds(up_of, 1), :].rearrange("p e h -> p (e h)"),
                                                start=(f == 0), stop=(f == 1))
                    last.then_inc(S["tile_up"], 1)
                if low + 1 < N:
                    turn_tile(s + 1, 1 - u, low + 1)
                if low >= 2:
                    pe.wait_ge(S["tile_hidt"], at(s - 2))
                    if low >= 4:
                        pe.wait_ge(S["tile_out"], at(s - 4))
                    for m in range(3):
                        last = nc.tensor.matmul(bank(k, 6 + u)[:, 0:C], hidt[u][:, m * P:(m + 1) * P],
                                                k.w2_sorted[:, bass.ds(down_of, 1), m, :].rearrange("p e c -> p (e c)"),
                                                start=(m == 0), stop=(m == 2))
                    last.then_inc(S["tile_down"], 1)

            keep_awake(nc, k, AWAKE_FIRST)
            turn_tile(0, 0, 0)
            in_time(pe, step, 4, N - 2)

        @block.scalar
        def _(act):
            def take_rows(tile, u, low):
                act.wait_ge(S["tile_turned"], at(tile))
                if low == 0 or low == 1:
                    act.wait_ge(S["ones_set"], 1)
                if low >= 2:
                    act.wait_ge(S["tile_up"], at(tile - 2))
                nc.scalar.activation(xt[u][0:KH, :, :].rearrange("p f t -> p (f t)"), bank(k, u)[0:KH, 0:2 * P],
                                     ACT.Copy).then_inc(S["tile_xt"], 1)

            def step(s, u, low):
                if low >= 2:
                    act.wait_ge(S["tile_hid_turned"], at(s - 2))
                    if low >= 4:
                        act.wait_ge(S["tile_down"], at(s - 4))
                    nc.scalar.activation(hidt[u][:, :], bank(k, 4 + u)[:, 0:H], ACT.Copy).then_inc(S["tile_hidt"], 1)
                if low < N:
                    act.wait_ge(S["tile_up"], at(s))
                    if low >= 2:
                        act.wait_ge(S["tile_normed"], at(s - 2))
                    nc.scalar.activation(hid[u][:, :], bank(k, 2 + u)[:, 0:H], ACT.Gelu).then_inc(S["tile_hid"], 1)
                if low + 1 < N:
                    take_rows(s + 1, 1 - u, low + 1)

            take_rows(0, 0, 0)
            in_time(act, step, 4, N - 2)

        @block.vector
        def _(dve):
            def step(s, u, low):
                v = 1 - u
                if 1 <= low <= N:
                    dve.wait_ge(S["tile_rstd"], at(s - 1))
                    if low >= 3:
                        dve.wait_ge(S["tile_hid_turned"], at(s - 3))
                    nc.vector.tensor_scalar(normed[v][:, :], hid[v][:, :], meanvar[v][:, 0:1], rstd[v][:, :], ALU.subtract,
                                            ALU.mult).then_inc(S["tile_normed"], 1)
                if low < N:
                    dve.wait_ge(S["tile_hid"], at(s))
                    nc.vector.bn_stats(stats[u][:, :], hid[u][:, :]).then_inc(S["tile_stats"], 1)
                    dve.wait_ge(S["tile_stats"], at(s))
                    if low >= 2:
                        dve.wait_ge(S["tile_normed"], at(s - 2))
                    nc.vector.memset(pause[:, :], 0.0)
                    nc.vector.bn_aggr(meanvar[u][:, :], stats[u][:, :]).then_inc(S["tile_meanvar"], 1)
                    dve.wait_ge(S["tile_meanvar"], at(s))
                    nc.vector.tensor_scalar_add(vareps[u][:, :], meanvar[u][:, 1:2], LN_EPS).then_inc(S["tile_vareps"], 1)
                if low >= 2:
                    dve.wait_ge(S["tile_down"], at(s - 2))
                    if low >= 4:
                        dve.wait_ge(S[f"tile_stored{u}"], (s - u) * 8 - 16)
                    nc.vector.tensor_copy(out[u][:, :], bank(k, 6 + u)[:, 0:C]).then_inc(S["tile_out"], 1)

            nc.vector.memset(xt[0][KH:KH + 1, :, :], 1.0)
            nc.vector.memset(xt[1][KH:KH + 1, :, :], 1.0).then_inc(S["ones_set"], 1)
            in_time(dve, step, 4, N - 2)


def rms_rows(nc, k):
    S = k.S
    with ExitStack() as own:
        sums = own.enter_context(nc.sbuf_tensor("rms_sums", [P, TILES], F32))
        rstd = own.enter_context(nc.sbuf_tensor("rms_rstd", [P, TILES], F32))
        block = own.enter_context(nc.Block())

        @block.gpsimd
        def _(pool):
            pool.wait_ge(S["rms_sums_ready"], 3)
            nc.gpsimd.tensor_tensor(rstd[:, :], sums[:, :], k.minus_half[:, 0:TILES], ALU.pow).then_inc(S["rms_rstd_ready"], 1)

        @block.vector
        def _(dve):
            nc.vector.tensor_tensor(k.rows[:, :, :], k.h[:, :, :], k.h[:, :, :], ALU.mult).then_inc(S["rms_sums_ready"], 1)
            dve.wait_ge(S["rms_sums_ready"], 1)
            nc.vector.tensor_reduce(sums[:, :], k.rows[:, :, :], AX.X, ALU.add).then_inc(S["rms_sums_ready"], 1)
            dve.wait_ge(S["rms_sums_ready"], 2)
            nc.vector.tensor_scalar(sums[:, :], sums[:, :], 4.0 / C, 1e-6, ALU.mult, ALU.add).then_inc(S["rms_sums_ready"], 1)
            dve.wait_ge(S["rms_rstd_ready"], 1)
            for t in range(TILES):
                nc.vector.tensor_scalar(k.rows[:, t, :], k.h[:, t, :], rstd[:, t:t + 1], 2.0, ALU.mult, ALU.mult)


def sent_experts(nc, k, io, layer):
    S = k.S
    M = MOES[f"l{layer}"]
    E, UP, HID = M["experts"], M["up"], M["hid"]
    W2 = HID * C + (C if layer == 0 else 0)
    RING = {0: 4, 2: 2}[layer]
    tag = f"l{layer}_"
    name = lambda x: "sent_" + x
    two = (0, 1)
    with ExitStack() as own:
        sb = lambda nm, shape: own.enter_context(nc.sbuf_tensor(tag + nm, shape, F32))
        w1 = [sb(f"w1_{s}", [KH, 2, UP * P]) for s in two]
        w2 = [sb(f"w2_{s}", [P, W2]) for s in two]
        side = [sb(f"side{s}", [P, 16]) for s in two]
        rows = [sb(f"rows{s}", [P, len(ROW_TILES), C]) for s in two]
        xt = [sb(f"xt{s}", [KH, 2, CAPACITY]) for s in two]
        hid = [sb(f"hid{s}", [P, HID, CAPACITY]) for s in two]
        out = [sb(f"out{s}", [P, len(ROW_TILES), C]) for s in two]
        silu = [sb(f"silu{b}", [P, CAPACITY]) for b in two] if layer == 2 else None
        block = own.enter_context(nc.Block())

        def n(what, i, s, each=1, j=0, credit=0):
            return i * (2 * each) + (S.at(name(what)) + s * each + j + 1 + credit)

        def in_pairs(eng, expert):
            with eng.Fori(0, E // 2 - 1) as i:
                expert(i, 0, True)
                expert(i, 1, True)
            expert(E // 2 - 1, 0, True)
            expert(E // 2 - 1, 1, False)

        def slots_of(t, i, s):
            part = t[0:SLOTS, :].rearrange("(e r) c -> e r c", r=CAPACITY)[bass.ds(i * 2 + s, 1), :, :]
            return (part[:, 0:2 * P, :].rearrange("e (j p) c -> p (e j) c", p=P),
                    part[:, 2 * P:CAPACITY, :].rearrange("e p c -> p (e c)"))

        @block.sync
        def _(sp):
            def load_rows(i, s):
                whole, rest = slots_of(k.sent, i, s)
                sp.dma_start(rows[s][:, 0:2, :], whole).then_inc(S[name(f"rows{s}_loaded")], 16)
                sp.dma_start(rows[s][0:ROW_TILES[2][1], 2, :], rest).then_inc(S[name(f"rows{s}_loaded")], 16)

            def load_weights(i, s):
                at = bass.ds(i * 2 + s, 1)
                sp.dma_start(w1[s][:, :, :].rearrange("p f h -> p (f h)"),
                             io[tag + "w1"][at, :, :].rearrange("a p x -> p (a x)")).then_inc(S[name(f"w{s}_loaded")], 16)
                sp.dma_start(side[s][:, :], io[tag + "side"][at, :, :].rearrange("a p x -> p (a x)")).then_inc(S[name(f"w{s}_loaded")], 16)
                sp.dma_start(w2[s][:, :], io[tag + "w2"][at, :, :].rearrange("a p x -> p (a x)")).then_inc(S[name(f"w{s}_loaded")], 16)

            def expert(i, s, more):
                sp.wait_ge(S[name("out_ready")], n("out_ready", i, s, 3, 2, 2))
                whole, rest = slots_of(k.returned, i, s)
                sp.dma_start(whole, out[s][:, 0:2, :]).then_inc(S[name("out_stored")], 16)
                sp.dma_start(rest, out[s][0:ROW_TILES[2][1], 2, :]).then_inc(S[name("out_stored")], 16)
                if more:
                    load_rows(i + 1, s)
                    load_weights(i + 1, s)
                sp.wait_ge(S[name("out_stored")], n("out_stored", i, s, 32, 31))
                sp.sem_inc(S[name("out_free")], 1)

            for s in two:
                load_weights(0, s)
            sp.wait_ge(S["rows_sent"], S.at("rows_sent"))
            for s in two:
                load_rows(0, s)
            sp.sem_inc(S[name("out_free")], 2)
            with sp.Fori(0, E // 2 - 1) as i:
                for s in two:
                    expert(i, s, True)
            for s in two:
                expert(E // 2 - 1, s, False)

        @block.gpsimd
        def _(pool):
            for t in range(TILES):
                send_rows(nc, k, k.rows, 1, t)

        @block.tensor
        def _(pe):
            def turn_rows(i, s, first=False):
                pe.wait_ge(S[name(f"rows{s}_loaded")], n(f"rows{s}_loaded", i, 0, 16, 31))
                if not first:
                    pe.wait_ge(S[name("xt_ready")], n("xt_ready", i, s - 1))
                for j, (at, size) in enumerate(ROW_TILES):
                    for f in two:
                        last = nc.tensor.transpose(bank(k, 4 + f)[0:KH, at:at + size], rows[s][0:size, j, f * KH:(f + 1) * KH],
                                                   const(k, "ident")[0:size, 0:size])
                last.then_inc(S[name("rows_turned")], 1)

            def expert(i, s, more):
                pe.wait_ge(S[name("xt_ready")], n("xt_ready", i, s))
                pe.wait_ge(S[name(f"w{s}_loaded")], n(f"w{s}_loaded", i, 0, 24, 47))
                for m in range(UP):
                    if layer == 0:
                        pe.wait_ge(S[name("hid_ready")], n("hid_ready", i, s, HID, m))
                    elif m % 2 == 0:
                        pe.wait_ge(S[name("hid_ready")], n("hid_ready", i, s, HID, m // 2))
                    b = (UP * s + m) % 4
                    for f in two:
                        last = nc.tensor.matmul(bank(k, b)[:, 0:CAPACITY], w1[s][:, f, m * P:(m + 1) * P], xt[s][:, f, :],
                                                start=(f == 0), stop=(f == 1))
                    last.then_inc(S[name("up_done")], 1)
                if more:
                    turn_rows(i + s, 1 - s)
                for j, (at, size) in enumerate(ROW_TILES):
                    if j == 0:
                        pe.wait_ge(S[name("hid_ready")], n("hid_ready", i, s, HID, HID - 1, RING))
                    pe.wait_ge(S[name("out_ready")], n("out_ready", i, s, 3, j))
                    for m in range(HID):
                        last = nc.tensor.matmul(bank(k, 6 + (3 * s + j) % 2)[0:size, 0:C], hid[s][:, m, at:at + size],
                                                w2[s][:, m * C:(m + 1) * C], start=(m == 0), stop=(m == HID - 1))
                    last.then_inc(S[name("down_done")], 1)

            pe.sem_inc(S[name("down_done")], 2 * 3)
            keep_awake(nc, k, AWAKE_FIRST)
            turn_rows(0, 0, first=True)
            in_pairs(pe, expert)

        @block.scalar
        def _(act):
            if layer == 0:
                act.sem_inc(S[name("hid_ready")], RING)
            with act.Fori(0, E // 2) as i:
                for s in two:
                    act.wait_ge(S[name(f"w{s}_loaded")], n(f"w{s}_loaded", i, 0, 24, 47))
                    if layer == 0:
                        act.wait_ge(S[name("down_done")], n("down_done", i, s, 3, 2))
                        for m in range(UP):
                            act.wait_ge(S[name("up_done")], n("up_done", i, s, UP, m))
                            nc.scalar.activation(hid[s][:, m, :], bank(k, (UP * s + m) % 4)[:, 0:CAPACITY], ACT.Gelu,
                                                 bias=side[s][:, m:m + 1]).then_inc(S[name("hid_ready")], 1)
                    else:
                        for j in range(HID):
                            act.wait_ge(S[name("up_done")], n("up_done", i, s, UP, 2 * j))
                            act.wait_ge(S[name("hid_ready")], n("hid_ready", i, s, HID, j))
                            nc.scalar.activation(silu[j % 2][:, :], bank(k, (2 * j) % 4)[:, 0:CAPACITY],
                                                 ACT.Silu).then_inc(S[name("silu_ready")], 1)

        @block.vector
        def _(dve):
            def take_rows(i, s, first=False):
                dve.wait_ge(S[name("rows_turned")], n("rows_turned", i, s))
                for f in two:
                    src = bank(k, 4 + f)[0:KH, 0:CAPACITY]
                    if layer == 0:
                        last = nc.vector.tensor_scalar(xt[s][:, f, :], src, small(k, "ln2_w")[0:KH, f, :],
                                                       small(k, "ln2_b")[0:KH, f, :], ALU.mult, ALU.add)
                    else:
                        if f == 0:
                            dve.wait_ge(S[name(f"w{s}_loaded")], n(f"w{s}_loaded", i, 0, 24, 47))
                        last = nc.vector.tensor_scalar(xt[s][:, f, :], src, side[s][0:KH, f:f + 1], None, ALU.mult)
                last.then_inc(S[name("xt_ready")], 1)

            def expert(i, s, more):
                if layer == 2:
                    dve.wait_ge(S[name("down_done")], n("down_done", i, s, 3, 2))
                    for j in range(HID):
                        dve.wait_ge(S[name("silu_ready")], n("silu_ready", i, s, HID, j))
                        dve.wait_ge(S[name("up_done")], n("up_done", i, s, UP, 2 * j + 1))
                        nc.vector.tensor_tensor(hid[s][:, j, :], silu[j % 2][:, :], bank(k, (2 * j + 1) % 4)[:, 0:CAPACITY],
                                                ALU.mult).then_inc(S[name("hid_ready")], 1)
                if more:
                    take_rows(i + s, 1 - s)
                for j, (at, size) in enumerate(ROW_TILES):
                    dve.wait_ge(S[name("down_done")], n("down_done", i, s, 3, j, 6))
                    if j == 0:
                        dve.wait_ge(S[name("out_free")], n("out_free", i, s))
                    src = bank(k, 6 + (3 * s + j) % 2)[0:size, 0:C]
                    if layer == 0:
                        last = nc.vector.tensor_tensor(out[s][0:size, j, :], src, w2[s][0:size, HID * C:], ALU.add)
                    else:
                        last = nc.vector.tensor_copy(out[s][0:size, j, :], src)
                    last.then_inc(S[name("out_ready")], 1)

            if layer == 2:
                dve.sem_inc(S[name("hid_ready")], RING)
            dve.sem_inc(S[name("out_ready")], 2)
            take_rows(0, 0)
            in_pairs(dve, expert)
    counts = dict(up_done=UP * E, hid_ready=HID * E + RING, down_done=3 * E + 6, out_ready=3 * E + 2, out_stored=32 * E,
                  out_free=E + 2, rows_turned=E, xt_ready=E, silu_ready=HID * E if layer == 2 else 0,
                  w0_loaded=24 * E, w1_loaded=24 * E, rows0_loaded=16 * E, rows1_loaded=16 * E)
    S.passed(**{name(x): c for x, c in counts.items()})


def collect(nc, k, choices, shared=False):
    S = k.S
    LATE = 2
    rows = SORTED * P if shared else SLOTS
    with ExitStack() as own:
        tag = f"collect{S.at('rows_back0')}_"
        sb = lambda nm, shape: own.enter_context(nc.sbuf_tensor(tag + nm, shape, F32))
        came = [sb(f"came{c}", [P, TILES, C]) for c in range(choices + shared)]
        stats, meanvar = sb("stats", [P, TILES, 6]), sb("meanvar", [P, TILES, 2])
        vareps, rstd = sb("vareps", [P, TILES]), sb("rstd", [P, TILES])
        block = own.enter_context(nc.Block())

        if shared:
            @block.sync
            def _(sp):
                sp.dma_start(came[choices][:, :, :], k.returned[0:TOKENS, :].rearrange("(t p) c -> p t c", p=P)).then_inc(S["shared_back"], 16)

        @block.gpsimd
        def _(pool):
            for t in range(TILES + LATE):
                if t < TILES:
                    for c in range(choices):
                        nc.gpsimd.indirect_dma_start(came[c][:, t, :], None, k.returned[0:rows, :],
                                                     bass.IndirectOffsetOnAxis(ap=k.back[:, c, t:t + 1], axis=0)).then_inc(S[f"rows_back{t}"], 16)
                if t >= LATE:
                    d = t - LATE
                    pool.wait_ge(S["collect_vareps"], S.at("collect_vareps") + d + 1)
                    nc.gpsimd.tensor_tensor(rstd[:, d:d + 1], vareps[:, d:d + 1], k.minus_half[:, 0:1], ALU.pow).then_inc(S["collect_rstd"], 1)

        @block.vector
        def _(dve):
            at = [S.at("collect_step")]

            def then(ins):
                at[0] += 1
                ins.then_inc(S["collect_step"], 1)
                dve.wait_ge(S["collect_step"], at[0])

            if shared:
                dve.wait_ge(S["shared_back"], 16)
                then(nc.vector.tensor_tensor(k.acc[:, :, :], k.acc[:, :, :], came[choices][:, :, :], ALU.add))
            for t in range(TILES + LATE):
                if t < TILES:
                    acc = k.acc[:, t, :]
                    dve.wait_ge(S[f"rows_back{t}"], S.at(f"rows_back{t}") + 16 * choices)
                    for c in range(choices):
                        then(nc.vector.scalar_tensor_tensor(out=acc, in0=came[c][:, t, :], scalar=k.share[:, c, t:t + 1], in1=acc,
                                                            op0=ALU.mult, op1=ALU.add))
                    then(nc.vector.bn_stats(stats[:, t, :], acc))
                    then(nc.vector.bn_aggr(meanvar[:, t, :], stats[:, t, :]))
                    nc.vector.tensor_scalar_add(vareps[:, t:t + 1], meanvar[:, t, 1:2], LN_EPS).then_inc(S["collect_vareps"], 1)
                if t >= LATE:
                    d = t - LATE
                    dve.wait_ge(S["collect_rstd"], S.at("collect_rstd") + d + 1)
                    nc.vector.tensor_scalar(k.h[:, d, :], k.acc[:, d, :], meanvar[:, d, 0:1], rstd[:, d:d + 1],
                                            ALU.subtract, ALU.mult)
            collect.steps = at[0] - S.at("collect_step")
    S.passed(collect_vareps=TILES, collect_rstd=TILES, collect_step=collect.steps,
             **{f"rows_back{t}": 16 * choices for t in range(TILES)})


def quantised(nc, k, io):
    S = k.S
    LATE = 2
    with ExitStack() as own:
        sb = lambda name, shape, dt=F32: own.enter_context(nc.sbuf_tensor("q_" + name, shape, dt))
        w_int = sb("w_int", [KH, 2, C], I32)
        wb = sb("wb", [KH, 2, C], BF16)
        xq = sb("xq", [KH, TILES, 2, P], BF16)
        rounded = sb("rounded", [P, TILES, C])
        y, out = sb("y", [P, TILES, C]), sb("out", [P, TILES, C])
        stats, meanvar = sb("stats", [P, TILES, 6]), sb("meanvar", [P, TILES, 2])
        vareps, rstd = sb("vareps", [P, TILES]), sb("rstd", [P, TILES])
        block = own.enter_context(nc.Block())
        turned = lambda t: bank(k, t % 4)[0:KH, 0:2 * P]
        product = lambda t: bank(k, 4 + t % 4)[:, 0:C]

        @block.sync
        def _(sp):
            sp.dma_start(w_int[:, :, :], io["l3_w"]).then_inc(S["w_int_loaded"], 16)
            rows = io["out"].rearrange("(t p) c -> t p c", p=P)
            for t in range(TILES):
                sp.wait_ge(S["result_ready"], t + 1)
                sp.dma_start(rows[t], out[:, t, :]).then_inc(S["stored"], 16)
            sp.wait_ge(S["stored"], 16 * TILES)

        @block.gpsimd
        def _(pool):
            for t in range(TILES):
                pool.wait_ge(S["collect_vareps"], S.at("collect_vareps") + t + 1)
                nc.gpsimd.tensor_tensor(rstd[:, t:t + 1], vareps[:, t:t + 1], k.minus_half[:, 0:1], ALU.pow).then_inc(S["collect_rstd"], 1)

        @block.tensor
        def _(pe):
            for t in range(TILES + 1):
                if t < TILES:
                    pe.wait_ge(S["q_rounded"], 3 * t + 3)
                    if t >= 4:
                        pe.wait_ge(S["xt_ready"], S.at("xt_ready") + t - 3)
                    for f in range(2):
                        last = nc.tensor.transpose(turned(t)[:, f * P:(f + 1) * P], rounded[:, t, f * KH:(f + 1) * KH],
                                                   const(k, "ident"))
                    last.then_inc(S["x_turned"], 1)
                if t >= 1:
                    pe.wait_ge(S["xt_ready"], S.at("xt_ready") + t)
                    if t >= 5:
                        pe.wait_ge(S["q_scaled"], t - 4)
                    for f in range(2):
                        last = nc.tensor.matmul(product(t - 1), xq[:, t - 1, f, :], wb[:, f, :], start=(f == 0), stop=(f == 1))
                    last.then_inc(S["projected"], 1)

        @block.scalar
        def _(act):
            act.wait_ge(S["w_int_loaded"], 16)
            nc.scalar.activation(wb[:, :, :], w_int[:, :, :], ACT.Copy)
            for t in range(TILES):
                act.wait_ge(S["x_turned"], S.at("x_turned") + t + 1)
                nc.scalar.activation(xq[:, t, :, :].rearrange("p f t -> p (f t)"), turned(t), ACT.Copy).then_inc(S["xt_ready"], 1)

        @block.vector
        def _(dve):
            def round_tile(t):
                r = rounded[:, t, :]
                nc.vector.tensor_scalar(r, k.h[:, t, :], float(1.0 / np.float32(0.02)), 127.0, ALU.mult, ALU.min).then_inc(S["q_rounded"], 1)
                dve.wait_ge(S["q_rounded"], 3 * t + 1)
                nc.vector.tensor_scalar(r, r, -128.0, ROUND, ALU.max, ALU.add).then_inc(S["q_rounded"], 1)
                dve.wait_ge(S["q_rounded"], 3 * t + 2)
                nc.vector.tensor_scalar_add(r, r, -ROUND).then_inc(S["q_rounded"], 1)

            def add_tile(t):
                dve.wait_ge(S["projected"], S.at("projected") + t + 1)
                nc.vector.scalar_tensor_tensor(out=y[:, t, :], in0=product(t), scalar=float(np.float32(0.02 * 0.01)),
                                               in1=const(k, "l3_bias"), op0=ALU.mult, op1=ALU.add).then_inc(S["q_scaled"], 1)
                dve.wait_ge(S["q_scaled"], t + 1)
                nc.vector.tensor_tensor(y[:, t, :], y[:, t, :], k.h[:, t, :], ALU.add).then_inc(S["collect_step"], 1)
                dve.wait_ge(S["collect_step"], S.at("collect_step") + 3 * t + 1)
                nc.vector.bn_stats(stats[:, t, :], y[:, t, :]).then_inc(S["collect_step"], 1)
                dve.wait_ge(S["collect_step"], S.at("collect_step") + 3 * t + 2)
                nc.vector.bn_aggr(meanvar[:, t, :], stats[:, t, :]).then_inc(S["collect_step"], 1)
                dve.wait_ge(S["collect_step"], S.at("collect_step") + 3 * t + 3)
                nc.vector.tensor_scalar_add(vareps[:, t:t + 1], meanvar[:, t, 1:2], LN_EPS).then_inc(S["collect_vareps"], 1)

            def store_tile(t):
                dve.wait_ge(S["collect_rstd"], S.at("collect_rstd") + t + 1)
                nc.vector.tensor_scalar(out[:, t, :], y[:, t, :], meanvar[:, t, 0:1], rstd[:, t:t + 1],
                                        ALU.subtract, ALU.mult).then_inc(S["result_ready"], 1)

            for t in range(TILES + 2 * LATE - 1):
                if t < TILES:
                    round_tile(t)
                if LATE <= t < TILES + LATE:
                    add_tile(t - LATE)
                if t >= 2 * LATE - 1:
                    store_tile(t - 2 * LATE + 1)


def program(nc, io):
    with ExitStack() as ctx:
        k = allocate(nc, ctx)
        load_constants(nc, k, io)
        embed(nc, k, io)
        allocate_experts(nc, k, ctx)

        with ExitStack() as buffers:
            allocate_attention(nc, k, buffers, "a_")
            clear_attention(nc, k, slots=True)
            attention(nc, k, io, 0, "segments")
            attention(nc, k, io, 1, "softmax", pre_ln="ln1", keep=True)
            turn(nc, k, k.x1, ln2=True)
            route(nc, k, 0, io)
            sent_experts(nc, k, io, 0)
            collect(nc, k, 2)

        with ExitStack() as weights:
            allocate_sorted(nc, k, weights)
            with ExitStack() as buffers:
                allocate_attention(nc, k, buffers, "b_")
                clear_attention(nc, k)
                attention(nc, k, io, 2, "softmax", ahead=lambda sp: load_sorted(k, io, sp))
            turn(nc, k, k.h)
            route(nc, k, 1, io)
            sorted_experts(nc, k)
        collect(nc, k, CHOICES, shared=True)

        with ExitStack() as buffers:
            allocate_attention(nc, k, buffers, "c_")
            clear_attention(nc, k)
            turn(nc, k, k.h)
            gates(nc, k)
            attention(nc, k, io, 3, "linear", pre_ln="l2")
            turn(nc, k, k.h)
            rms_rows(nc, k)
            route(nc, k, 2, io)
            sent_experts(nc, k, io, 2)
            collect(nc, k, 2)
            attention(nc, k, io, 4, "rotary")
            quantised(nc, k, io)


def _constants(inp):
    f = np.float32
    c = np.zeros((P, CONST_WIDTH), f)

    def put(name, a):
        at, w = CONST_AT[name]
        c[:, at:at + w] = a

    p = np.arange(P)
    t = p % PATCHES
    key = np.arange(PATCHES)
    put("ident", np.eye(P, dtype=f))
    put("fold64", (t[:, None] == key[None, :]).astype(f))
    put("fold128", (t[:, None] == t[None, :]).astype(f))
    put("earlier", (p[:, None] < p[None, :]).astype(f))
    put("ones", np.ones((P, P), f))
    causal = key[None, :] <= t[:, None]
    put("causal_add", np.where(causal, 0, MASKED).astype(f))
    put("causal01", causal.astype(f))
    put("tail01", (causal & (key[None, :] >= t[:, None] // SEG * SEG)).astype(f))
    ends = np.array([15, 31, 47, 63, 31, 63, 63, 0])
    put("seg_add", np.where(t[:, None] >= ends[None, :], 0, MASKED).astype(f))
    freqs = (f(1.0 / 1024.0) ** np.linspace(0, 1, HD // 4, dtype=f)).astype(f)
    theta = t[:, None].astype(f) * np.concatenate([freqs, np.zeros(HD // 4, f)])[None, :]
    put("cos", np.cos(theta).astype(f))
    put("sin", np.sin(theta).astype(f))
    put("nsin", -np.sin(theta).astype(f))
    put("iota", np.arange(16, dtype=f)[None, :])
    put("refused", (SLOTS + np.arange(16)[None, :] * P + p[:, None]).astype(f))
    put("tile_start", (P * np.arange(48)[None, :]).astype(f))
    put("bv", inp["L0_attn_bv"][None, :])
    put("mn_w", inp["L2_attn_mn_w"][None, :])
    put("mn_b", inp["L2_attn_mn_b"][None, :])
    put("temperature", inp["L2_attn_temperature"][None, :])
    put("l3_bias", inp["L3_ffn_bias"][None, :])
    put("wb2", inp["L2_attn_Wb2"].reshape(128, HEADS, 5).transpose(0, 2, 1).reshape(128, 60))
    return c


def _halves(w, bias=None):
    out = np.zeros((KH + 1, 2, w.shape[1]), np.float32)
    out[0:KH] = w.reshape(2, KH, -1).transpose(1, 0, 2)
    if bias is not None:
        out[KH, 1] = bias
    return out


def _layouts(inp):
    f = np.float32
    x = inp["x"].reshape(IMAGES, 3, 8, 16, 8, 16).transpose(1, 3, 5, 0, 2, 4)
    a = {"patches_t": x.reshape(KT_PATCH, P, TOKENS)}
    a["w_embed"] = inp["L0_tok_W"].T.reshape(KT_PATCH, P, C).transpose(1, 0, 2)
    a["const"] = _constants(inp)
    small = np.zeros((KH + 1, 2, SMALL_WIDTH), f)
    for name, w, b in (("gate0", inp["L0_ffn_w_g"], None), ("gate1", inp["L1_ffn_gate_w"], inp["L1_ffn_gate_b"]),
                       ("gate2", inp["L2_ffn_gate_w"].T, None), ("wb1", inp["L2_attn_Wb1"], None)):
        at, width = SMALL_AT[name]
        small[:, :, at:at + width] = _halves(w, b)
    for name, v in (("ln1_w", "L0_ffn_ln1_w"), ("ln1_b", "L0_ffn_ln1_b"), ("ln2_w", "L0_ffn_ln2_w"),
                    ("ln2_b", "L0_ffn_ln2_b"), ("l2_w", "L2_attn_ln_w"), ("l2_b", "L2_attn_ln_b")):
        at, _ = SMALL_AT[name]
        small[0:KH, :, at] = inp[v].reshape(2, KH).T
    a["small"] = small
    cat = np.concatenate
    z3, z = np.zeros(3 * C, f), np.zeros(C, f)
    a["wattn"] = np.stack([
        _halves(cat([inp["L0_attn_Wqkv"].T, inp["L0_attn_Wproj"].T], 1), cat([z3, z])),
        _halves(cat([inp["L0_ffn_attn_qkv_w"], inp["L0_ffn_attn_proj_w"]], 1),
                cat([inp["L0_ffn_attn_qkv_b"], inp["L0_ffn_attn_proj_b"]])),
        _halves(cat([inp[f"L1_attn_W{c}"].T for c in "qkvo"], 1), cat([inp[f"L1_attn_b{c}"] for c in "qkvo"])),
        _halves(cat([inp["L2_attn_Wqkv"], inp["L2_attn_Wproj"]], 1), cat([inp["L2_attn_bqkv"], inp["L2_attn_bproj"]])),
        _halves(cat([inp["L3_attn_qkv_w"][c].T for c in range(3)] + [inp["L3_attn_c_proj_w"].T], 1), cat([z3, z])),
    ])
    bil = np.zeros((PAIRS, HD, PAIRS, 256), f)
    wv = inp["L0_attn_Wv"].reshape(HD, HD, HD).transpose(1, 0, 2).reshape(HD, 256)
    for h in range(PAIRS):
        bil[h, :, h, :] = wv
    a["bil_w"] = bil.reshape(KH, PAIRS, 256)

    def up(w):
        e, _, n = w.shape
        return w.reshape(e, 2, KH, n).transpose(0, 2, 1, 3).reshape(e, KH, 2 * n)

    def down(w):
        e, h, _ = w.shape
        return w.reshape(e, h // P, P, C).transpose(0, 2, 1, 3).reshape(e, P, -1)

    def side(e, *cols):
        out = np.zeros((e, P, 16), f)
        for at, v in cols:
            out[:, 0:v.shape[1], at:at + v.shape[2]] = v
        return out

    tiles = lambda v: v.reshape(v.shape[0], -1, P).transpose(0, 2, 1)
    a["l0_w1"], a["l0_w2"] = up(inp["L0_ffn_exp_fc_w"]), cat([down(inp["L0_ffn_exp_proj_w"]),
                                                                       np.broadcast_to(inp["L0_ffn_exp_proj_b"], (8, P, C))], 2)
    a["l0_side"] = side(8, (0, tiles(inp["L0_ffn_exp_fc_b"][:, 0])))
    halves = [_halves(w, b) for w, b in zip(inp["L1_ffn_fc1_w"], inp["L1_ffn_fc1_b"])]
    a["l1_w1"] = np.stack(halves, 2)
    a["l1_w2"] = inp["L1_ffn_fc2_w"].reshape(16, 3, P, C).transpose(2, 0, 1, 3)
    a["l1_side"] = np.stack([inp["L1_ffn_ln_w"], inp["L1_ffn_ln_b"]]).reshape(2, 16, 3, P).transpose(3, 0, 2, 1)
    a["l1_rows"] = inp["L1_ffn_fc2_b"]
    w13 = inp["L2_ffn_w13"].transpose(0, 2, 1).reshape(8, C, 2, 4, P).transpose(0, 1, 3, 2, 4).reshape(8, C, 1024)
    a["l2_w1"], a["l2_w2"] = up(w13), down(inp["L2_ffn_w2"].transpose(0, 2, 1))
    a["l2_side"] = side(8, (0, inp["L2_ffn_norm_w"].reshape(8, 2, KH).transpose(0, 2, 1)))
    a["l3_w"] = inp["L3_ffn_weight_t"].reshape(2, KH, C).transpose(1, 0, 2)
    return {n: np.ascontiguousarray(v.astype(np.int32) if v.dtype.kind in "iu" else v) for n, v in a.items()}


def kernel(**inputs):
    import concourse.bacc as bacc
    from concourse.bass_utils import run_bass_kernel_spmd as run

    arrays = _layouts({n: np.asarray(v) for n, v in inputs.items()})
    nc = bacc.Bacc("TRN2", target_bir_lowering=False, num_devices=1)
    io = {n: nc.dram_tensor("in_" + n, v.shape, mybir.dt.from_np(v.dtype), kind="ExternalInput").ap()
          for n, v in arrays.items()}
    io["out"] = nc.dram_tensor("out", (TOKENS, C), F32, kind="ExternalOutput").ap()
    program(nc, io)
    r = run(nc, [{"in_" + n: v for n, v in arrays.items()}], core_ids=[0])
    return r.results[0]["out"].reshape(IMAGES, PATCHES, C)
```
